# Optimizing a Trainium2 kernel written in Bass

```python
import numpy as np
import jax
import jax.numpy as jnp

def _softmax(x, axis=-1):
    return jax.nn.softmax(x, axis=axis)

def _gelu(x):
    return jax.nn.gelu(x, approximate=True)

def _silu(x):
    return jax.nn.silu(x)

def _sigmoid(x):
    return jax.nn.sigmoid(x)

def _layernorm(x, axis=-1, eps=1e-05):
    m = jnp.mean(x, axis=axis, keepdims=True)
    v = jnp.var(x, axis=axis, keepdims=True)
    return (x - m) / jnp.sqrt(v + eps)

def _scatter_add(tgt, idx, src, axis=0):
    return tgt.at[idx].add(src)

def _segment_sum(src, seg, n):
    return jax.ops.segment_sum(src, seg, n)
kernel_name = 'mk_hybrid_d1_jaxref_r4_f88e99'

def setup_inputs(seed: int=0):
    np.random.seed(seed)
    _w = jnp.asarray

    def _L0_attn_a_setup():
        import jax, jax.numpy as jnp
        import numpy as np
        from jax import lax
        H = 4
        CHUNK = 64
        EPS = 1e-05

        def _rope(t, cos, sin):
            t1, t2 = jnp.split(t, 2, axis=-1)
            c = cos[None, :, None, :]
            s = sin[None, :, None, :]
            return jnp.concatenate([t1 * c - t2 * s, t2 * c + t1 * s], axis=-1)
        key = jax.random.key(seed)
        ks = jax.random.split(key, 8)
        B, T, D = (4, 1024, 256)
        s = lambda fan: 1.0 / np.sqrt(fan)
        return {'x': jax.random.normal(ks[0], (B, T, D), jnp.float32), 'ln_w': jnp.ones((D,), jnp.float32), 'ln_b': jnp.zeros((D,), jnp.float32), 'Wq': jax.random.normal(ks[1], (D, D), jnp.float32) * s(D), 'Wk': jax.random.normal(ks[2], (D, D), jnp.float32) * s(D), 'Wv': jax.random.normal(ks[3], (D, 2 * D), jnp.float32) * s(D), 'Wg': jax.random.normal(ks[4], (D, 2 * D), jnp.float32) * s(D), 'g_norm_w': jnp.ones((2 * D // H,), jnp.float32), 'Wo': jax.random.normal(ks[5], (2 * D, D), jnp.float32) * s(2 * D)}
    _L0_attn_a_in = _L0_attn_a_setup()

    def _L0_attn_b_setup():
        import jax, jax.numpy as jnp
        import numpy as np
        EMBED = 256
        HEADS = 16
        HEAD_DIM = EMBED // HEADS
        NUM_BUCKETS = 32
        MAX_DISTANCE = 128
        B, L = (4, 512)

        def relative_position_bucket(relative_position, num_buckets=NUM_BUCKETS, max_distance=MAX_DISTANCE):
            n = -relative_position
            max_exact = num_buckets // 2
            is_small = n < max_exact
            nf = jnp.maximum(n, 1).astype(jnp.float32)
            val_if_large = max_exact + (jnp.log(nf / max_exact) / np.log(max_distance / max_exact) * (num_buckets - max_exact)).astype(jnp.int32)
            val_if_large = jnp.minimum(val_if_large, num_buckets - 1)
            ret = jnp.where(is_small, n, val_if_large)
            return jnp.maximum(ret, 0)
        key = jax.random.key(seed)
        ks = jax.random.split(key, 11)
        s = 0.02
        return {'x': jax.random.normal(ks[0], (B, L, EMBED), dtype=jnp.float32), 'wq': jax.random.normal(ks[1], (EMBED, EMBED), dtype=jnp.float32) * s, 'bq': jnp.zeros((EMBED,), dtype=jnp.float32), 'wk': jax.random.normal(ks[2], (EMBED, EMBED), dtype=jnp.float32) * s, 'bk': jnp.zeros((EMBED,), dtype=jnp.float32), 'wv': jax.random.normal(ks[3], (EMBED, EMBED), dtype=jnp.float32) * s, 'bv': jnp.zeros((EMBED,), dtype=jnp.float32), 'wo': jax.random.normal(ks[4], (EMBED, EMBED), dtype=jnp.float32) * s, 'bo': jnp.zeros((EMBED,), dtype=jnp.float32), 'rel_bias': jax.random.normal(ks[5], (NUM_BUCKETS, HEADS), dtype=jnp.float32) * s}
    _L0_attn_b_in = _L0_attn_b_setup()

    def _L0_ffn_setup():
        import jax, jax.numpy as jnp
        import numpy as np
        DIM = 256

        def _reference_tuple_inner(x, W_r, W_k, W_v, mu_r, mu_k):
            B, T, C = x.shape
            x_prev = jnp.concatenate([jnp.zeros((B, 1, C), x.dtype), x[:, :-1, :]], axis=1)
            xr = mu_r * x + (1.0 - mu_r) * x_prev
            xk = mu_k * x + (1.0 - mu_k) * x_prev
            r = jax.nn.sigmoid(jnp.einsum('btc,dc->btd', xr, W_r))
            k = jnp.einsum('btc,dc->btd', xk, W_k)
            k_act = jnp.square(jax.nn.relu(k))
            out = r * jnp.einsum('btc,dc->btd', k_act, W_v)
            new_state = x[:, -1, :]
            return (out, new_state)
        key = jax.random.key(seed)
        ks = jax.random.split(key, 6)
        B, T, C = (8, 512, DIM)
        x = jax.random.normal(ks[0], (B, T, C), dtype=jnp.float32)
        s = 1.0 / np.sqrt(C)
        W_r = jax.random.uniform(ks[1], (C, C), jnp.float32, -s, s)
        W_k = jax.random.uniform(ks[2], (C, C), jnp.float32, -s, s)
        W_v = jax.random.uniform(ks[3], (C, C), jnp.float32, -s, s)
        mu_r = jax.random.uniform(ks[4], (C,), jnp.float32)
        mu_k = jax.random.uniform(ks[5], (C,), jnp.float32)
        return {'x': x, 'W_r': W_r, 'W_k': W_k, 'W_v': W_v, 'mu_r': mu_r, 'mu_k': mu_k}
    _L0_ffn_in = _L0_ffn_setup()
    _d = {'L0_attn_a_x': _L0_attn_a_in['x'], 'L0_attn_a_ln_w': _L0_attn_a_in['ln_w'], 'L0_attn_a_ln_b': _L0_attn_a_in['ln_b'], 'L0_attn_a_Wq': _L0_attn_a_in['Wq'], 'L0_attn_a_Wk': _L0_attn_a_in['Wk'], 'L0_attn_a_Wv': _L0_attn_a_in['Wv'], 'L0_attn_a_Wg': _L0_attn_a_in['Wg'], 'L0_attn_a_g_norm_w': _L0_attn_a_in['g_norm_w'], 'L0_attn_a_Wo': _L0_attn_a_in['Wo'], 'L0_attn_b_wq': _L0_attn_b_in['wq'], 'L0_attn_b_bq': _L0_attn_b_in['bq'], 'L0_attn_b_wk': _L0_attn_b_in['wk'], 'L0_attn_b_bk': _L0_attn_b_in['bk'], 'L0_attn_b_wv': _L0_attn_b_in['wv'], 'L0_attn_b_bv': _L0_attn_b_in['bv'], 'L0_attn_b_wo': _L0_attn_b_in['wo'], 'L0_attn_b_bo': _L0_attn_b_in['bo'], 'L0_attn_b_rel_bias': _L0_attn_b_in['rel_bias'], 'L0_ffn_W_r': _L0_ffn_in['W_r'], 'L0_ffn_W_k': _L0_ffn_in['W_k'], 'L0_ffn_W_v': _L0_ffn_in['W_v'], 'L0_ffn_mu_r': _L0_ffn_in['mu_r'], 'L0_ffn_mu_k': _L0_ffn_in['mu_k']}
    _x0 = _d['L0_attn_a_x']
    _d['L0_attn_a_x'] = jax.random.normal(jax.random.fold_in(jax.random.key(seed), 1), (8, 1024, 256), dtype=_x0.dtype)
    del _x0
    return _d

def reference(L0_attn_a_x, L0_attn_a_ln_w, L0_attn_a_ln_b, L0_attn_a_Wq, L0_attn_a_Wk, L0_attn_a_Wv, L0_attn_a_Wg, L0_attn_a_g_norm_w, L0_attn_a_Wo, L0_attn_b_wq, L0_attn_b_bq, L0_attn_b_wk, L0_attn_b_bk, L0_attn_b_wv, L0_attn_b_bv, L0_attn_b_wo, L0_attn_b_bo, L0_attn_b_rel_bias, L0_ffn_W_r, L0_ffn_W_k, L0_ffn_W_v, L0_ffn_mu_r, L0_ffn_mu_k):

    def _L0_attn_a_ref(x, ln_w, ln_b, Wq, Wk, Wv, Wg, g_norm_w, Wo):
        import jax, jax.numpy as jnp
        import numpy as np
        from jax import lax
        H = 4
        CHUNK = 64
        EPS = 1e-05

        def _rope(t, cos, sin):
            t1, t2 = jnp.split(t, 2, axis=-1)
            c = cos[None, :, None, :]
            s = sin[None, :, None, :]
            return jnp.concatenate([t1 * c - t2 * s, t2 * c + t1 * s], axis=-1)
        B, T, D = x.shape
        dk, dv = (D // H, 2 * D // H)
        C = CHUNK
        N = T // C
        mu = x.mean(-1, keepdims=True)
        var = ((x - mu) ** 2).mean(-1, keepdims=True)
        normed = (x - mu) * lax.rsqrt(var + EPS) * ln_w + ln_b
        q = (normed @ Wq).reshape(B, T, H, dk)
        k = (normed @ Wk).reshape(B, T, H, dk)
        v = (normed @ Wv).reshape(B, T, H, dv)
        g = (normed @ Wg).reshape(B, T, H, dv)
        inv_freq = 1.0 / 10000.0 ** (jnp.arange(0, dk, 2, dtype=jnp.float32) / dk)
        freqs = jnp.arange(T, dtype=jnp.float32)[:, None] * inv_freq[None, :]
        cos, sin = (jnp.cos(freqs), jnp.sin(freqs))
        q = _rope(q, cos, sin) * dk ** (-0.5)
        k = _rope(k, cos, sin)
        gamma = 1.0 - jnp.exp2(-5.0 - jnp.arange(H, dtype=jnp.float32))
        i = jnp.arange(C, dtype=jnp.float32)
        Dmask = jnp.where(i[:, None] >= i[None, :], gamma[:, None, None] ** (i[:, None] - i[None, :]), 0.0)
        cross = gamma[:, None] ** (i + 1.0)
        kdec = gamma[:, None] ** (C - 1.0 - i)
        gC = gamma ** C
        to_chunks = lambda t, d: t.reshape(B, N, C, H, d).transpose(1, 0, 3, 2, 4)
        qc, kc, vc = (to_chunks(q, dk), to_chunks(k, dk), to_chunks(v, dv))

        def step(S, inp):
            qn, kn, vn = inp
            attn = jnp.einsum('bhid,bhjd->bhij', qn, kn) * Dmask
            o = jnp.einsum('bhij,bhjv->bhiv', attn, vn) + jnp.einsum('bhid,bhdv->bhiv', qn * cross[None, :, :, None], S)
            S = S * gC[None, :, None, None] + jnp.einsum('bhid,bhiv->bhdv', kn * kdec[None, :, :, None], vn)
            return (S, o)
        S0 = jnp.zeros((B, H, dk, dv), x.dtype)
        _, o = lax.scan(step, S0, (qc, kc, vc))
        o = o.transpose(1, 0, 3, 2, 4).reshape(B, T, H, dv)
        o = o * lax.rsqrt((o ** 2).mean(-1, keepdims=True) + EPS) * g_norm_w
        o = o * (g * jax.nn.sigmoid(g))
        out = o.reshape(B, T, 2 * D) @ Wo
        return x + out

    def _L0_attn_b_ref(x, wq, bq, wk, bk, wv, bv, wo, bo, rel_bias):
        import jax, jax.numpy as jnp
        import numpy as np
        EMBED = 256
        HEADS = 16
        HEAD_DIM = EMBED // HEADS
        NUM_BUCKETS = 32
        MAX_DISTANCE = 128
        B, L = (4, 512)

        def relative_position_bucket(relative_position, num_buckets=NUM_BUCKETS, max_distance=MAX_DISTANCE):
            n = -relative_position
            max_exact = num_buckets // 2
            is_small = n < max_exact
            nf = jnp.maximum(n, 1).astype(jnp.float32)
            val_if_large = max_exact + (jnp.log(nf / max_exact) / np.log(max_distance / max_exact) * (num_buckets - max_exact)).astype(jnp.int32)
            val_if_large = jnp.minimum(val_if_large, num_buckets - 1)
            ret = jnp.where(is_small, n, val_if_large)
            return jnp.maximum(ret, 0)
        Bx, Lx, C = x.shape

        def proj(w, b):
            y = jnp.einsum('blc,dc->bld', x, w) + b
            return y.reshape(Bx, Lx, HEADS, HEAD_DIM).transpose(0, 2, 1, 3)
        q = proj(wq, bq)
        k = proj(wk, bk)
        v = proj(wv, bv)
        scores = jnp.einsum('bhqd,bhkd->bhqk', q, k) / np.sqrt(HEAD_DIM)
        ctx = jnp.arange(Lx, dtype=jnp.int32)
        relative = ctx[None, :] - ctx[:, None]
        bucket_ids = relative_position_bucket(relative)
        bias = rel_bias[bucket_ids]
        bias = jnp.transpose(bias, (2, 0, 1))
        attn = jax.nn.softmax(scores + bias[None], axis=-1)
        out = jnp.einsum('bhqk,bhkd->bhqd', attn, v)
        out = out.transpose(0, 2, 1, 3).reshape(Bx, Lx, C)
        return jnp.einsum('blc,dc->bld', out, wo) + bo

    def _L0_ffn_ref(x, W_r, W_k, W_v, mu_r, mu_k):
        import jax, jax.numpy as jnp
        import numpy as np
        DIM = 256

        def _reference_tuple_inner(x, W_r, W_k, W_v, mu_r, mu_k):
            B, T, C = x.shape
            x_prev = jnp.concatenate([jnp.zeros((B, 1, C), x.dtype), x[:, :-1, :]], axis=1)
            xr = mu_r * x + (1.0 - mu_r) * x_prev
            xk = mu_k * x + (1.0 - mu_k) * x_prev
            r = jax.nn.sigmoid(jnp.einsum('btc,dc->btd', xr, W_r))
            k = jnp.einsum('btc,dc->btd', xk, W_k)
            k_act = jnp.square(jax.nn.relu(k))
            out = r * jnp.einsum('btc,dc->btd', k_act, W_v)
            new_state = x[:, -1, :]
            return (out, new_state)
        return _reference_tuple_inner(x, W_r, W_k, W_v, mu_r, mu_k)[0]
    x = L0_attn_a_x
    x = x + _L0_attn_a_ref(_layernorm(x, axis=-1), L0_attn_a_ln_w, L0_attn_a_ln_b, L0_attn_a_Wq, L0_attn_a_Wk, L0_attn_a_Wv, L0_attn_a_Wg, L0_attn_a_g_norm_w, L0_attn_a_Wo)
    x = x + _L0_ffn_ref(_layernorm(x, axis=-1), L0_ffn_W_r, L0_ffn_W_k, L0_ffn_W_v, L0_ffn_mu_r, L0_ffn_mu_k)
    x = x + _L0_attn_b_ref(_layernorm(x, axis=-1), L0_attn_b_wq, L0_attn_b_bq, L0_attn_b_wk, L0_attn_b_bk, L0_attn_b_wv, L0_attn_b_bv, L0_attn_b_wo, L0_attn_b_bo, L0_attn_b_rel_bias)
    x = x + _L0_ffn_ref(_layernorm(x, axis=-1), L0_ffn_W_r, L0_ffn_W_k, L0_ffn_W_v, L0_ffn_mu_r, L0_ffn_mu_k)
    return x

_drawn_inputs = setup_inputs


def setup_inputs(seed=0):
    import zlib

    import numpy as np

    out = dict(_drawn_inputs(seed))
    spreads = {'L0_attn_a_ln_w': (1.0, 0.2),
     'L0_attn_a_ln_b': (0.0, 0.1),
     'L0_attn_a_g_norm_w': (1.0, 0.2),
     'L0_attn_b_bq': (0.0, 0.8),
     'L0_attn_b_bk': (0.0, 0.8),
     'L0_attn_b_bv': (0.0, 0.503),
     'L0_attn_b_bo': (0.0, 0.1)}
    factors = {'L0_attn_b_wq': 8.0,
     'L0_attn_b_wk': 8.0,
     'L0_attn_b_wv': 8.0,
     'L0_attn_b_wo': 3.444,
     'L0_attn_b_rel_bias': 8.0,
     'L0_ffn_W_r': 3.34,
     'L0_ffn_mu_r': 6.728}
    for name, (base, spread) in spreads.items():
        noise = np.random.default_rng([zlib.crc32(name.encode()), seed]).standard_normal(out[name].shape)
        drawn = base * np.exp(spread * noise) if base else spread * noise
        out[name] = jnp.asarray(drawn.astype(out[name].dtype))
    for name, factor in factors.items():
        out[name] = (out[name] * factor).astype(out[name].dtype)
    return out
```

```python
from contextlib import ExitStack

import concourse.bass as bass
from concourse import mybir

F32 = mybir.dt.float32
BF16 = mybir.dt.bfloat16
ALU = mybir.AluOpType
ACT = mybir.ActivationFunctionType
AX_X = mybir.AxisListType.X

P = 128
EPS = 1e-5
RET_HEADS = 4
HEADS = 16
BUCKETS = 32
PARTS = 3
Q_PARTS = (0, 0, 1, 0, 1, 2)
K_PARTS = (0, 1, 0, 2, 1, 0)
MAX_ROW = 96
RING = 12
LAG = 2
AHEAD = 24
SLOTS = 2
KEY_ORDER = ((0, 4, 1, 5, 2, 6, 3, 7), (3, 0, 4, 1, 5, 2, 6, 7))


class Tally:

    def __init__(self, sem, each, step=1):
        self.sem, self.each, self.step = sem, each, step

    def at(self, b, n):
        return (b + 1) * (self.each * self.step) + n * self.step


def band(half, j):
    lo, hi = P * j - 512 * half, P * j + 2 * P - 512 * half
    a, z = max(lo, 0), min(hi, 512)
    return (a, z, a - lo) if a < z else None


def build(nc, ins, out):
    x, ln_w, ln_b, Wq, Wk, Wv, Wg, g_norm_w, Wo = ins[:9]
    wq, bq, wk, bk, wv, bv, wo, bo, rel_bias, W_r, W_k, W_v, mu_r, mu_k = ins[9:23]
    c_ident, c_cos, c_sin, c_decay, c_mask, c_gamma, c_onehot, c_rows = ins[23:]

    B, T, D = x.shape
    NT = T // P
    NG = NT // 4
    C = D // P
    DK, DV = D // RET_HEADS, 2 * D // RET_HEADS
    HD = D // HEADS
    NU = HEADS * NT
    NS = HEADS // 4 * 2 * NT

    with ExitStack() as ctx:
        def sb(name, shape, dt=F32):
            return ctx.enter_context(nc.sbuf_tensor(name, shape, dt))

        def sem(name):
            return ctx.enter_context(nc.semaphore(name))

        tallies = {"pe": [], "act": [], "dve": [], "pool": [], "sp": []}

        def tally(owner, name, each, step=1):
            t = Tally(sem(name), each, step)
            tallies[owner].append(t)
            return t

        psum = ctx.enter_context(nc.psum_tensor("psum", [P, 8, 512], F32))
        bank = [psum[:, i, :] for i in range(8)]
        bank_pair = [psum[:, 2 * i:2 * i + 2, :].rearrange("p a n -> p (a n)") for i in range(2)]

        ident = sb("ident", [P, P])
        cos = sb("cos", [P, NT, DK])
        sin = sb("sin", [P, NT, DK])
        decay = sb("decay", [P, 8])
        mask = sb("mask", [P, 512])
        gamma = sb("gamma", [P, 2])
        Wqkvg = sb("Wqkvg", [P, C, 6 * D])
        WoS = sb("WoS", [P, 4, D])
        WT = sb("WT", [P, 7, C, D])
        W_R, W_K, W_V, A_Q, A_K, A_V, A_O = range(7)
        vec = sb("vec", [P, 24])
        LN_W, LN_B, BQ, BK, BV, MU_R, MU_K, GW, NU_R, NU_K = [slice(2 * i, 2 * i + 2) for i in range(10)]
        cbias = sb("cbias", [P, D])
        power = sb("power", [P, 16])
        X = sb("X", [P, NT, D])
        Xin = sb("Xin", [P, NT, D])
        aO = Xin
        SQ = sb("SQ", [P, HEADS, T], BF16)
        SK = sb("SK", [P, HEADS, T], BF16)
        Vx = sb("Vx", [P, NT, HEADS, HD + 1])
        band_exp = sb("band_exp", [P, HEADS, 2 * P])
        nT = sb("nT", [P, C, 1 + T])
        nrm = sb("nrm", [P, 4, D])
        xrT = sb("xrT", [P, C, 512])
        xkT = sb("xkT", [P, C, 512])
        kact = sb("kact", [P, 2, 512])
        th = sb("th", [P, 2, 512])
        aT = xrT
        qbd = sb("qbd", [P, 2, 2, 2, P])
        S = sb("S", [P, 2, DV])
        stat = sb("stat", [P, NT, 6])
        mv = sb("mv", [P, NT, 2])
        var2 = sb("var2", [P, 2, NT])
        rs2 = sb("rs2", [P, 2, NT])
        one_r = sb("one_r", [P, NT])
        neg_mr = sb("neg_mr", [P, NT])
        fstat = sb("fstat", [P, 4, 6])
        fmv = sb("fmv", [P, 4, 2])
        farg = sb("farg", [P, 4])
        frs = sb("frs", [P, 4])
        oss = sb("oss", [P, 2, 4])
        oarg = sb("oarg", [P, 4])
        ors = sb("ors", [P, 2, 4])
        mx = sb("mx", [P, 8, 16])
        mrow = sb("mrow", [16, 2, P], BF16)
        orc = sb("orc", [P, 4, 4])
        Z = sb("Z", [P, 7680])

        def cut(at, n):
            return Z[:, at:at + n]

        zn = cut(0, 512).rearrange("p (a n) -> p a n", a=2)
        zT = cut(512, 512).rearrange("p (a c n) -> p a c n", a=2, c=C)
        ra = cut(1024, 512)
        rb = cut(1536, 512)
        qkr = cut(2048, 1024).rearrange("p (a n) -> p a n", a=2)
        kT = cut(3072, 512).rearrange("p (a c n) -> p a c n", a=2, c=2)
        AT = cut(3584, 512)
        v_sb = cut(4096, 1024).rearrange("p (a n) -> p a n", a=2)
        gt = cut(5120, 1024).rearrange("p (a n) -> p a n", a=2)
        y = cut(6144, 512)
        yT = cut(6656, 512)
        sq_junk = cut(7168, 512)
        ring = cut(0, RING * 512).rearrange("p (s n) -> p s n", s=RING)
        cmp = cut(0, 6144).bitcast(BF16).rearrange("p (h s k n) -> p h s k n", h=2, s=2, k=PARTS)
        r1 = cut(6144, 1024).rearrange("p (a n) -> p a n", a=2)
        oT = cut(7168, 512)
        raw = cut(0, 3584).rearrange("p (w c n) -> p w c n", w=7, c=C)

        scratch = nc.dram_tensor("bias_scratch", (HEADS, 384), F32, kind="Internal").ap()
        rows_scratch = nc.dram_tensor("bias_rows", (P, HEADS * 384), F32, kind="Internal").ap()

        parts_scratch = nc.dram_tensor("parts", (2, PARTS, D, T), BF16, kind="Internal").ap()

        s_const = sem("s_const")
        s_w = sem("s_w")
        s_wt = sem("s_wt")
        s_wts = sem("s_wts")
        s_prep = sem("s_prep")
        s_prepv = sem("s_prepv")
        s_bvb = sem("s_bvb")
        s_cb = sem("s_cb")
        s_bb = sem("s_bb")
        s_oh = sem("s_oh")
        s_eb = sem("s_eb")
        s_scr = sem("s_scr")
        s_rep = sem("s_rep")
        s_band = sem("s_band")
        s_rows = sem("s_rows")
        s_rowsk = sem("s_rowsk")
        x_in = Tally(sem("x_in"), 1, 16)
        stored = [tally("sp", f"stored{g}", 1, 16) for g in range(NG)]
        ln1_stat = tally("dve", "ln1_stat", NT)
        ln1_mv = tally("dve", "ln1_mv", NT)
        ln1_arg = tally("pool", "ln1_arg", 2)
        ln1_rs = tally("pool", "ln1_rs", 1)
        ln1_sc = tally("dve", "ln1_sc", 2)
        z_norm = tally("dve", "z_norm", NT)
        resid = tally("pool", "resid", NT)
        z_tp = tally("pe", "z_tp", NT)
        z_T = tally("act", "z_T", 2 * NT)
        p_qk = tally("pe", "p_qk", NT)
        p_v = tally("pe", "p_v", NT)
        p_g = tally("pe", "p_g", NT)
        rope_ab = tally("dve", "rope_ab", 3 * NT)
        rope_sum = tally("pool", "rope_sum", NT)
        rope_qk = tally("pool", "rope_qk", NT)
        qk_tp = tally("pe", "qk_tp", NT)
        kq_T = tally("act", "kq_T", 3 * NT)
        att = tally("pe", "att", NT)
        att_m = tally("dve", "att_m", NT)
        v_cp = tally("act", "v_cp", NT)
        p_o = tally("pe", "p_o", NT)
        p_st = tally("pe", "p_st", NT)
        s_upd = tally("dve", "s_upd", 2 * NT)
        o_sq = tally("act", "o_sq", 4 * NT)
        o_arg = tally("pool", "o_arg", NT)
        o_rs = tally("pool", "o_rs", NT)
        g_tanh = tally("act", "g_tanh", NT)
        gate = tally("dve", "gate", NT)
        y_h = tally("dve", "y_h", 4 * NT)
        y_tp = tally("pe", "y_tp", NT)
        y_T = tally("act", "y_T", NT)
        p_w = tally("pe", "p_w", NT)
        x1 = tally("dve", "x1", NT)
        fn_stat = tally("dve", "fn_stat", 24)
        fn_mv = tally("dve", "fn_mv", 24)
        fn_arg = tally("pool", "fn_arg", 6)
        fn_rs = tally("pool", "fn_rs", 6)
        fn_norm = tally("dve", "fn_norm", 24)
        fn_tp = tally("pe", "fn_tp", 12)
        fn_T = tally("act", "fn_T", 12)
        mix_a = tally("dve", "mix_a", 16)
        mix_b = tally("dve", "mix_b", 16)
        p_k = tally("pe", "p_k", 8)
        k_relu = tally("act", "k_relu", 8)
        k_sq = tally("pool", "k_sq", 8)
        p_r = tally("pe", "p_r", 8)
        r_tanh = tally("act", "r_tanh", 8)
        p_kv = tally("pe", "p_kv", 8)
        kv_r = tally("dve", "kv_r", 8)
        x_ffn = tally("pool", "x_ffn", 8)
        x_cb = tally("pool", "x_cb", 4)
        p_qkT = tally("pe", "p_qkT", 8)
        c_hi = tally("act", "c_hi", 8)
        c_r1 = tally("dve", "c_r1", 8)
        c_mid = tally("dve", "c_mid", 8)
        c_lo = tally("pool", "c_lo", 8)
        parts_out = [tally("sp", f"parts_out{h}", 4, 16) for h in range(2)]
        spread = [tally("sp", f"spread{h}", 12, 16) for h in range(2)]
        p_vx = tally("pe", "p_vx", 4)
        vx_cp = tally("act", "vx_cp", 4)
        mx_s = tally("pe", "mx_s", NU)
        mx_r = tally("dve", "mx_r", NU)
        mx_tp = tally("pe", "mx_tp", 8)
        mx_row = tally("act", "mx_row", 8)
        mx_in = [tally("sp", f"mx_in{i}", 16, 16) for i in range(2)]
        e_s = tally("pe", "e_s", 4 * NS)
        e_p = tally("act", "e_p", 4 * NS)
        e_band = tally("pool", "e_band", 36 * 4)
        e_pv = tally("pe", "e_pv", NS)
        o_cp = tally("act", "o_cp", 8)
        o_tp = tally("pe", "o_tp", 8)
        o_rc = tally("dve", "o_rc", 8)
        o_n = tally("dve", "o_n", 8)
        w_tp = tally("pe", "w_tp", 4)
        w_T = tally("act", "w_T", 4)
        p_wo = tally("pe", "p_wo", 4)
        x_att = tally("dve", "x_att", 4)

        def prime(eng, owner):
            for t in tallies[owner]:
                eng.sem_inc(t.sem, t.each * t.step)

        def need(eng, t, b, n):
            eng.wait_ge(t.sem, t.at(b, n))

        def stand_alone(eng):
            eng.nop(nofuse=True)

        bands = [band((s // 8) % 2, KEY_ORDER[(s // 8) % 2][s % 8]) for s in range(NS)]
        banded = [sum(z is not None for z in bands[:s + 1]) for s in range(NS)]
        units = [min(NU, AHEAD + 2 * (s + 1)) for s in range(NS)]

        def unit(u):
            blk, ii, hh = u // 16, u % 16 // 4, u % 4
            return blk // 2 * 4 + hh, blk % 2 * 4 + ii, blk, hh * 4 + ii

        def qk_order(n):
            return n // 4, n // 2 % 2, n % 2

        def step(s):
            hg, half = s // 16, s // 8 % 2
            return hg, half, KEY_ORDER[half][s % 8]

        WIDE = range(units.index(NU) + 1, NS - 3)

        def col_bank(s, c):
            return bank[(4, 5, 2, 3)[c] if s in WIDE else 4 + c % 2]

        def block_before(s):
            return (s + 3) // 8 if (s + 3) % 8 == 0 and 0 < (s + 3) // 8 < 8 else None

        def output_before(s):
            return (s - 11) // 8 if s >= 11 and (s - 11) % 8 == 0 else None

        N_CONST, N_W = 20, 12

        block = ctx.enter_context(nc.Block())

        @block.sync
        def _(sp):
            prime(sp, "sp")
            xv = x.rearrange("b (t p) d -> b p t d", p=P)
            ov = out.rearrange("b (t p) d -> b p t d", p=P)
            sp.dma_start(Xin[:, :, :], xv[0]).then_inc(x_in.sem, 16)
            n = 0

            def const(dst, src):
                nonlocal n
                n += 1
                sp.dma_start(dst, src, allow_slow_non_contiguous=True).then_inc(s_const, 16)

            const(ident[:, :], c_ident)
            const(vec[:, LN_W], ln_w.rearrange("(c p) -> p c", p=P))
            const(vec[:, LN_B], ln_b.rearrange("(c p) -> p c", p=P))
            const(vec[:, BQ], bq.rearrange("(c p) -> p c", p=P))
            const(vec[:, BK], bk.rearrange("(c p) -> p c", p=P))
            const(vec[:, BV], bv.rearrange("(c p) -> p c", p=P))
            const(vec[:, MU_R], mu_r.rearrange("(c p) -> p c", p=P))
            const(vec[:, MU_K], mu_k.rearrange("(c p) -> p c", p=P))
            const(vec[:, GW.start:GW.start + 1], g_norm_w.rearrange("(p c) -> p c", c=1))
            const(cos[:, :, :], c_cos.rearrange("(t p) n -> p t n", p=P))
            const(sin[:, :, :], c_sin.rearrange("(t p) n -> p t n", p=P))
            const(decay[:, :], c_decay)
            const(mask[:, :], c_mask)
            const(gamma[:, :], c_gamma)
            const(xkT[0:BUCKETS, 0, 0:384], c_onehot)
            const(xkT[0:BUCKETS, 1, 0:HEADS], rel_bias)
            const(xkT[0:HEADS, 1, 32:64], rel_bias.rearrange("k h -> h k"))
            const(xrT[96:128, 0, :], bass.AP(rel_bias.tensor, 0, [[0, 32], [1, BUCKETS * HEADS]]))
            const(xrT[96:128, 1, 0:64], c_rows)
            const(cbias[:, :], bass.AP(bo.tensor, 0, [[0, P], [1, D]]))
            assert n == N_CONST
            n = 0

            def weight(dst, src):
                nonlocal n
                n += 1
                sp.dma_start(dst, src).then_inc(s_w, 16)

            for w, c0, c1 in ((Wq, 0, D), (Wk, D, 2 * D), (Wv, 2 * D, 4 * D), (Wg, 4 * D, 6 * D)):
                weight(Wqkvg[:, :, c0:c1], w.rearrange("(c p) n -> p c n", p=P))
            weight(WoS[:, :, :], Wo.rearrange("(c p) n -> p c n", p=P))
            for i, w in enumerate((W_r, W_k, W_v, wq, wk, wv, wo)):
                weight(raw[:, i], w.rearrange("(c p) n -> p c n", p=P))
            assert n == N_W
            sp.wait_ge(s_eb, 1)
            sp.dma_start(scratch, kact[0:HEADS, 0, 0:384]).then_inc(s_scr, 16)
            sp.wait_ge(s_scr, 16)
            sp.dma_start(rows_scratch, bass.AP(scratch.tensor, 0, [[0, P], [1, HEADS * 384]])).then_inc(s_rep, 16)
            sp.wait_ge(s_rep, 16)
            sp.dma_start(band_exp[:, :, :],
                         bass.AP(rows_scratch.tensor, P - 1, [[HEADS * 384 - 1, P], [384, HEADS], [1, 2 * P]]))\
                .then_inc(s_band, 16)

            def spread_rows(b, h):
                need(sp, parts_out[h], b, 4)
                for i in range(6):
                    for s, (stack, parts) in enumerate(((SQ, Q_PARTS), (SK, K_PARTS))):
                        sp.dma_start(stack[HD * i:HD * i + HD, 8 * h:8 * h + 8, :],
                                     parts_scratch[s, parts[i], h * P:h * P + P, :]
                                     .rearrange("(h d) n -> d h n", d=HD)).then_inc(spread[h].sem, 16)

            with sp.Fori(0, B) as b:
                for h in range(2):
                    for n in range(4 * h, 4 * h + 4):
                        _, g, s = qk_order(n)
                        need(sp, c_lo, b, n + 1)
                        sp.dma_start(parts_scratch[s, :, h * P:h * P + P, 512 * g:512 * g + 512]
                                     .rearrange("k p n -> p k n"),
                                     cmp[:, h, s, :, 512 * g:512 * g + 512]).then_inc(parts_out[h].sem, 16)
                    if h == 0:
                        spread_rows(b, 0)
                spread_rows(b, 1)
                for blk in range(8):
                    need(sp, mx_row, b, blk + 1)
                    h0, q0 = blk // 2 * 4, blk % 2 * 512
                    for hh in range(4):
                        sp.dma_start(SQ[MAX_ROW:MAX_ROW + 1, h0 + hh, q0:q0 + 512],
                                     mrow[4 * hh:4 * hh + 4, blk % 2, :]).then_inc(mx_in[blk % 2].sem, 16)
                need(sp, w_tp, b, 4)
                sp.dma_start(Xin[:, :, :], xv[(b + 1) % B]).then_inc(x_in.sem, 16)
                for g in range(NG):
                    need(sp, x_ffn, b, 4 + 2 * g + 2)
                    sp.dma_start(ov[b, :, 4 * g:4 * g + 4], X[:, 4 * g:4 * g + 4, :]).then_inc(stored[g].sem, 16)
            for g in range(NG):
                need(sp, stored[g], B - 1, 1)
            sp.wait_ge(x_in.sem, 16 * (B + 1))

        @block.tensor
        def _(pe):
            prime(pe, "pe")
            pe.wait_ge(s_const, 16 * N_CONST)
            pe.wait_ge(s_w, 16 * N_W)
            for w in range(7):
                for ci in range(C):
                    for co in range(C):
                        mm = pe.transpose(bank[w][:, ci * D + co * P:ci * D + co * P + P],
                                          raw[:, w, co, ci * P:ci * P + P], ident[:, :])
                mm.then_inc(s_wt, 1)
            pe.matmul(bank[7][0:HEADS, 0:384], xkT[0:BUCKETS, 1, 0:HEADS], xkT[0:BUCKETS, 0, 0:384],
                      start=True, stop=True).then_inc(s_oh, 1)
            pe.wait_ge(s_wts, 7)
            pe.wait_ge(s_bvb, 2)
            for c in range(C):
                mm = pe.matmul(bank[0][:, 0:D], nrm[:, 0, c * P:c * P + P], WT[:, A_O, c, :],
                               start=c == 0, stop=c == C - 1)
            mm.then_inc(s_bb, 1)
            pe.wait_ge(s_cb, 1)
            pe.wait_ge(s_eb, 1)
            pe.wait_ge(s_prep, 1)

            def z_transposes(b, t):
                need(pe, z_norm, b, t + 1)
                need(pe, s_upd, b, 2 * (t - 1) if t else 0)
                if t == 0:
                    need(pe, kv_r, b, 0)
                else:
                    need(pe, z_T, b, 2 * t)
                for c in range(C):
                    mm = pe.transpose(bank[6][:, c * P:c * P + P], zn[:, t % 2, c * P:c * P + P], ident[:, :])
                mm.then_inc(z_tp.sem, 1)

            def project(b, t, dst, c0, done):
                for c in range(C):
                    mm = pe.matmul(bank[dst], zT[:, t % 2, c, :], Wqkvg[:, c, c0:c0 + 512],
                                   start=c == 0, stop=c == C - 1)
                mm.then_inc(done.sem, 1)

            def ln_transposes(b, n):
                need(pe, fn_norm, b, 4 * n + 4)
                need(pe, fn_T, b, 2 * n)
                for c in range(C):
                    for i in range(4):
                        mm = pe.transpose(bank[c][:, i * P:i * P + P], nrm[:, i, c * P:c * P + P], ident[:, :])
                    mm.then_inc(fn_tp.sem, 1)

            def mix_k(b, q):
                need(pe, mix_b, b, 4 * q + 2)
                need(pe, k_relu, b, 2 * q)
                for o in range(2):
                    for c in range(C):
                        mm = pe.matmul(bank[2 + o], WT[:, W_K, c, o * P:o * P + P], xkT[:, c, :],
                                       start=c == 0, stop=c == C - 1)
                    mm.then_inc(p_k.sem, 1)

            def mix_r(b, q):
                need(pe, mix_b, b, 4 * q + 4)
                need(pe, r_tanh, b, 2 * q)
                for pr in range(2):
                    for i in range(2):
                        t = 2 * pr + i
                        for c in range(C):
                            mm = pe.matmul(bank[4 + pr][:, i * D:i * D + D], xrT[:, c, t * P:t * P + P],
                                           WT[:, W_R, c, :], start=c == 0, stop=c == C - 1)
                    mm.then_inc(p_r.sem, 1)

            def mix_kv(b, q):
                need(pe, k_sq, b, 2 * q + 2)
                need(pe, kv_r, b, 2 * q)
                for pr in range(2):
                    for i in range(2):
                        t = 2 * pr + i
                        for o in range(2):
                            mm = pe.matmul(bank[6 + pr][:, i * D:i * D + D], kact[:, o, t * P:t * P + P],
                                           WT[:, W_V, o, :], start=o == 0, stop=o == 1)
                    mm.then_inc(p_kv.sem, 1)

            def channel_mix(b, f, first):
                n, q = (0, 4)[f], 2 * f
                if first:
                    ln_transposes(b, n)
                    mix_k(b, q)
                mix_r(b, q)
                ln_transposes(b, n + 1)
                mix_kv(b, q)
                mix_k(b, q + 1)
                mix_r(b, q + 1)
                mix_kv(b, q + 1)

            def qk_project(b, n):
                h, g, side = qk_order(n)
                need(pe, c_r1, b, n - 1)
                for c in range(C):
                    mm = pe.matmul(bank[2 + n % 2], WT[:, A_Q + side, c, h * P:h * P + P],
                                   nT[:, c, 1 + 512 * g:513 + 512 * g], start=c == 0, stop=c == C - 1)
                mm.then_inc(p_qkT.sem, 1)

            def v_project(b, pr):
                need(pe, vx_cp, b, pr - 1)
                for i in range(2):
                    t = 2 * pr + i
                    for c in range(C):
                        mm = pe.matmul(bank[4 + pr % 2][:, i * D:i * D + D], nT[:, c, 1 + t * P:1 + t * P + P],
                                       WT[:, A_V, c, :], start=c == 0, stop=c == C - 1)
                mm.then_inc(p_vx.sem, 1)

            def score_rows(b, u):
                h, i, _, _ = unit(u)
                if u % (NU // 2) == 0:
                    need(pe, spread[u // (NU // 2)], b, 12)
                if u < 2:
                    need(pe, fn_T, b, 8)
                    need(pe, c_r1, b, 8)
                else:
                    need(pe, mx_r, b, u - 1)
                for k in range(2):
                    mm = pe.matmul(bank[2 * (u % 2) + k], SQ[0:MAX_ROW, h, i * P:i * P + P],
                                   SK[0:MAX_ROW, h, 512 * k:512 * k + 512], start=True, stop=True)
                mm.then_inc(mx_s.sem, 1)

            def max_transpose(b, blk):
                need(pe, mx_r, b, 16 * blk + 16)
                if blk == 0:
                    need(pe, kv_r, b, 4)
                else:
                    need(pe, mx_row, b, blk)
                    need(pe, o_n, b, blk - 1)
                pe.transpose(bank[7][0:16, 0:P], mx[:, blk, :], ident[:, :]).then_inc(mx_tp.sem, 1)

            def score_cols(b, s, c):
                hg, half, j = step(s)
                n = 4 * s + c
                if c == 0 and s % 8 == 0:
                    need(pe, mx_in[(s // 8) % 2], b, 4 * (s // 16 + 1))
                if n < 2:
                    need(pe, vx_cp, b, 4)
                elif s == WIDE.start and c >= 2:
                    need(pe, mx_r, b, NU)
                elif s in WIDE and s > WIDE.start:
                    need(pe, e_p, b, n - 3)
                else:
                    need(pe, e_p, b, n - 1)
                h = 4 * hg + c
                pe.matmul(col_bank(s, c), SK[:, h, j * P:j * P + P], SQ[:, h, 512 * half:512 * half + 512],
                          start=True, stop=True).then_inc(e_s.sem, 1)

            def weigh(b, s):
                hg, half, j = step(s)
                if bands[s]:
                    need(pe, e_band, b, 4 * banded[s])
                else:
                    need(pe, e_p, b, 4 * s + 4)
                if s == 0:
                    need(pe, kv_r, b, 4)
                elif s % 8 == 0:
                    need(pe, o_cp, b, s // 8)
                for c in range(4):
                    mm = pe.matmul(bank[6][32 * c:32 * c + HD + 1, :], Vx[:, j, 4 * hg + c, :],
                                   ring[:, (4 * s + c) % RING, :], start=s % 8 == 0, stop=s % 8 == 7)
                mm.then_inc(e_pv.sem, 1)

            def output_transposes(b, k):
                need(pe, o_cp, b, k + 1)
                need(pe, mx_row, b, min(k + 2, 8))
                need(pe, o_n, b, k)
                for i in range(4):
                    mm = pe.transpose(bank[7][:, i * P:i * P + P], oT[:, i * P:i * P + P], ident[:, :])
                mm.then_inc(o_tp.sem, 1)

            def w_transposes(b, pr):
                need(pe, o_n, b, 7 + pr // 2)
                if pr < 2:
                    need(pe, mx_r, b, NU)
                else:
                    need(pe, w_T, b, pr - 1)
                if pr == 1:
                    need(pe, e_p, b, 4 * WIDE.stop)
                for i in range(2):
                    for c in range(C):
                        mm = pe.transpose(bank[2 * (pr % 2)][:, (2 * i + c) * P:(2 * i + c) * P + P],
                                          aO[:, 2 * pr + i, c * P:c * P + P], ident[:, :])
                mm.then_inc(w_tp.sem, 1)

            def w_project(b, pr):
                need(pe, w_T, b, pr + 1)
                if pr >= 2:
                    need(pe, x_att, b, pr - 1)
                for i in range(2):
                    for c in range(C):
                        mm = pe.matmul(bank[2 * (pr % 2) + 1][:, i * D:i * D + D],
                                       aT[:, pr % 2, (2 * i + c) * P:(2 * i + c) * P + P],
                                       WT[:, A_O, c, :], start=c == 0, stop=c == C - 1)
                mm.then_inc(p_wo.sem, 1)

            with pe.Fori(0, B) as b:
                z_transposes(b, 0)
                for t in range(NT + 2):
                    if t == NT:
                        need(pe, rope_ab, b, 3 * NT)
                        need(pe, v_cp, b, NT)
                        ln_transposes(b, 0)
                    if t < NT:
                        need(pe, z_T, b, 2 * t + 2)
                        need(pe, rope_ab, b, 3 * t)
                        if t == 0:
                            need(pe, fn_T, b, 0)
                        project(b, t, 0, 0, p_qk)
                    if 1 <= t <= NT:
                        u = t - 1
                        need(pe, kq_T, b, 3 * u + 3)
                        need(pe, att_m, b, u)
                        if u == 0:
                            need(pe, r_tanh, b, 0)
                        for pr in range(2):
                            mm = pe.matmul(bank[4][:, 256 * pr:256 * pr + 256], kT[:, u % 2, pr, :],
                                           qbd[:, u % 2, pr, :, :].rearrange("p a n -> p (a n)"),
                                           start=True, stop=True)
                        mm.then_inc(att.sem, 1)
                    if t < NT:
                        need(pe, v_cp, b, t)
                        project(b, t, 1, 512, p_v)
                    if 1 <= t <= NT:
                        need(pe, att_m, b, u + 1)
                        need(pe, v_cp, b, u + 1)
                        need(pe, s_upd, b, 2 * u)
                        need(pe, y_h, b, 4 * u)
                        for h in range(RET_HEADS):
                            o = bank[5][:, h * DV:h * DV + DV]
                            mm = pe.matmul(o, AT[:, h * P:h * P + P], v_sb[:, u % 2, h * DV:h * DV + DV],
                                           start=True, stop=u == 0)
                            if u > 0:
                                mm = pe.matmul(o, qbd[:, u % 2, h // 2, h % 2, :], S[:, h // 2, :],
                                               start=False, stop=True)
                        mm.then_inc(p_o.sem, 1)
                        need(pe, z_T, b, min(2 * u + 4, 2 * NT))
                        for h in range(RET_HEADS):
                            mm = pe.matmul(bank[6][64 * (h % 2):64 * (h % 2) + 64, (h // 2) * DV:(h // 2) * DV + DV],
                                           qkr[:, u % 2, 256 + h * DK:256 + h * DK + DK],
                                           v_sb[:, u % 2, h * DV:h * DV + DV], start=True, stop=True,
                                           skip_group_check=True)
                        mm.then_inc(p_st.sem, 1)
                    if t < NT:
                        need(pe, gate, b, t)
                        if t == 0:
                            need(pe, k_relu, b, 0)
                        project(b, t, 2, 1024, p_g)
                        need(pe, rope_qk, b, t + 1)
                        need(pe, kq_T, b, 3 * t)
                        for i in range(4):
                            mm = pe.transpose(bank[3][:, i * P:i * P + P], qkr[:, t % 2, i * P:i * P + P], ident[:, :])
                        mm.then_inc(qk_tp.sem, 1)
                    if t >= 2:
                        u = t - 2
                        need(pe, y_h, b, 4 * u + 4)
                        need(pe, x1, b, u)
                        if u == 0:
                            need(pe, kv_r, b, 0)
                        for i in range(4):
                            mm = pe.transpose(bank[7][:, i * P:i * P + P], y[:, i * P:i * P + P], ident[:, :])
                        mm.then_inc(y_tp.sem, 1)
                    if t + 1 < NT:
                        z_transposes(b, t + 1)
                    if t >= 2:
                        need(pe, y_T, b, u + 1)
                        for h in range(RET_HEADS):
                            mm = pe.matmul(bank[7][:, 0:D], yT[:, h * P:h * P + P], WoS[:, h, :],
                                           start=h == 0, stop=h == 3)
                        mm.then_inc(p_w.sem, 1)
                    if t == NT:
                        need(pe, gate, b, NT)
                        need(pe, kq_T, b, 3 * NT)
                        mix_k(b, 0)
                need(pe, s_upd, b, 2 * NT)
                need(pe, x1, b, NT)
                channel_mix(b, 0, False)
                ln_transposes(b, 2)
                need(pe, k_relu, b, 4)
                need(pe, fn_T, b, 6)
                need(pe, r_tanh, b, 4)
                for n in range(8):
                    if n == 2:
                        v_project(b, 0)
                        v_project(b, 1)
                        ln_transposes(b, 3)
                        need(pe, fn_T, b, 8)
                    qk_project(b, n)
                v_project(b, 2)
                v_project(b, 3)
                for u in range(AHEAD):
                    score_rows(b, u)
                    if u == 17:
                        max_transpose(b, 0)
                u = AHEAD
                for s in range(NS + LAG):
                    if output_before(s) is not None:
                        output_transposes(b, output_before(s))
                    if s < NS:
                        for c in range(4):
                            score_cols(b, s, c)
                            while c == 1 and u < units[s]:
                                score_rows(b, u)
                                u += 1
                        if block_before(s) is not None:
                            max_transpose(b, block_before(s))
                    if s >= LAG:
                        weigh(b, s - LAG)
                    if s == NS - 3:
                        w_transposes(b, 0)
                    if s == NS - 2:
                        w_project(b, 0)
                        w_transposes(b, 1)
                    if s == NS - 1:
                        w_project(b, 1)
                output_transposes(b, 7)
                for pr in (2, 3):
                    w_transposes(b, pr)
                for pr in (2, 3):
                    w_project(b, pr)
                need(pe, x_att, b, 4)
                channel_mix(b, 1, True)

        @block.scalar
        def _(act):
            prime(act, "act")
            for w in range(7):
                act.wait_ge(s_wt, w + 1)
                scale = {A_Q: 0.25, W_V: 0.5}.get(w, 1.0)
                nc.scalar.activation(WT[:, w].rearrange("p c n -> p (c n)"), bank[w], ACT.Identity,
                                     scale=scale).then_inc(s_wts, 1)
            act.wait_ge(s_oh, 1)
            act.wait_ge(s_prepv, 1)
            nc.scalar.activation(kact[0:HEADS, 0, 0:384], bank[7][0:HEADS, 0:384], ACT.Exp,
                                 bias=frs[0:HEADS, 0:1]).then_inc(s_eb, 1)
            act.wait_ge(s_const, 16 * N_CONST)
            for h in range(HEADS):
                nc.scalar.activation(SK[96:128, h, :].rearrange("p (k n) -> p k n", n=P),
                                     xrT[96:128, 1, 0:8].unsqueeze(2).to_broadcast([32, 8, P]),
                                     ACT.Identity).then_inc(s_rowsk, 1)
            act.wait_ge(s_cb, 1)
            act.wait_ge(s_scr, 16)

            def ln_copies(b, n):
                g = n % 2
                if n < 2:
                    need(act, mix_b, b, 0)
                elif n < 4:
                    need(act, mix_b, b, 8)
                else:
                    need(act, p_vx, b, 4)
                for c in range(C):
                    need(act, fn_tp, b, 2 * n + c + 1)
                    nc.scalar.copy(nT[:, c, 1 + 512 * g:513 + 512 * g], bank[c]).then_inc(fn_T.sem, 1)

            def relus(b, q):
                for o in range(2):
                    need(act, p_k, b, 2 * q + o + 1)
                    need(act, p_kv, b, 2 * q)
                    nc.scalar.activation(kact[:, o, :], bank[2 + o], ACT.Relu).then_inc(k_relu.sem, 1)

            def tanhs(b, q):
                for pr in range(2):
                    need(act, p_r, b, 2 * q + pr + 1)
                    need(act, x_ffn, b, 2 * q + pr - 1)
                    nc.scalar.activation(th[:, pr, :], bank[4 + pr], ACT.Tanh, scale=0.5)\
                        .then_inc(r_tanh.sem, 1)

            def channel_mix(b, f, first):
                n, q = (0, 4)[f], 2 * f
                if first:
                    ln_copies(b, n)
                    relus(b, q)
                tanhs(b, q)
                ln_copies(b, n + 1)
                relus(b, q + 1)
                tanhs(b, q + 1)

            def z_copies(b, t):
                need(act, z_tp, b, t + 1)
                for c in range(C):
                    need(act, p_g, b, t - 1)
                    nc.scalar.activation(zT[:, t % 2, c, :], bank[6][:, c * P:c * P + P], ACT.Identity,
                                         scale=vec[:, LN_W.start + c:LN_W.start + c + 1],
                                         bias=vec[:, LN_B.start + c:LN_B.start + c + 1]).then_inc(z_T.sem, 1)

            with act.Fori(0, B) as b:
                z_copies(b, 0)
                for t in range(NT + 2):
                    if t < NT:
                        need(act, p_v, b, t + 1)
                        need(act, p_st, b, t - 1)
                        nc.scalar.copy(v_sb[:, t % 2, :], bank[1]).then_inc(v_cp.sem, 1)
                    if 1 <= t <= NT:
                        u = t - 1
                        need(act, p_o, b, u + 1)
                        need(act, o_arg, b, u - 1)
                        need(act, o_sq, b, 4 * u)
                        for h in range(RET_HEADS):
                            nc.scalar.activation(sq_junk[:, h * DV:h * DV + DV], bank[5][:, h * DV:h * DV + DV], ACT.Square,
                                                 accum_out=oss[:, u % 2, h:h + 1]).then_inc(o_sq.sem, 1)
                    if t < NT:
                        need(act, p_g, b, t + 1)
                        need(act, y_h, b, 4 * (t - 1))
                        nc.scalar.activation(gt[:, t % 2, :], bank[2], ACT.Tanh, scale=0.5)\
                            .then_inc(g_tanh.sem, 1)
                        need(act, qk_tp, b, t + 1)
                        need(act, p_o, b, t - 1)
                        quad = bank[3].rearrange("p (a n) -> p a n", a=4)
                        nc.scalar.copy(qbd[0:64, t % 2, :, 0, :], quad[0:64, 0:2, :]).then_inc(kq_T.sem, 1)
                        nc.scalar.copy(qbd[64:128, t % 2, :, 1, :], quad[64:128, 0:2, :]).then_inc(kq_T.sem, 1)
                        nc.scalar.copy(kT[:, t % 2, :, :], quad[:, 2:4, :]).then_inc(kq_T.sem, 1)
                    if t == NT:
                        ln_copies(b, 0)
                    if t >= 2:
                        need(act, y_tp, b, t - 1)
                        need(act, p_w, b, t - 2)
                        nc.scalar.copy(yT[:, :], bank[7]).then_inc(y_T.sem, 1)
                    if t + 1 < NT:
                        z_copies(b, t + 1)
                    if t == NT:
                        relus(b, 0)
                channel_mix(b, 0, False)
                def v_copies(pr):
                    need(act, p_vx, b, pr + 1)
                    nc.scalar.copy(Vx[:, 2 * pr:2 * pr + 2, :, 0:HD],
                                   bank[4 + pr % 2].rearrange("p (t h d) -> p t h d", t=2, h=HEADS))\
                        .then_inc(vx_cp.sem, 1)

                ln_copies(b, 2)
                for n in range(8):
                    h, g, s = qk_order(n)
                    if n == 2:
                        v_copies(0)
                        v_copies(1)
                        ln_copies(b, 3)
                    need(act, p_qkT, b, n + 1)
                    at = (BQ, BK)[s].start + h
                    nc.scalar.activation(cmp[:, h, s, 0, 512 * g:512 * g + 512], bank[2 + n % 2],
                                         ACT.Identity, bias=vec[:, at:at + 1]).then_inc(c_hi.sem, 1)
                v_copies(2)
                v_copies(3)

                def max_rows(blk):
                    need(act, mx_tp, b, blk + 1)
                    need(act, mx_in[blk % 2], b, 4 * (blk // 2))
                    nc.scalar.mul(mrow[:, blk % 2, :], bank[7][0:16, 0:P], -1.0).then_inc(mx_row.sem, 1)

                def output_copy(k):
                    need(act, e_pv, b, 8 * k + 8)
                    need(act, o_tp, b, k)
                    nc.scalar.copy(oT[:, :], bank[6]).then_inc(o_cp.sem, 1)

                max_rows(0)
                for h in range(2):
                    need(act, parts_out[h], b, 4)
                for s in range(NS):
                    if s < NS:
                        need(act, e_pv, b, max(s - 2, 0))
                        for c in range(4):
                            n = 4 * s + c
                            need(act, e_s, b, n + 1)
                            nc.scalar.activation(ring[:, n % RING, :], col_bank(s, c), ACT.Exp)\
                                .then_inc(e_p.sem, 1)
                            if c == 3 and block_before(s) is not None:
                                max_rows(block_before(s))
                            if c == 1 and s % 8 == 2 and s > 2:
                                output_copy(s // 8 - 1)
                    for pr, at in ((0, NS - 3), (1, NS - 2)):
                        if s == at:
                            need(act, w_tp, b, pr + 1)
                            nc.scalar.copy(aT[:, pr % 2, :], bank[2 * (pr % 2)]).then_inc(w_T.sem, 1)
                output_copy(7)
                for pr in (2, 3):
                    need(act, w_tp, b, pr + 1)
                    need(act, p_wo, b, pr - 1)
                    nc.scalar.copy(aT[:, pr % 2, :], bank[2 * (pr % 2)]).then_inc(w_T.sem, 1)
                channel_mix(b, 1, True)

        @block.vector
        def _(dve):
            prime(dve, "dve")
            chain = [1]

            def link(i):
                chain[0] += 1
                i.then_inc(s_prepv, 1)
                dve.wait_ge(s_prepv, chain[0])

            dve.wait_ge(s_const, 16 * N_CONST)
            nc.vector.tensor_reduce(frs[0:HEADS, 0:1], xkT[0:HEADS, 1, 32:64], AX_X, ALU.max, negate=True)\
                .then_inc(s_prepv, 1)
            link(nc.vector.memset(nT[:, :, 0:1], 0.0))
            link(nc.vector.memset(qbd[:, :, :, :, :], 0.0))
            link(nc.vector.memset(Vx[:, :, :, HD:HD + 1], 1.0))
            link(nc.vector.memset(power[:, :], -0.5))
            link(nc.vector.memset(S[:, :, :], 0.0))
            for a, z in ((MU_R, NU_R), (MU_K, NU_K)):
                link(nc.vector.tensor_scalar(vec[:, z], vec[:, a], -1.0, 1.0, ALU.mult, ALU.add))
            link(nc.vector.tensor_scalar(vec[:, BQ], vec[:, BQ], 0.25, None, ALU.mult))
            link(nc.vector.memset(nrm[:, 0, :], 1.0))
            for c in range(C):
                nc.vector.tensor_scalar(nrm[:, 0, c * P:c * P + P], nrm[:, 0, c * P:c * P + P],
                                        vec[:, BV.start + c:BV.start + c + 1], None, ALU.mult).then_inc(s_bvb, 1)
            dve.wait_ge(s_w, 16 * N_W)
            link(nc.vector.tensor_scalar(WoS[:, :, :], WoS[:, :, :], vec[:, GW.start:GW.start + 1], 0.5,
                                         ALU.mult, ALU.mult))
            R = slice(96, 128)
            table = xrT[R, 0, :].rearrange("p (k h) -> p h k", k=BUCKETS)
            top, d0, d1 = (xrT[R, 1, 64 + 16 * i:80 + 16 * i] for i in range(3))
            wide = [xrT[R, 1, 128 + 128 * i:256 + 128 * i] for i in range(3)]
            cut3 = [w.rearrange("p (h k) -> p h k", h=HEADS) for w in wide]
            hi = nrm[R, 2, 0:64].bitcast(BF16).rearrange("p (h k) -> p h k", h=HEADS)
            mid = nrm[R, 2, 64:128].bitcast(BF16).rearrange("p (h k) -> p h k", h=HEADS)
            low = nrm[R, 2, 128:192].bitcast(BF16).rearrange("p (h k) -> p h k", h=HEADS)
            where0 = xrT[R, 1, 8:16].unsqueeze(1).to_broadcast([32, HEADS, 8])
            where1 = xrT[R, 1, 16:24].unsqueeze(1).to_broadcast([32, HEADS, 8])
            link(nc.vector.tensor_reduce(top, table, AX_X, ALU.max))
            link(nc.vector.tensor_tensor(d0, table[:, :, 0], top, ALU.subtract))
            link(nc.vector.tensor_tensor(d1, table[:, :, BUCKETS - 1], top, ALU.subtract))
            link(nc.vector.tensor_tensor(cut3[0], d0.unsqueeze(2).to_broadcast([32, HEADS, 8]), where0, ALU.mult))
            link(nc.vector.tensor_tensor(cut3[1], d1.unsqueeze(2).to_broadcast([32, HEADS, 8]), where1, ALU.mult))
            link(nc.vector.tensor_tensor(wide[0], wide[0], wide[1], ALU.add))
            link(nc.vector.tensor_copy(hi, cut3[0]))
            link(nc.vector.scalar_tensor_tensor(cut3[1], hi, xrT[R, 1, 24:25], cut3[0], ALU.mult, ALU.add))
            link(nc.vector.tensor_copy(mid, cut3[1]))
            link(nc.vector.scalar_tensor_tensor(cut3[2], mid, xrT[R, 1, 25:26], cut3[1], ALU.mult, ALU.add))
            link(nc.vector.tensor_copy(low, cut3[2]))
            for h in range(HEADS):
                nc.vector.tensor_copy(SQ[R, h, :].rearrange("p (k n) -> p k n", n=P),
                                      low[:, h, :].unsqueeze(2).to_broadcast([32, 8, P])).then_inc(s_rows, 1)
            dve.wait_ge(s_rowsk, HEADS)
            dve.wait_ge(s_rows, HEADS)
            dve.wait_ge(s_bb, 1)
            nc.vector.tensor_tensor(cbias[:, :], bank[0][:, 0:D], cbias[:, :], ALU.add).then_inc(s_cb, 1)
            dve.wait_ge(s_cb, 1)
            dve.wait_ge(s_wts, 7)
            nc.vector.memset(bank[6], 0.0).then_inc(s_prep, 1)
            dve.wait_ge(s_prep, 1)

            def ln_stats(b, n):
                g = n % 2
                if n < 2:
                    need(dve, x1, b, 4 * g + 4)
                elif n < 4:
                    need(dve, x_ffn, b, 2 * g + 2)
                else:
                    need(dve, x_att, b, 2 * g + 2)
                need(dve, fn_norm, b, 4 * n)
                for i in range(4):
                    nc.vector.bn_stats(fstat[:, i, :], X[:, 4 * g + i, :]).then_inc(fn_stat.sem, 1)
                need(dve, fn_stat, b, 4 * n + 4)
                stand_alone(dve)
                for i in range(4):
                    nc.vector.bn_aggr(fmv[:, i, :], fstat[:, i, :]).then_inc(fn_mv.sem, 1)

            def ln_norms(b, n):
                g = n % 2
                need(dve, fn_rs, b, n + 1)
                need(dve, fn_tp, b, 2 * n)
                for i in range(4):
                    nc.vector.tensor_scalar(nrm[:, i, :], X[:, 4 * g + i, :], fmv[:, i, 0:1], frs[:, i:i + 1],
                                            ALU.subtract, ALU.mult).then_inc(fn_norm.sem, 1)

            def mixes(b, q):
                g, n = q % 2, q % 2 + (0, 4)[q // 2]
                need(dve, fn_T, b, 2 * n + 2)
                for i, (dst, mu, nu, read) in enumerate(((xkT, MU_K, NU_K, p_k), (xrT, MU_R, NU_R, p_r))):
                    need(dve, read, b, 2 * q)
                    if q == 2 and dst is xrT:
                        need(dve, p_wo, b, 4)
                    for c in range(C):
                        nc.vector.tensor_scalar(dst[:, c, :], nT[:, c, 1 + 512 * g:513 + 512 * g],
                                                vec[:, mu.start + c:mu.start + c + 1], None, ALU.mult)\
                            .then_inc(mix_a.sem, 1)
                    for c in range(C):
                        need(dve, mix_a, b, 4 * q + 2 * i + c + 1)
                        nc.vector.scalar_tensor_tensor(dst[:, c, :], nT[:, c, 512 * g:512 + 512 * g],
                                                       vec[:, nu.start + c:nu.start + c + 1], dst[:, c, :],
                                                       ALU.mult, ALU.add).then_inc(mix_b.sem, 1)

            def gated(b, q):
                for pr in range(2):
                    need(dve, p_kv, b, 2 * q + pr + 1)
                    need(dve, r_tanh, b, 2 * q + pr + 1)
                    nc.vector.scalar_tensor_tensor(th[:, pr, :], th[:, pr, :], 1.0, bank[6 + pr],
                                                   ALU.add, ALU.mult).then_inc(kv_r.sem, 1)

            def x_out(b, t):
                need(dve, p_w, b, t + 1)
                need(dve, resid, b, t + 1)
                nc.vector.tensor_tensor(X[:, t, :], bank[7][:, 0:D], X[:, t, :], ALU.add).then_inc(x1.sem, 1)

            def z_norms(b, t):
                need(dve, z_tp, b, t - 1)
                nc.vector.tensor_scalar(zn[:, t % 2, :], Xin[:, t, :], mv[:, t, 0:1], rs2[:, 1, t:t + 1],
                                        ALU.subtract, ALU.mult).then_inc(z_norm.sem, 1)

            with dve.Fori(0, B) as b:
                dve.wait_ge(x_in.sem, 16 * (b + 1))
                for t in range(NT):
                    nc.vector.bn_stats(stat[:, t, :], Xin[:, t, :]).then_inc(ln1_stat.sem, 1)
                need(dve, resid, b, 0)
                need(dve, ln1_stat, b, NT)
                stand_alone(dve)
                for t in range(NT):
                    nc.vector.bn_aggr(mv[:, t, :], stat[:, t, :]).then_inc(ln1_mv.sem, 1)
                need(dve, ln1_rs, b, 1)
                z_norms(b, 0)
                nc.vector.tensor_scalar(one_r[:, :], rs2[:, 0, :], 1.0, None, ALU.add).then_inc(ln1_sc.sem, 1)
                nc.vector.scalar_tensor_tensor(neg_mr[:, :], mv[:, :, 0], -1.0, rs2[:, 0, :], ALU.mult, ALU.mult)\
                    .then_inc(ln1_sc.sem, 1)
                for t in range(NT + 2):
                    if t + 1 < NT:
                        z_norms(b, t + 1)
                    if t < NT:
                        need(dve, p_qk, b, t + 1)
                        need(dve, rope_sum, b, t)
                        qk = bank[0].rearrange("p (h a d) -> p h a d", h=8, a=2)
                        rbv = rb[:, :].rearrange("p (h a d) -> p h a d", h=8, a=2)
                        nc.vector.tensor_tensor(ra[:, :].rearrange("p (h d) -> p h d", h=8),
                                                bank[0].rearrange("p (h d) -> p h d", h=8),
                                                cos[:, t, :].unsqueeze(1).to_broadcast([P, 8, DK]), ALU.mult)\
                            .then_inc(rope_ab.sem, 1)
                        for a in range(2):
                            sn = sin[:, t, 32 * a:32 * a + 32].unsqueeze(1).to_broadcast([P, 8, DK // 2])
                            nc.vector.tensor_tensor(rbv[:, :, a, :], qk[:, :, 1 - a, :], sn, ALU.mult)\
                                .then_inc(rope_ab.sem, 1)
                    if 1 <= t <= NT:
                        u = t - 1
                        need(dve, att, b, u + 1)
                        need(dve, p_o, b, u)
                        nc.vector.tensor_tensor(AT[:, :], bank[4], mask[:, :], ALU.mult)\
                            .then_inc(att_m.sem, 1)
                        need(dve, p_st, b, u + 1)
                        for pr in range(2):
                            new = bank[6][:, pr * DV:pr * DV + DV]
                            if u == 0:
                                i = nc.vector.tensor_copy(S[:, pr, :], new)
                            else:
                                need(dve, s_upd, b, 2 * u + pr - 1)
                                i = nc.vector.scalar_tensor_tensor(S[:, pr, :], S[:, pr, :], gamma[:, pr:pr + 1],
                                                                   new, ALU.mult, ALU.add)
                            i.then_inc(s_upd.sem, 1)
                    if t == NT:
                        mixes(b, 0)
                    if t < NT:
                        need(dve, p_g, b, t + 1)
                        need(dve, g_tanh, b, t + 1)
                        nc.vector.scalar_tensor_tensor(gt[:, t % 2, :], gt[:, t % 2, :], 1.0, bank[2],
                                                       ALU.add, ALU.mult).then_inc(gate.sem, 1)
                    if 1 <= t <= NT:
                        need(dve, o_rs, b, u + 1)
                        need(dve, gate, b, u + 1)
                        need(dve, y_tp, b, u)
                        for h in range(RET_HEADS):
                            nc.vector.scalar_tensor_tensor(y[:, h * DV:h * DV + DV], bank[5][:, h * DV:h * DV + DV],
                                                           ors[:, u % 2, h:h + 1], gt[:, u % 2, h * DV:h * DV + DV],
                                                           ALU.mult, ALU.mult).then_inc(y_h.sem, 1)
                    if t >= 2:
                        x_out(b, t - 2)
                    if t == 6:
                        ln_stats(b, 0)
                        ln_norms(b, 0)
                ln_stats(b, 1)
                ln_norms(b, 1)
                mixes(b, 1)
                gated(b, 0)
                ln_stats(b, 2)
                ln_norms(b, 2)
                gated(b, 1)
                ln_stats(b, 3)

                ln_norms(b, 3)
                for n in range(8):
                    h, g, s = qk_order(n)
                    need(dve, c_hi, b, n + 1)
                    need(dve, c_lo, b, n - 1)
                    at = (BQ, BK)[s].start + h
                    tok = slice(512 * g, 512 * g + 512)
                    nc.vector.scalar_tensor_tensor(r1[:, n % 2, :], bank[2 + n % 2], vec[:, at:at + 1],
                                                   cmp[:, h, s, 0, tok], ALU.add, ALU.subtract)\
                        .then_inc(c_r1.sem, 1)
                    need(dve, c_r1, b, n + 1)
                    nc.vector.tensor_copy(cmp[:, h, s, 1, tok], r1[:, n % 2, :]).then_inc(c_mid.sem, 1)

                def row_max(u):
                    _, _, blk, col = unit(u)
                    need(dve, mx_s, b, u + 1)
                    nc.vector.tensor_reduce(mx[:, blk, col:col + 1], bank_pair[u % 2], AX_X, ALU.max)\
                        .then_inc(mx_r.sem, 1)

                def attention_out(pr):
                    need(dve, p_wo, b, pr + 1)
                    need(dve, x_cb, b, pr + 1)
                    xs = X[:, 2 * pr:2 * pr + 2, :].rearrange("p t n -> p (t n)")
                    nc.vector.tensor_tensor(xs, bank[2 * (pr % 2) + 1], xs, ALU.add).then_inc(x_att.sem, 1)

                for u in range(AHEAD):
                    row_max(u)
                u = AHEAD
                for s in range(NS + 4):
                    if s < NS:
                        while u < units[s]:
                            row_max(u)
                            u += 1
                    k = output_before(s)
                    if k is not None:
                        need(dve, o_tp, b, k + 1)
                        o = bank[7].rearrange("p (t h d) -> p t h d", t=4, h=4)
                        hg, half = k // 2, k % 2
                        nc.vector.reciprocal(orc[:, :, :], o[:, :, :, HD]).then_inc(o_rc.sem, 1)
                        need(dve, o_rc, b, k + 1)
                        dst = aO[:, 4 * half:4 * half + 4, 64 * hg:64 * hg + 64].rearrange("p t (h d) -> p t h d", h=4)
                        for i in range(4):
                            ins_ = nc.vector.tensor_tensor(dst[:, i], o[:, i, :, 0:HD],
                                                           orc[:, i, :].unsqueeze(2).to_broadcast([P, 4, HD]), ALU.mult)
                        ins_.then_inc(o_n.sem, 1)
                    if s in (NS - 2, NS - 1):
                        attention_out(s - NS + 2)
                attention_out(2)
                attention_out(3)
                ln_stats(b, 4)
                ln_norms(b, 4)
                mixes(b, 2)
                ln_stats(b, 5)
                ln_norms(b, 5)
                mixes(b, 3)
                gated(b, 2)
                gated(b, 3)

        @block.gpsimd
        def _(pool):
            prime(pool, "pool")
            pool.wait_ge(s_prep, 1)
            pool.wait_ge(s_eb, 1)

            def rsqrts(b, n):
                need(pool, fn_mv, b, 4 * n + 4)
                need(pool, fn_norm, b, 4 * n)
                stand_alone(pool)
                nc.gpsimd.tensor_scalar(farg[:, :], fmv[:, :, 1], EPS, None, ALU.add).then_inc(fn_arg.sem, 1)
                need(pool, fn_arg, b, n + 1)
                nc.gpsimd.tensor_tensor(frs[:, :], farg[:, :], power[:, 0:4], ALU.pow).then_inc(fn_rs.sem, 1)

            def squares(b, q):
                for o in range(2):
                    need(pool, k_relu, b, 2 * q + o + 1)
                    nc.gpsimd.tensor_tensor(kact[:, o, :], kact[:, o, :], kact[:, o, :], ALU.mult)\
                        .then_inc(k_sq.sem, 1)

            def adds(b, q):
                g = q % 2
                for pr in range(2):
                    need(pool, kv_r, b, 2 * q + pr + 1)
                    t = 4 * g + 2 * pr
                    xs = X[:, t:t + 2, :].rearrange("p t n -> p (t n)")
                    nc.gpsimd.tensor_tensor(xs, xs, th[:, pr, :], ALU.add).then_inc(x_ffn.sem, 1)

            with pool.Fori(0, B) as b:
                need(pool, ln1_mv, b, NT)
                need(pool, z_norm, b, 0)
                stand_alone(pool)
                nc.gpsimd.tensor_scalar(var2[:, 0, :], mv[:, :, 1], 1.0, EPS, ALU.mult, ALU.add)\
                    .then_inc(ln1_arg.sem, 1)
                nc.gpsimd.tensor_scalar(var2[:, 1, :], mv[:, :, 1], 1.0 + EPS, EPS * EPS, ALU.mult, ALU.add)\
                    .then_inc(ln1_arg.sem, 1)
                need(pool, ln1_arg, b, 2)
                nc.gpsimd.tensor_tensor(rs2[:, :, :].rearrange("p a t -> p (a t)"),
                                        var2[:, :, :].rearrange("p a t -> p (a t)"), power[:, 0:16], ALU.pow)\
                    .then_inc(ln1_rs.sem, 1)
                for t in range(NT + 1):
                    if t < NT:
                        if t == 0:
                            need(pool, ln1_sc, b, 2)
                        if t % 4 == 0:
                            need(pool, stored[t // 4], b, 0)
                        need(pool, rope_ab, b, 3 * t + 3)
                        nc.gpsimd.tensor_tensor(ra[:, :], ra[:, :], rb[:, :], ALU.add).then_inc(rope_sum.sem, 1)
                        nc.gpsimd.tensor_scalar(X[:, t, :], Xin[:, t, :], one_r[:, t:t + 1], neg_mr[:, t:t + 1],
                                                ALU.mult, ALU.add).then_inc(resid.sem, 1)
                        need(pool, rope_sum, b, t + 1)
                        need(pool, att, b, t)
                        nc.gpsimd.tensor_tensor(qkr[:, t % 2, :].rearrange("p (h d) -> p h d", h=8),
                                                ra[:, :].rearrange("p (h d) -> p h d", h=8),
                                                decay[:, :].unsqueeze(2).to_broadcast([P, 8, DK]), ALU.mult)\
                            .then_inc(rope_qk.sem, 1)
                    if t >= 1:
                        u = t - 1
                        need(pool, o_sq, b, 4 * u + 4)
                        stand_alone(pool)
                        nc.gpsimd.tensor_scalar(oarg[:, :], oss[:, u % 2, :], 1.0 / DV, EPS, ALU.mult, ALU.add)\
                            .then_inc(o_arg.sem, 1)
                        need(pool, o_arg, b, u + 1)
                        need(pool, y_h, b, 4 * (u - 1))
                        nc.gpsimd.tensor_tensor(ors[:, u % 2, :], oarg[:, :], power[:, 0:4], ALU.pow)\
                            .then_inc(o_rs.sem, 1)
                    if t == 6:
                        rsqrts(b, 0)
                rsqrts(b, 1)
                squares(b, 0)
                adds(b, 0)
                squares(b, 1)
                rsqrts(b, 2)
                adds(b, 1)
                rsqrts(b, 3)
                for n in range(8):
                    h, g, s = qk_order(n)
                    need(pool, c_mid, b, n + 1)
                    tok = slice(512 * g, 512 * g + 512)
                    nc.gpsimd.tensor_tensor(cmp[:, h, s, 2, tok], r1[:, n % 2, :], cmp[:, h, s, 1, tok],
                                            ALU.subtract).then_inc(c_lo.sem, 1)
                need(pool, fn_norm, b, 16)
                for pr in range(4):
                    xs = X[:, 2 * pr:2 * pr + 2, :]
                    nc.gpsimd.tensor_tensor(xs, xs, cbias[:, :].unsqueeze(1).to_broadcast([P, 2, D]), ALU.add)\
                        .then_inc(x_cb.sem, 1)
                pool.wait_ge(s_band, 16)
                for s in range(NS):
                    if not bands[s]:
                        continue
                    hg = s // 16
                    a, z, at = bands[s]
                    for c in range(4):
                        n = 4 * s + c
                        need(pool, e_p, b, n + 1)
                        nc.gpsimd.tensor_tensor(ring[:, n % RING, a:z], ring[:, n % RING, a:z],
                                                band_exp[:, 4 * hg + c, at:at + z - a], ALU.mult)\
                            .then_inc(e_band.sem, 1)
                rsqrts(b, 4)
                rsqrts(b, 5)
                squares(b, 2)
                adds(b, 2)
                squares(b, 3)
                adds(b, 3)


def shape_constants(T, D):
    import numpy as np

    f32 = np.float32
    dk = D // RET_HEADS
    one = f32(1)
    freq = one / (10000.0 ** (np.arange(0, dk, 2, dtype=f32) / f32(dk)).astype(np.float64)).astype(f32)
    angle = (np.arange(T, dtype=f32)[:, None] * freq[None, :]).astype(np.float64)
    c, s = np.cos(angle), np.sin(angle)
    g = 1.0 - np.exp2(-5.0 - np.arange(RET_HEADS))
    i = np.arange(P)
    decay = np.concatenate([g[None] ** (i[:, None] + 1.0) * dk ** -0.5, g[None] ** (P - 1.0 - i[:, None])], 1)
    mask = (i[:, None, None] <= i[None, None, :]) * (g ** -float(P))[None, :, None]
    head = np.arange(P) // 64
    gamma = np.stack([g[2 * pr + head] ** P for pr in range(2)], 1)
    n = np.maximum(np.arange(384) - (P - 1), 0)
    big = 16 + (np.log(np.maximum(n, 1).astype(f32) / f32(16)) / f32(np.log(8)) * f32(16)).astype(np.int32)
    bucket = np.where(n < 16, n, np.minimum(big, BUCKETS - 1))
    rows = np.zeros((32, 64))
    rows[0, 0:8] = 1
    for part in range(PARTS):
        for j in range(8):
            r, blk = 1 + 8 * part + j, np.arange(8)
            rows[r, 0:8] = blk == j
            rows[r, 8:16] = blk < j
            rows[r, 16:24] = blk > j + 1
            rows[r, 24], rows[r, 25] = -(part >= 1), -(part >= 2)
    return {
        "c_ident": np.eye(P), "c_cos": np.concatenate([c, c], 1), "c_sin": np.concatenate([-s, s], 1),
        "c_decay": decay, "c_mask": mask.reshape(P, -1), "c_gamma": gamma,
        "c_onehot": bucket[None, :] == np.arange(BUCKETS)[:, None], "c_rows": rows,
    }


_INS = ["L0_attn_a_x", "L0_attn_a_ln_w", "L0_attn_a_ln_b", "L0_attn_a_Wq", "L0_attn_a_Wk", "L0_attn_a_Wv",
        "L0_attn_a_Wg", "L0_attn_a_g_norm_w", "L0_attn_a_Wo", "L0_attn_b_wq", "L0_attn_b_bq", "L0_attn_b_wk",
        "L0_attn_b_bk", "L0_attn_b_wv", "L0_attn_b_bv", "L0_attn_b_wo", "L0_attn_b_bo", "L0_attn_b_rel_bias",
        "L0_ffn_W_r", "L0_ffn_W_k", "L0_ffn_W_v", "L0_ffn_mu_r", "L0_ffn_mu_k"]


def kernel(**inputs):
    import numpy as np
    import concourse.bacc as bacc
    from concourse.bass_utils import run_bass_kernel_spmd

    nc = bacc.Bacc("TRN2", target_bir_lowering=False, num_devices=1)
    arrays = {n: np.ascontiguousarray(inputs[n]) for n in _INS}
    shape = arrays[_INS[0]].shape
    arrays |= {n: np.ascontiguousarray(a, np.float32) for n, a in shape_constants(shape[1], shape[2]).items()}
    aps = [nc.dram_tensor(n, a.shape, mybir.dt.from_np(a.dtype), kind="ExternalInput").ap()
           for n, a in arrays.items()]
    out = nc.dram_tensor("out", shape, F32, kind="ExternalOutput").ap()
    build(nc, aps, out)
    return run_bass_kernel_spmd(nc, [arrays], core_ids=[0]).results[0]["out"]
```

```python
from contextlib import ExitStack

import concourse.bass as bass
from concourse import mybir

F32 = mybir.dt.float32
BF16 = mybir.dt.bfloat16
ALU = mybir.AluOpType
ACT = mybir.ActivationFunctionType
AX_X = mybir.AxisListType.X

P = 128
EPS = 1e-5
RET_HEADS = 4
HEADS = 16
BUCKETS = 32
PARTS = 3
Q_PARTS = (2, 1, 0, 1, 0, 0)
K_PARTS = (0, 1, 2, 0, 1, 0)
RUNS = ((0, 3), (3, 2), (5, 1))
MAX_ROW = 96
RING = 12
LAG = 2
AHEAD = 24
SLOTS = 2
KEY_ORDER = ((0, 4, 1, 5, 2, 6, 3, 7), (3, 0, 4, 1, 5, 2, 6, 7))


class Tally:

    def __init__(self, sem, each, step=1):
        self.sem, self.each, self.step = sem, each, step

    def at(self, b, n):
        return (b + 1) * (self.each * self.step) + n * self.step


def band(half, j):
    lo, hi = P * j - 512 * half, P * j + 2 * P - 512 * half
    a, z = max(lo, 0), min(hi, 512)
    return (a, z, a - lo) if a < z else None


def build(nc, ins, out):
    x, ln_w, ln_b, Wq, Wk, Wv, Wg, g_norm_w, Wo = ins[:9]
    wq, bq, wk, bk, wv, bv, wo, bo, rel_bias, W_r, W_k, W_v, mu_r, mu_k = ins[9:23]
    c_ident, c_cos, c_sin, c_decay, c_mask, c_gamma, c_onehot, c_rows = ins[23:]

    B, T, D = x.shape
    NT = T // P
    NG = NT // 4
    C = D // P
    DK, DV = D // RET_HEADS, 2 * D // RET_HEADS
    HD = D // HEADS
    NU = HEADS * NT
    NS = HEADS // 4 * 2 * NT

    with ExitStack() as ctx:
        def sb(name, shape, dt=F32):
            return ctx.enter_context(nc.sbuf_tensor(name, shape, dt))

        def sem(name):
            return ctx.enter_context(nc.semaphore(name))

        tallies = {"pe": [], "act": [], "dve": [], "pool": [], "sp": []}

        def tally(owner, name, each, step=1):
            t = Tally(sem(name), each, step)
            tallies[owner].append(t)
            return t

        psum = ctx.enter_context(nc.psum_tensor("psum", [P, 8, 512], F32))
        bank = [psum[:, i, :] for i in range(8)]
        bank_pair = [psum[:, 2 * i:2 * i + 2, :].rearrange("p a n -> p (a n)") for i in range(2)]

        ident = sb("ident", [P, P])
        cos = sb("cos", [P, NT, DK])
        sin = sb("sin", [P, NT, DK])
        decay = sb("decay", [P, 8])
        mask = sb("mask", [P, 512])
        gamma = sb("gamma", [P, 2])
        Wqkvg = sb("Wqkvg", [P, C, 6 * D])
        WoS = sb("WoS", [P, 4, D])
        WT = sb("WT", [P, 7, C, D])
        W_R, W_K, W_V, A_Q, A_K, A_V, A_O = range(7)
        vec = sb("vec", [P, 24])
        LN_W, LN_B, BQ, BK, BV, MU_R, MU_K, GW, NU_R, NU_K = [slice(2 * i, 2 * i + 2) for i in range(10)]
        cbias = sb("cbias", [P, D])
        power = sb("power", [P, 16])
        X = sb("X", [P, NT, D])
        Xin = sb("Xin", [P, NT, D])
        SQ = sb("SQ", [P, HEADS, T], BF16)
        SK = sb("SK", [P, HEADS, T], BF16)
        Vx = sb("Vx", [P, NT, HEADS, HD + 1])
        band_exp = sb("band_exp", [P, HEADS, 2 * P])
        nT = sb("nT", [P, C, 1 + T])
        nrm = sb("nrm", [P, 4, D])
        xrT = sb("xrT", [P, C, 512])
        xkT = sb("xkT", [P, C, 512])
        mixed = sb("mixed", [P, 2048])
        kact = mixed[:, 0:1024].rearrange("p (a n) -> p a n", a=2)
        th = mixed[:, 1024:2048].rearrange("p (a n) -> p a n", a=2)
        aO = mixed[:, :].rearrange("p (t n) -> p t n", t=NT)
        qbd = sb("qbd", [P, 2, 2, 2, P])
        S = sb("S", [P, 2, DV])
        stat = sb("stat", [P, NT, 6])
        mv = sb("mv", [P, NT, 2])
        var2 = sb("var2", [P, 2, NT])
        rs2 = sb("rs2", [P, 2, NT])
        one_r = sb("one_r", [P, NT])
        neg_mr = sb("neg_mr", [P, NT])
        fstat = sb("fstat", [P, 4, 6])
        fmv = sb("fmv", [P, 4, 2])
        farg = sb("farg", [P, 4])
        frs = sb("frs", [P, 4])
        oss = sb("oss", [P, 2, 4])
        oarg = sb("oarg", [P, 4])
        ors = sb("ors", [P, 2, 4])
        mx = sb("mx", [P, 8, 16])
        mrow = sb("mrow", [16, 2, P], BF16)
        orc = sb("orc", [P, 4, 4])
        Z = sb("Z", [P, 7680])

        def cut(at, n):
            return Z[:, at:at + n]

        zn = cut(0, 512).rearrange("p (a n) -> p a n", a=2)
        zT = cut(512, 512).rearrange("p (a c n) -> p a c n", a=2, c=C)
        ra = cut(1024, 512)
        rb = cut(1536, 512)
        qkr = cut(2048, 1024).rearrange("p (a n) -> p a n", a=2)
        kT = cut(3072, 512).rearrange("p (a c n) -> p a c n", a=2, c=2)
        AT = cut(3584, 512)
        v_sb = cut(4096, 1024).rearrange("p (a n) -> p a n", a=2)
        gt = cut(5120, 1024).rearrange("p (a n) -> p a n", a=2)
        y = cut(6144, 512)
        yT = cut(6656, 512)
        sq_junk = cut(7168, 512)
        ring = cut(0, RING * 512).rearrange("p (s n) -> p s n", s=RING)
        cmp = cut(0, 6144).bitcast(BF16).rearrange("p (h s k n) -> p h s k n", h=2, s=2, k=PARTS)
        r1 = cut(6144, 1024).rearrange("p (a n) -> p a n", a=2)
        aT = r1
        oT = cut(7168, 512)
        raw = cut(0, 3584).rearrange("p (w c n) -> p w c n", w=7, c=C)

        scratch = nc.dram_tensor("bias_scratch", (HEADS, 384), F32, kind="Internal").ap()
        rows_scratch = nc.dram_tensor("bias_rows", (P, HEADS * 384), F32, kind="Internal").ap()

        parts_scratch = nc.dram_tensor("parts", (2, HEADS, PARTS, HD, T), BF16, kind="Internal").ap()

        s_const = sem("s_const")
        s_w = sem("s_w")
        s_wt = sem("s_wt")
        s_wts = sem("s_wts")
        s_prep = sem("s_prep")
        s_prepv = sem("s_prepv")
        s_bvb = sem("s_bvb")
        s_cb = sem("s_cb")
        s_bb = sem("s_bb")
        s_oh = sem("s_oh")
        s_eb = sem("s_eb")
        s_scr = sem("s_scr")
        s_rep = sem("s_rep")
        s_band = sem("s_band")
        s_rows = sem("s_rows")
        s_rowsk = sem("s_rowsk")
        x_in = Tally(sem("x_in"), 1, 16)
        stored = [tally("sp", f"stored{g}", 1, 16) for g in range(NG)]
        ln1_stat = tally("dve", "ln1_stat", NT)
        ln1_mv = tally("dve", "ln1_mv", NT)
        ln1_arg = tally("pool", "ln1_arg", 2)
        ln1_rs = tally("pool", "ln1_rs", 1)
        ln1_sc = tally("dve", "ln1_sc", 2)
        z_norm = tally("dve", "z_norm", NT)
        resid = tally("pool", "resid", NT)
        z_tp = tally("pe", "z_tp", NT)
        z_T = tally("act", "z_T", 2 * NT)
        p_qk = tally("pe", "p_qk", NT)
        p_v = tally("pe", "p_v", NT)
        p_g = tally("pe", "p_g", NT)
        rope_ab = tally("dve", "rope_ab", 3 * NT)
        rope_sum = tally("pool", "rope_sum", NT)
        rope_qk = tally("pool", "rope_qk", NT)
        qk_tp = tally("pe", "qk_tp", NT)
        kq_T = tally("act", "kq_T", 3 * NT)
        att = tally("pe", "att", NT)
        att_m = tally("dve", "att_m", NT)
        v_cp = tally("act", "v_cp", NT)
        p_o = tally("pe", "p_o", NT)
        p_st = tally("pe", "p_st", NT)
        s_upd = tally("dve", "s_upd", 2 * NT)
        o_sq = tally("act", "o_sq", 4 * NT)
        o_arg = tally("pool", "o_arg", NT)
        o_rs = tally("pool", "o_rs", NT)
        g_tanh = tally("act", "g_tanh", NT)
        gate = tally("dve", "gate", NT)
        y_h = tally("dve", "y_h", 4 * NT)
        y_tp = tally("pe", "y_tp", NT)
        y_T = tally("act", "y_T", NT)
        p_w = tally("pe", "p_w", NT)
        x1 = tally("dve", "x1", NT)
        fn_stat = tally("dve", "fn_stat", 24)
        fn_mv = tally("dve", "fn_mv", 24)
        fn_arg = tally("pool", "fn_arg", 6)
        fn_rs = tally("pool", "fn_rs", 6)
        fn_norm = tally("dve", "fn_norm", 24)
        fn_tp = tally("pe", "fn_tp", 12)
        fn_T = tally("act", "fn_T", 12)
        mix_a = tally("dve", "mix_a", 16)
        mix_b = tally("dve", "mix_b", 16)
        p_k = tally("pe", "p_k", 8)
        k_relu = tally("act", "k_relu", 8)
        k_sq = tally("pool", "k_sq", 8)
        p_r = tally("pe", "p_r", 8)
        r_tanh = tally("act", "r_tanh", 8)
        p_kv = tally("pe", "p_kv", 8)
        kv_r = tally("dve", "kv_r", 8)
        x_ffn = tally("pool", "x_ffn", 6)
        x_end = tally("dve", "x_end", 2)
        x_cb = tally("pool", "x_cb", 4)
        p_qkT = tally("pe", "p_qkT", 8)
        c_hi = tally("act", "c_hi", 8)
        c_r1 = tally("dve", "c_r1", 8)
        c_mid = tally("dve", "c_mid", 8)
        c_lo = tally("pool", "c_lo", 8)
        parts_out = [tally("sp", f"parts_out_{side}", 6, 16) for side in "qk"]
        spread = [tally("sp", f"spread{share}", 6, 16) for share in range(3)]
        p_vx = tally("pe", "p_vx", 4)
        vx_cp = tally("act", "vx_cp", 4)
        mx_s = tally("pe", "mx_s", NU)
        mx_r = tally("dve", "mx_r", NU)
        mx_tp = tally("pe", "mx_tp", 8)
        mx_row = tally("act", "mx_row", 8)
        mx_in = [tally("sp", f"mx_in{i}", 16, 16) for i in range(2)]
        e_s = tally("pe", "e_s", 4 * NS)
        e_p = tally("act", "e_p", 4 * NS)
        e_band = tally("pool", "e_band", 36 * 4)
        e_pv = tally("pe", "e_pv", NS)
        o_cp = tally("act", "o_cp", 8)
        o_tp = tally("pe", "o_tp", 8)
        o_rc = tally("dve", "o_rc", 8)
        o_n = tally("dve", "o_n", 8)
        w_tp = tally("pe", "w_tp", 4)
        w_T = tally("act", "w_T", 4)
        p_wo = tally("pe", "p_wo", 4)
        x_att = tally("dve", "x_att", 4)

        def prime(eng, owner):
            for t in tallies[owner]:
                eng.sem_inc(t.sem, t.each * t.step)

        def need(eng, t, b, n):
            eng.wait_ge(t.sem, t.at(b, n))

        def stand_alone(eng):
            eng.nop(nofuse=True)

        bands = [band((s // 8) % 2, KEY_ORDER[(s // 8) % 2][s % 8]) for s in range(NS)]
        banded = [sum(z is not None for z in bands[:s + 1]) for s in range(NS)]
        units = [min(NU, AHEAD + 2 * (s + 1)) for s in range(NS)]

        def unit(u):
            blk, ii, hh = u // 16, u % 16 // 4, u % 4
            return blk // 2 * 4 + hh, blk % 2 * 4 + ii, blk, hh * 4 + ii

        def qk_order(n):
            return n // 4, n // 2 % 2, n % 2

        def step(s):
            hg, half = s // 16, s // 8 % 2
            return hg, half, KEY_ORDER[half][s % 8]

        WIDE = range(units.index(NU) + 1, NS - 4)
        W_BANKS = (0, 2, 0, 6)

        def col_bank(s, c):
            return bank[(4, 5, 2, 3)[c] if s in WIDE else 4 + c % 2]

        def block_before(s):
            return (s + 3) // 8 if (s + 3) % 8 == 0 and 0 < (s + 3) // 8 < 8 else None

        def output_before(s):
            return (s - 11) // 8 if s >= 11 and (s - 11) % 8 == 0 else None

        SHARES = (slice(0, 4), slice(4, 8), slice(8, 16))
        N_CONST, N_W = 20, 12

        block = ctx.enter_context(nc.Block())

        @block.sync
        def _(sp):
            prime(sp, "sp")
            xv = x.rearrange("b (t p) d -> b p t d", p=P)
            ov = out.rearrange("b (t p) d -> b p t d", p=P)
            sp.dma_start(Xin[:, :, :], xv[0]).then_inc(x_in.sem, 16)
            n = 0

            def const(dst, src):
                nonlocal n
                n += 1
                sp.dma_start(dst, src, allow_slow_non_contiguous=True).then_inc(s_const, 16)

            const(ident[:, :], c_ident)
            const(vec[:, LN_W], ln_w.rearrange("(c p) -> p c", p=P))
            const(vec[:, LN_B], ln_b.rearrange("(c p) -> p c", p=P))
            const(vec[:, BQ], bq.rearrange("(c p) -> p c", p=P))
            const(vec[:, BK], bk.rearrange("(c p) -> p c", p=P))
            const(vec[:, BV], bv.rearrange("(c p) -> p c", p=P))
            const(vec[:, MU_R], mu_r.rearrange("(c p) -> p c", p=P))
            const(vec[:, MU_K], mu_k.rearrange("(c p) -> p c", p=P))
            const(vec[:, GW.start:GW.start + 1], g_norm_w.rearrange("(p c) -> p c", c=1))
            const(cos[:, :, :], c_cos.rearrange("(t p) n -> p t n", p=P))
            const(sin[:, :, :], c_sin.rearrange("(t p) n -> p t n", p=P))
            const(decay[:, :], c_decay)
            const(mask[:, :], c_mask)
            const(gamma[:, :], c_gamma)
            const(xkT[0:BUCKETS, 0, 0:384], c_onehot)
            const(xkT[0:BUCKETS, 1, 0:HEADS], rel_bias)
            const(xkT[0:HEADS, 1, 32:64], rel_bias.rearrange("k h -> h k"))
            const(xrT[96:128, 0, :], bass.AP(rel_bias.tensor, 0, [[0, 32], [1, BUCKETS * HEADS]]))
            const(xrT[96:128, 1, 0:64], c_rows)
            const(cbias[:, :], bass.AP(bo.tensor, 0, [[0, P], [1, D]]))
            assert n == N_CONST
            n = 0

            def weight(dst, src):
                nonlocal n
                n += 1
                sp.dma_start(dst, src).then_inc(s_w, 16)

            for w, c0, c1 in ((Wq, 0, D), (Wk, D, 2 * D), (Wv, 2 * D, 4 * D), (Wg, 4 * D, 6 * D)):
                weight(Wqkvg[:, :, c0:c1], w.rearrange("(c p) n -> p c n", p=P))
            weight(WoS[:, :, :], Wo.rearrange("(c p) n -> p c n", p=P))
            for i, w in enumerate((W_r, W_k, W_v, wq, wk, wv, wo)):
                weight(raw[:, i], w.rearrange("(c p) n -> p c n", p=P))
            assert n == N_W
            sp.wait_ge(s_eb, 1)
            sp.dma_start(scratch, kact[0:HEADS, 0, 0:384]).then_inc(s_scr, 16)
            sp.wait_ge(s_scr, 16)
            sp.dma_start(rows_scratch, bass.AP(scratch.tensor, 0, [[0, P], [1, HEADS * 384]])).then_inc(s_rep, 16)
            sp.wait_ge(s_rep, 16)
            sp.dma_start(band_exp[:, :, :],
                         bass.AP(rows_scratch.tensor, P - 1, [[HEADS * 384 - 1, P], [384, HEADS], [1, 2 * P]]))\
                .then_inc(s_band, 16)

            def parts_store(b, h, s):
                need(sp, c_lo, b, 4 * h + 3 + s)
                for part in range(PARTS):
                    slot = (PARTS - 1 - part, part)[s]
                    sp.dma_start(parts_scratch[s, 8 * h:8 * h + 8, slot],
                                 cmp[:, h, s, part, :]).then_inc(parts_out[s].sem, 16)

            def spread_rows(b, share, s):
                heads = SHARES[share]
                need(sp, parts_out[s], b, 3 * (heads.start // 8) + 3)
                stack, parts = ((SQ, Q_PARTS), (SK, K_PARTS))[s]
                for first, length in RUNS:
                    slot = (PARTS - 1 - parts[first], parts[first])[s]
                    sp.dma_start(stack[HD * first:HD * (first + length), heads, :],
                                 parts_scratch[s, heads, slot:slot + length]
                                 .rearrange("h k d n -> (k d) h n")).then_inc(spread[share].sem, 16)

            with sp.Fori(0, B) as b:
                need(sp, z_norm, b, NT)
                need(sp, resid, b, NT)
                sp.dma_start(Xin[:, :, :], xv[(b + 1) % B]).then_inc(x_in.sem, 16)
                for h in range(2):
                    for s in range(2):
                        parts_store(b, h, s)
                    for share in ((0, 1), (2,))[h]:
                        for s in range(2):
                            spread_rows(b, share, s)
                for blk in range(8):
                    need(sp, mx_row, b, blk + 1)
                    h0, q0 = blk // 2 * 4, blk % 2 * 512
                    for hh in range(4):
                        sp.dma_start(SQ[MAX_ROW:MAX_ROW + 1, h0 + hh, q0:q0 + 512],
                                     mrow[4 * hh:4 * hh + 4, blk % 2, :]).then_inc(mx_in[blk % 2].sem, 16)
                for g in range(NG):
                    need(sp, *((x_ffn, b, 6), (x_end, b, 2))[g])
                    sp.dma_start(ov[b, :, 4 * g:4 * g + 4], X[:, 4 * g:4 * g + 4, :]).then_inc(stored[g].sem, 16)
            for g in range(NG):
                need(sp, stored[g], B - 1, 1)
            sp.wait_ge(x_in.sem, 16 * (B + 1))

        @block.tensor
        def _(pe):
            prime(pe, "pe")
            pe.wait_ge(s_const, 16 * N_CONST)
            pe.wait_ge(s_w, 16 * N_W)
            for w in range(7):
                for ci in range(C):
                    for co in range(C):
                        mm = pe.transpose(bank[w][:, ci * D + co * P:ci * D + co * P + P],
                                          raw[:, w, co, ci * P:ci * P + P], ident[:, :])
                mm.then_inc(s_wt, 1)
            pe.matmul(bank[7][0:HEADS, 0:384], xkT[0:BUCKETS, 1, 0:HEADS], xkT[0:BUCKETS, 0, 0:384],
                      start=True, stop=True).then_inc(s_oh, 1)
            pe.wait_ge(s_wts, 7)
            pe.wait_ge(s_bvb, 2)
            for c in range(C):
                mm = pe.matmul(bank[0][:, 0:D], nrm[:, 0, c * P:c * P + P], WT[:, A_O, c, :],
                               start=c == 0, stop=c == C - 1)
            mm.then_inc(s_bb, 1)
            pe.wait_ge(s_cb, 1)
            pe.wait_ge(s_eb, 1)
            pe.wait_ge(s_prep, 1)

            def z_transposes(b, t):
                need(pe, z_norm, b, t + 1)
                if t == 0:
                    need(pe, fn_T, b, 0)
                else:
                    need(pe, s_upd, b, 2 * (t - 1))
                    need(pe, z_T, b, 2 * t)
                    need(pe, kv_r, b, 0)
                for c in range(C):
                    mm = pe.transpose(bank[6 if t else 0][:, c * P:c * P + P], zn[:, t % 2, c * P:c * P + P], ident[:, :])
                mm.then_inc(z_tp.sem, 1)

            def project(b, t, dst, c0, done):
                for c in range(C):
                    mm = pe.matmul(bank[dst], zT[:, t % 2, c, :], Wqkvg[:, c, c0:c0 + 512],
                                   start=c == 0, stop=c == C - 1)
                mm.then_inc(done.sem, 1)

            def ln_transposes(b, n):
                need(pe, fn_norm, b, 4 * n + 4)
                need(pe, fn_T, b, 2 * n)
                for c in range(C):
                    for i in range(4):
                        mm = pe.transpose(bank[c][:, i * P:i * P + P], nrm[:, i, c * P:c * P + P], ident[:, :])
                    mm.then_inc(fn_tp.sem, 1)

            def mix_k(b, q, o):
                need(pe, mix_b, b, 4 * q + 2)
                need(pe, k_relu, b, 2 * q + o - 1)
                for c in range(C):
                    mm = pe.matmul(bank[2 + o], WT[:, W_K, c, o * P:o * P + P], xkT[:, c, :],
                                   start=c == 0, stop=c == C - 1)
                mm.then_inc(p_k.sem, 1)

            def mix_r(b, q, pr):
                need(pe, mix_b, b, 4 * q + 4)
                need(pe, r_tanh, b, 2 * q + pr - 1)
                if q == 0 and pr == 0:
                    need(pe, att_m, b, NT)
                if q == 0 and pr == 1:
                    need(pe, y_h, b, 4 * NT)
                for i in range(2):
                    t = 2 * pr + i
                    for c in range(C):
                        mm = pe.matmul(bank[4 + pr][:, i * D:i * D + D], xrT[:, c, t * P:t * P + P],
                                       WT[:, W_R, c, :], start=c == 0, stop=c == C - 1)
                mm.then_inc(p_r.sem, 1)

            def mix_kv(b, q, pr):
                need(pe, k_sq, b, 2 * q + 2)
                need(pe, kv_r, b, 2 * q + pr - 1)
                if q == 2:
                    need(pe, *((w_T, b, 4), (x_att, b, 4))[pr])
                if q == 0 and pr == 1:
                    need(pe, x1, b, NT)
                for i in range(2):
                    t = 2 * pr + i
                    for o in range(2):
                        mm = pe.matmul(bank[6 + pr][:, i * D:i * D + D], kact[:, o, t * P:t * P + P],
                                       WT[:, W_V, o, :], start=o == 0, stop=o == 1)
                mm.then_inc(p_kv.sem, 1)

            def channel_mix(b, f):
                n, q = (0, 4)[f], 2 * f
                mix_kv(b, q, 0)
                ln_transposes(b, n + 1)
                mix_kv(b, q, 1)
                for o in range(2):
                    mix_k(b, q + 1, o)
                for pr in range(2):
                    mix_r(b, q + 1, pr)
                if f == 1:
                    z_transposes(b + 1, 0)
                for pr in range(2):
                    mix_kv(b, q + 1, pr)

            def qk_project(b, n):
                h, g, side = qk_order(n)
                need(pe, c_r1, b, n - 1)
                for c in range(C):
                    mm = pe.matmul(bank[2 + n % 2], WT[:, A_Q + side, c, h * P:h * P + P],
                                   nT[:, c, 1 + 512 * g:513 + 512 * g], start=c == 0, stop=c == C - 1)
                mm.then_inc(p_qkT.sem, 1)

            def v_project(b, pr):
                need(pe, vx_cp, b, pr - 1)
                for i in range(2):
                    t = 2 * pr + i
                    for c in range(C):
                        mm = pe.matmul(bank[4 + pr % 2][:, i * D:i * D + D], nT[:, c, 1 + t * P:1 + t * P + P],
                                       WT[:, A_V, c, :], start=c == 0, stop=c == C - 1)
                mm.then_inc(p_vx.sem, 1)

            def score_rows(b, u):
                h, i, _, _ = unit(u)
                for share, heads in enumerate(SHARES):
                    if u == NT * heads.start:
                        need(pe, spread[share], b, 6)
                if u < 2:
                    need(pe, fn_T, b, 8)
                    need(pe, c_r1, b, 8)
                else:
                    need(pe, mx_r, b, u - 1)
                for k in range(2):
                    mm = pe.matmul(bank[2 * (u % 2) + k], SQ[0:MAX_ROW, h, i * P:i * P + P],
                                   SK[0:MAX_ROW, h, 512 * k:512 * k + 512], start=True, stop=True)
                mm.then_inc(mx_s.sem, 1)

            def max_transpose(b, blk):
                need(pe, mx_r, b, 16 * blk + 16)
                if blk == 0:
                    need(pe, kv_r, b, 4)
                else:
                    need(pe, mx_row, b, blk)
                    need(pe, o_n, b, blk - 1)
                pe.transpose(bank[7][0:16, 0:P], mx[:, blk, :], ident[:, :]).then_inc(mx_tp.sem, 1)

            def score_cols(b, s, c):
                hg, half, j = step(s)
                n = 4 * s + c
                if c == 0 and s % 8 == 0:
                    need(pe, mx_in[(s // 8) % 2], b, 4 * (s // 16 + 1))
                if n < 2:
                    need(pe, vx_cp, b, 4)
                elif s == WIDE.start and c >= 2:
                    need(pe, mx_r, b, NU)
                elif s in WIDE and s > WIDE.start:
                    need(pe, e_p, b, n - 3)
                else:
                    need(pe, e_p, b, n - 1)
                h = 4 * hg + c
                pe.matmul(col_bank(s, c), SK[:, h, j * P:j * P + P], SQ[:, h, 512 * half:512 * half + 512],
                          start=True, stop=True).then_inc(e_s.sem, 1)

            def weigh(b, s):
                hg, half, j = step(s)
                if bands[s]:
                    need(pe, e_band, b, 4 * banded[s])
                else:
                    need(pe, e_p, b, 4 * s + 4)
                if s == 0:
                    need(pe, kv_r, b, 4)
                elif s % 8 == 0:
                    need(pe, o_cp, b, s // 8)
                for c in range(4):
                    mm = pe.matmul(bank[6][32 * c:32 * c + HD + 1, :], Vx[:, j, 4 * hg + c, :],
                                   ring[:, (4 * s + c) % RING, :], start=s % 8 == 0, stop=s % 8 == 7)
                mm.then_inc(e_pv.sem, 1)

            def output_transposes(b, k):
                need(pe, o_cp, b, k + 1)
                need(pe, mx_row, b, min(k + 2, 8))
                need(pe, o_n, b, k)
                for i in range(4):
                    mm = pe.transpose(bank[7][:, i * P:i * P + P], oT[:, i * P:i * P + P], ident[:, :])
                mm.then_inc(o_tp.sem, 1)

            def w_transposes(b, pr):
                need(pe, o_n, b, 7 + pr // 2)
                if pr == 0:
                    need(pe, mx_r, b, NU)
                elif pr == 1:
                    need(pe, e_p, b, 4 * WIDE.stop)
                elif pr == 2:
                    need(pe, fn_T, b, 10)
                else:
                    need(pe, o_cp, b, 8)
                for i in range(2):
                    for c in range(C):
                        mm = pe.transpose(bank[W_BANKS[pr]][:, (2 * i + c) * P:(2 * i + c) * P + P],
                                          aO[:, 2 * pr + i, c * P:c * P + P], ident[:, :])
                mm.then_inc(w_tp.sem, 1)

            def w_project(b, pr):
                need(pe, w_T, b, pr + 1)
                for i in range(2):
                    for c in range(C):
                        mm = pe.matmul(bank[W_BANKS[pr] + 1][:, i * D:i * D + D],
                                       aT[:, pr % 2, (2 * i + c) * P:(2 * i + c) * P + P],
                                       WT[:, A_O, c, :], start=c == 0, stop=c == C - 1)
                mm.then_inc(p_wo.sem, 1)

            def y_transposes(b, u):
                need(pe, y_h, b, 4 * u + 4)
                need(pe, x1, b, u)
                if u == 0:
                    need(pe, kv_r, b, 0)
                for i in range(4):
                    mm = pe.transpose(bank[7][:, i * P:i * P + P], y[:, i * P:i * P + P], ident[:, :])
                mm.then_inc(y_tp.sem, 1)

            def y_project(b, u):
                need(pe, y_T, b, u + 1)
                for h in range(RET_HEADS):
                    mm = pe.matmul(bank[7][:, 0:D], yT[:, h * P:h * P + P], WoS[:, h, :],
                                   start=h == 0, stop=h == 3)
                mm.then_inc(p_w.sem, 1)

            z_transposes(0, 0)
            with pe.Fori(0, B) as b:
                for t in range(NT + 1):
                    if t == NT:
                        need(pe, rope_ab, b, 3 * NT)
                        need(pe, v_cp, b, NT)
                        ln_transposes(b, 0)
                    if t < NT:
                        need(pe, z_T, b, 2 * t + 2)
                        need(pe, rope_ab, b, 3 * t)
                        project(b, t, 0, 0, p_qk)
                    if 3 <= t <= NT:
                        y_project(b, t - 3)
                    if 1 <= t <= NT:
                        u = t - 1
                        need(pe, kq_T, b, 3 * u + 3)
                        need(pe, att_m, b, u)
                        if u == 0:
                            need(pe, r_tanh, b, 0)
                        for pr in range(2):
                            mm = pe.matmul(bank[4][:, 256 * pr:256 * pr + 256], kT[:, u % 2, pr, :],
                                           qbd[:, u % 2, pr, :, :].rearrange("p a n -> p (a n)"),
                                           start=True, stop=True)
                        mm.then_inc(att.sem, 1)
                    if t < NT:
                        need(pe, v_cp, b, t)
                        project(b, t, 1, 512, p_v)
                    if 1 <= t <= NT:
                        need(pe, att_m, b, u + 1)
                        need(pe, v_cp, b, u + 1)
                        need(pe, s_upd, b, 2 * u)
                        need(pe, y_h, b, 4 * u)
                        for h in range(RET_HEADS):
                            o = bank[5][:, h * DV:h * DV + DV]
                            mm = pe.matmul(o, AT[:, h * P:h * P + P], v_sb[:, u % 2, h * DV:h * DV + DV],
                                           start=True, stop=u == 0)
                            if u > 0:
                                mm = pe.matmul(o, qbd[:, u % 2, h // 2, h % 2, :], S[:, h // 2, :],
                                               start=False, stop=True)
                        mm.then_inc(p_o.sem, 1)
                        need(pe, z_T, b, min(2 * u + 4, 2 * NT))
                        for h in range(RET_HEADS):
                            mm = pe.matmul(bank[6][64 * (h % 2):64 * (h % 2) + 64, (h // 2) * DV:(h // 2) * DV + DV],
                                           qkr[:, u % 2, 256 + h * DK:256 + h * DK + DK],
                                           v_sb[:, u % 2, h * DV:h * DV + DV], start=True, stop=True,
                                           skip_group_check=True)
                        mm.then_inc(p_st.sem, 1)
                    if t < NT:
                        need(pe, gate, b, t)
                        if t == 0:
                            need(pe, k_relu, b, 0)
                        project(b, t, 2, 1024, p_g)
                        if t + 1 < NT:
                            z_transposes(b, t + 1)
                        need(pe, rope_qk, b, t + 1)
                        need(pe, kq_T, b, 3 * t)
                        for i in range(4):
                            mm = pe.transpose(bank[3][:, i * P:i * P + P], qkr[:, t % 2, i * P:i * P + P], ident[:, :])
                        mm.then_inc(qk_tp.sem, 1)
                    if 2 <= t <= NT:
                        y_transposes(b, t - 2)
                need(pe, gate, b, NT)
                need(pe, kq_T, b, 3 * NT)
                mix_k(b, 0, 0)
                y_project(b, NT - 2)
                y_transposes(b, NT - 1)
                mix_k(b, 0, 1)
                y_project(b, NT - 1)
                mix_r(b, 0, 0)
                mix_r(b, 0, 1)
                need(pe, s_upd, b, 2 * NT)
                channel_mix(b, 0)
                ln_transposes(b, 2)
                need(pe, k_relu, b, 4)
                need(pe, fn_T, b, 6)
                need(pe, r_tanh, b, 4)
                for n in range(8):
                    if n == 2:
                        v_project(b, 0)
                        ln_transposes(b, 3)
                        v_project(b, 1)
                        need(pe, fn_T, b, 8)
                    qk_project(b, n)
                v_project(b, 2)
                v_project(b, 3)
                for u in range(AHEAD):
                    score_rows(b, u)
                    if u == 17:
                        max_transpose(b, 0)
                u = AHEAD
                for s in range(NS + LAG):
                    if output_before(s) is not None:
                        output_transposes(b, output_before(s))
                    if s < NS:
                        for c in range(4):
                            score_cols(b, s, c)
                            while c == 1 and u < units[s]:
                                score_rows(b, u)
                                u += 1
                        if block_before(s) is not None:
                            max_transpose(b, block_before(s))
                    if s == NS + 1:
                        need(pe, x_att, b, 1)
                        ln_transposes(b, 4)
                    if s >= LAG:
                        weigh(b, s - LAG)
                    if s == NS - 4:
                        w_transposes(b, 0)
                    if s == NS - 3:
                        w_project(b, 0)
                        w_transposes(b, 1)
                    if s == NS - 2:
                        w_project(b, 1)
                output_transposes(b, 7)
                need(pe, x_att, b, 2)
                mix_k(b, 2, 0)
                mix_k(b, 2, 1)
                for pr in (2, 3):
                    w_transposes(b, pr)
                for pr in (2, 3):
                    w_project(b, pr)
                mix_r(b, 2, 0)
                mix_r(b, 2, 1)
                channel_mix(b, 1)

        @block.scalar
        def _(act):
            prime(act, "act")
            for w in range(7):
                act.wait_ge(s_wt, w + 1)
                scale = {A_Q: 0.25, W_V: 0.5}.get(w, 1.0)
                nc.scalar.activation(WT[:, w].rearrange("p c n -> p (c n)"), bank[w], ACT.Identity,
                                     scale=scale).then_inc(s_wts, 1)
            act.wait_ge(s_oh, 1)
            act.wait_ge(s_prepv, 1)
            nc.scalar.activation(kact[0:HEADS, 0, 0:384], bank[7][0:HEADS, 0:384], ACT.Exp,
                                 bias=frs[0:HEADS, 0:1]).then_inc(s_eb, 1)
            act.wait_ge(s_const, 16 * N_CONST)
            for h in range(HEADS):
                nc.scalar.activation(SK[96:128, h, :].rearrange("p (k n) -> p k n", n=P),
                                     xrT[96:128, 1, 0:8].unsqueeze(2).to_broadcast([32, 8, P]),
                                     ACT.Identity).then_inc(s_rowsk, 1)
            act.wait_ge(s_cb, 1)
            act.wait_ge(s_scr, 16)

            def ln_copies(b, n):
                g = n % 2
                if n < 2:
                    need(act, mix_b, b, 0)
                elif n < 4:
                    need(act, mix_b, b, 8)
                else:
                    need(act, p_vx, b, 4)
                for c in range(C):
                    need(act, fn_tp, b, 2 * n + c + 1)
                    nc.scalar.copy(nT[:, c, 1 + 512 * g:513 + 512 * g], bank[c]).then_inc(fn_T.sem, 1)

            def relus(b, q, chunks=(0, 1)):
                for o in chunks:
                    need(act, p_k, b, 2 * q + o + 1)
                    need(act, p_kv, b, 2 * q)
                    nc.scalar.activation(kact[:, o, :], bank[2 + o], ACT.Relu).then_inc(k_relu.sem, 1)

            def tanhs(b, q):
                for pr in range(2):
                    need(act, p_r, b, 2 * q + pr + 1)
                    if q == 0:
                        need(act, x_end, b, 0)
                    else:
                        need(act, x_ffn, b, 2 * q + pr - 1)
                    nc.scalar.activation(th[:, pr, :], bank[4 + pr], ACT.Tanh, scale=0.5)\
                        .then_inc(r_tanh.sem, 1)

            def channel_mix(b, f):
                n, q = (0, 4)[f], 2 * f
                tanhs(b, q)
                ln_copies(b, n + 1)
                relus(b, q + 1)
                tanhs(b, q + 1)

            def z_copies(b, t):
                need(act, z_tp, b, t + 1)
                for c in range(C):
                    need(act, p_g, b, t - 1)
                    nc.scalar.activation(zT[:, t % 2, c, :], bank[6 if t else 0][:, c * P:c * P + P], ACT.Identity,
                                         scale=vec[:, LN_W.start + c:LN_W.start + c + 1],
                                         bias=vec[:, LN_B.start + c:LN_B.start + c + 1]).then_inc(z_T.sem, 1)

            z_copies(0, 0)
            with act.Fori(0, B) as b:
                for t in range(NT + 2):
                    if t == NT:
                        ln_copies(b, 0)
                    if t < NT:
                        need(act, p_v, b, t + 1)
                        need(act, p_st, b, t - 1)
                        nc.scalar.copy(v_sb[:, t % 2, :], bank[1]).then_inc(v_cp.sem, 1)
                    if 1 <= t <= NT:
                        u = t - 1
                        need(act, p_o, b, u + 1)
                        need(act, o_arg, b, u - 1)
                        need(act, o_sq, b, 4 * u)
                        for h in range(RET_HEADS):
                            nc.scalar.activation(sq_junk[:, h * DV:h * DV + DV], bank[5][:, h * DV:h * DV + DV], ACT.Square,
                                                 accum_out=oss[:, u % 2, h:h + 1]).then_inc(o_sq.sem, 1)
                    if t < NT:
                        need(act, p_g, b, t + 1)
                        need(act, y_h, b, 4 * (t - 1))
                        nc.scalar.activation(gt[:, t % 2, :], bank[2], ACT.Tanh, scale=0.5)\
                            .then_inc(g_tanh.sem, 1)
                        if t + 1 < NT:
                            z_copies(b, t + 1)
                        need(act, qk_tp, b, t + 1)
                        need(act, p_o, b, t - 1)
                        quad = bank[3].rearrange("p (a n) -> p a n", a=4)
                        nc.scalar.copy(qbd[0:64, t % 2, :, 0, :], quad[0:64, 0:2, :]).then_inc(kq_T.sem, 1)
                        nc.scalar.copy(qbd[64:128, t % 2, :, 1, :], quad[64:128, 0:2, :]).then_inc(kq_T.sem, 1)
                        nc.scalar.copy(kT[:, t % 2, :, :], quad[:, 2:4, :]).then_inc(kq_T.sem, 1)
                    if t >= 2:
                        need(act, y_tp, b, t - 1)
                        need(act, p_w, b, t - 2)
                        nc.scalar.copy(yT[:, :], bank[7]).then_inc(y_T.sem, 1)
                    if t == NT:
                        relus(b, 0, (0,))
                relus(b, 0, (1,))
                channel_mix(b, 0)
                def v_copies(pr):
                    need(act, p_vx, b, pr + 1)
                    nc.scalar.copy(Vx[:, 2 * pr:2 * pr + 2, :, 0:HD],
                                   bank[4 + pr % 2].rearrange("p (t h d) -> p t h d", t=2, h=HEADS))\
                        .then_inc(vx_cp.sem, 1)

                ln_copies(b, 2)
                for n in range(8):
                    h, g, s = qk_order(n)
                    if n == 2:
                        v_copies(0)
                        ln_copies(b, 3)
                        v_copies(1)
                    need(act, p_qkT, b, n + 1)
                    at = (BQ, BK)[s].start + h
                    nc.scalar.activation(cmp[:, h, s, 0, 512 * g:512 * g + 512], bank[2 + n % 2],
                                         ACT.Identity, bias=vec[:, at:at + 1]).then_inc(c_hi.sem, 1)
                v_copies(2)
                v_copies(3)

                def max_rows(blk):
                    need(act, mx_tp, b, blk + 1)
                    need(act, mx_in[blk % 2], b, 4 * (blk // 2))
                    nc.scalar.mul(mrow[:, blk % 2, :], bank[7][0:16, 0:P], -1.0).then_inc(mx_row.sem, 1)

                def output_copy(k):
                    need(act, e_pv, b, 8 * k + 8)
                    need(act, o_tp, b, k)
                    nc.scalar.copy(oT[:, :], bank[6]).then_inc(o_cp.sem, 1)

                def w_copy(pr):
                    need(act, w_tp, b, pr + 1)
                    if pr >= 2:
                        need(act, p_wo, b, pr - 1)
                    nc.scalar.copy(aT[:, pr % 2, :], bank[W_BANKS[pr]]).then_inc(w_T.sem, 1)

                max_rows(0)
                for out_side in parts_out:
                    need(act, out_side, b, 6)
                for s in range(NS):
                    need(act, e_pv, b, max(s - 2, 0))
                    for c in range(4):
                        n = 4 * s + c
                        need(act, e_s, b, n + 1)
                        nc.scalar.activation(ring[:, n % RING, :], col_bank(s, c), ACT.Exp)\
                            .then_inc(e_p.sem, 1)
                        if c == 3 and block_before(s) is not None:
                            max_rows(block_before(s))
                        if c == 1 and s % 8 == 2 and s > 2:
                            output_copy(s // 8 - 1)
                    if s in (NS - 4, NS - 3):
                        w_copy(s - NS + 4)
                ln_copies(b, 4)
                output_copy(7)
                relus(b, 2)
                w_copy(2)
                w_copy(3)
                channel_mix(b, 1)
                z_copies(b + 1, 0)

        @block.vector
        def _(dve):
            prime(dve, "dve")
            chain = [1]

            def link(i):
                chain[0] += 1
                i.then_inc(s_prepv, 1)
                dve.wait_ge(s_prepv, chain[0])

            dve.wait_ge(s_const, 16 * N_CONST)
            nc.vector.tensor_reduce(frs[0:HEADS, 0:1], xkT[0:HEADS, 1, 32:64], AX_X, ALU.max, negate=True)\
                .then_inc(s_prepv, 1)
            link(nc.vector.memset(nT[:, :, 0:1], 0.0))
            link(nc.vector.memset(qbd[:, :, :, :, :], 0.0))
            link(nc.vector.memset(Vx[:, :, :, HD:HD + 1], 1.0))
            link(nc.vector.memset(power[:, :], -0.5))
            link(nc.vector.memset(S[:, :, :], 0.0))
            for a, z in ((MU_R, NU_R), (MU_K, NU_K)):
                link(nc.vector.tensor_scalar(vec[:, z], vec[:, a], -1.0, 1.0, ALU.mult, ALU.add))
            link(nc.vector.tensor_scalar(vec[:, BQ], vec[:, BQ], 0.25, None, ALU.mult))
            link(nc.vector.memset(nrm[:, 0, :], 1.0))
            for c in range(C):
                nc.vector.tensor_scalar(nrm[:, 0, c * P:c * P + P], nrm[:, 0, c * P:c * P + P],
                                        vec[:, BV.start + c:BV.start + c + 1], None, ALU.mult).then_inc(s_bvb, 1)
            dve.wait_ge(s_w, 16 * N_W)
            link(nc.vector.tensor_scalar(WoS[:, :, :], WoS[:, :, :], vec[:, GW.start:GW.start + 1], 0.5,
                                         ALU.mult, ALU.mult))
            R = slice(96, 128)
            table = xrT[R, 0, :].rearrange("p (k h) -> p h k", k=BUCKETS)
            top, d0, d1 = (xrT[R, 1, 64 + 16 * i:80 + 16 * i] for i in range(3))
            wide = [xrT[R, 1, 128 + 128 * i:256 + 128 * i] for i in range(3)]
            cut3 = [w.rearrange("p (h k) -> p h k", h=HEADS) for w in wide]
            hi = nrm[R, 2, 0:64].bitcast(BF16).rearrange("p (h k) -> p h k", h=HEADS)
            mid = nrm[R, 2, 64:128].bitcast(BF16).rearrange("p (h k) -> p h k", h=HEADS)
            low = nrm[R, 2, 128:192].bitcast(BF16).rearrange("p (h k) -> p h k", h=HEADS)
            where0 = xrT[R, 1, 8:16].unsqueeze(1).to_broadcast([32, HEADS, 8])
            where1 = xrT[R, 1, 16:24].unsqueeze(1).to_broadcast([32, HEADS, 8])
            link(nc.vector.tensor_reduce(top, table, AX_X, ALU.max))
            link(nc.vector.tensor_tensor(d0, table[:, :, 0], top, ALU.subtract))
            link(nc.vector.tensor_tensor(d1, table[:, :, BUCKETS - 1], top, ALU.subtract))
            link(nc.vector.tensor_tensor(cut3[0], d0.unsqueeze(2).to_broadcast([32, HEADS, 8]), where0, ALU.mult))
            link(nc.vector.tensor_tensor(cut3[1], d1.unsqueeze(2).to_broadcast([32, HEADS, 8]), where1, ALU.mult))
            link(nc.vector.tensor_tensor(wide[0], wide[0], wide[1], ALU.add))
            link(nc.vector.tensor_copy(hi, cut3[0]))
            link(nc.vector.scalar_tensor_tensor(cut3[1], hi, xrT[R, 1, 24:25], cut3[0], ALU.mult, ALU.add))
            link(nc.vector.tensor_copy(mid, cut3[1]))
            link(nc.vector.scalar_tensor_tensor(cut3[2], mid, xrT[R, 1, 25:26], cut3[1], ALU.mult, ALU.add))
            link(nc.vector.tensor_copy(low, cut3[2]))
            for h in range(HEADS):
                nc.vector.tensor_copy(SQ[R, h, :].rearrange("p (k n) -> p k n", n=P),
                                      low[:, h, :].unsqueeze(2).to_broadcast([32, 8, P])).then_inc(s_rows, 1)
            dve.wait_ge(s_rowsk, HEADS)
            dve.wait_ge(s_rows, HEADS)
            dve.wait_ge(s_bb, 1)
            nc.vector.tensor_tensor(cbias[:, :], bank[0][:, 0:D], cbias[:, :], ALU.add).then_inc(s_cb, 1)
            dve.wait_ge(s_cb, 1)
            dve.wait_ge(s_wts, 7)
            nc.vector.memset(bank[6], 0.0).then_inc(s_prep, 1)
            dve.wait_ge(s_prep, 1)

            def ln_stats(b, n):
                g = n % 2
                if n < 2:
                    need(dve, x1, b, 4 * g + 4)
                elif n < 4:
                    need(dve, x_ffn, b, 2 * g + 2)
                else:
                    need(dve, x_att, b, 2 * g + 2)
                need(dve, fn_norm, b, 4 * n)
                for i in range(4):
                    nc.vector.bn_stats(fstat[:, i, :], X[:, 4 * g + i, :]).then_inc(fn_stat.sem, 1)
                need(dve, fn_stat, b, 4 * n + 4)
                stand_alone(dve)
                for i in range(4):
                    nc.vector.bn_aggr(fmv[:, i, :], fstat[:, i, :]).then_inc(fn_mv.sem, 1)

            def ln_norms(b, n):
                g = n % 2
                need(dve, fn_rs, b, n + 1)
                need(dve, fn_tp, b, 2 * n)
                for i in range(4):
                    nc.vector.tensor_scalar(nrm[:, i, :], X[:, 4 * g + i, :], fmv[:, i, 0:1], frs[:, i:i + 1],
                                            ALU.subtract, ALU.mult).then_inc(fn_norm.sem, 1)

            def mixes(b, q, sides=(0, 1)):
                g, n = q % 2, q % 2 + (0, 4)[q // 2]
                need(dve, fn_T, b, 2 * n + 2)
                for i in sides:
                    dst, mu, nu, read = ((xkT, MU_K, NU_K, p_k), (xrT, MU_R, NU_R, p_r))[i]
                    need(dve, read, b, 2 * q)
                    for c in range(C):
                        nc.vector.tensor_scalar(dst[:, c, :], nT[:, c, 1 + 512 * g:513 + 512 * g],
                                                vec[:, mu.start + c:mu.start + c + 1], None, ALU.mult)\
                            .then_inc(mix_a.sem, 1)
                    for c in range(C):
                        need(dve, mix_a, b, 4 * q + 2 * i + c + 1)
                        nc.vector.scalar_tensor_tensor(dst[:, c, :], nT[:, c, 512 * g:512 + 512 * g],
                                                       vec[:, nu.start + c:nu.start + c + 1], dst[:, c, :],
                                                       ALU.mult, ALU.add).then_inc(mix_b.sem, 1)

            def gated(b, q):
                for pr in range(2):
                    need(dve, p_kv, b, 2 * q + pr + 1)
                    need(dve, r_tanh, b, 2 * q + pr + 1)
                    nc.vector.scalar_tensor_tensor(th[:, pr, :], th[:, pr, :], 1.0, bank[6 + pr],
                                                   ALU.add, ALU.mult).then_inc(kv_r.sem, 1)

            def x_out(b, t):
                need(dve, p_w, b, t + 1)
                need(dve, resid, b, t + 1)
                nc.vector.tensor_tensor(X[:, t, :], bank[7][:, 0:D], X[:, t, :], ALU.add).then_inc(x1.sem, 1)

            def z_norms(b, t):
                need(dve, z_tp, b, t - 1)
                nc.vector.tensor_scalar(zn[:, t % 2, :], Xin[:, t, :], mv[:, t, 0:1], rs2[:, 1, t:t + 1],
                                        ALU.subtract, ALU.mult).then_inc(z_norm.sem, 1)

            def ln1_stats(b):
                dve.wait_ge(x_in.sem, 16 * (b + 1))
                for t in range(NT):
                    nc.vector.bn_stats(stat[:, t, :], Xin[:, t, :]).then_inc(ln1_stat.sem, 1)
                need(dve, resid, b, 0)
                need(dve, ln1_stat, b, NT)
                stand_alone(dve)
                for t in range(NT):
                    nc.vector.bn_aggr(mv[:, t, :], stat[:, t, :]).then_inc(ln1_mv.sem, 1)

            def ln1_scales(b):
                need(dve, ln1_rs, b, 1)
                z_norms(b, 0)
                nc.vector.tensor_scalar(one_r[:, :], rs2[:, 0, :], 1.0, None, ALU.add).then_inc(ln1_sc.sem, 1)
                nc.vector.scalar_tensor_tensor(neg_mr[:, :], mv[:, :, 0], -1.0, rs2[:, 0, :], ALU.mult, ALU.mult)\
                    .then_inc(ln1_sc.sem, 1)

            ln1_stats(0)
            ln1_scales(0)
            with dve.Fori(0, B) as b:
                for t in range(NT + 1):
                    if t + 1 < NT:
                        z_norms(b, t + 1)
                    if t < NT:
                        need(dve, p_qk, b, t + 1)
                        need(dve, rope_sum, b, t)
                        qk = bank[0].rearrange("p (h a d) -> p h a d", h=8, a=2)
                        rbv = rb[:, :].rearrange("p (h a d) -> p h a d", h=8, a=2)
                        nc.vector.tensor_tensor(ra[:, :].rearrange("p (h d) -> p h d", h=8),
                                                bank[0].rearrange("p (h d) -> p h d", h=8),
                                                cos[:, t, :].unsqueeze(1).to_broadcast([P, 8, DK]), ALU.mult)\
                            .then_inc(rope_ab.sem, 1)
                        for a in range(2):
                            sn = sin[:, t, 32 * a:32 * a + 32].unsqueeze(1).to_broadcast([P, 8, DK // 2])
                            nc.vector.tensor_tensor(rbv[:, :, a, :], qk[:, :, 1 - a, :], sn, ALU.mult)\
                                .then_inc(rope_ab.sem, 1)
                    if t >= 3:
                        x_out(b, t - 3)
                    if 1 <= t <= NT:
                        u = t - 1
                        need(dve, att, b, u + 1)
                        need(dve, p_o, b, u)
                        nc.vector.tensor_tensor(AT[:, :], bank[4], mask[:, :], ALU.mult)\
                            .then_inc(att_m.sem, 1)
                        if t == NT:
                            mixes(b, 0, (0,))
                        need(dve, p_st, b, u + 1)
                        for pr in range(2):
                            new = bank[6][:, pr * DV:pr * DV + DV]
                            if u == 0:
                                i = nc.vector.tensor_copy(S[:, pr, :], new)
                            else:
                                need(dve, s_upd, b, 2 * u + pr - 1)
                                i = nc.vector.scalar_tensor_tensor(S[:, pr, :], S[:, pr, :], gamma[:, pr:pr + 1],
                                                                   new, ALU.mult, ALU.add)
                            i.then_inc(s_upd.sem, 1)
                    if t == 7:
                        ln_norms(b, 0)
                    if t < NT:
                        need(dve, p_g, b, t + 1)
                        need(dve, g_tanh, b, t + 1)
                        nc.vector.scalar_tensor_tensor(gt[:, t % 2, :], gt[:, t % 2, :], 1.0, bank[2],
                                                       ALU.add, ALU.mult).then_inc(gate.sem, 1)
                    if 1 <= t <= NT:
                        need(dve, o_rs, b, u + 1)
                        need(dve, gate, b, u + 1)
                        need(dve, y_tp, b, u)
                        for h in range(RET_HEADS):
                            nc.vector.scalar_tensor_tensor(y[:, h * DV:h * DV + DV], bank[5][:, h * DV:h * DV + DV],
                                                           ors[:, u % 2, h:h + 1], gt[:, u % 2, h * DV:h * DV + DV],
                                                           ALU.mult, ALU.mult).then_inc(y_h.sem, 1)
                    if t == 6:
                        ln_stats(b, 0)
                x_out(b, NT - 2)
                mixes(b, 0, (1,))
                x_out(b, NT - 1)
                ln_stats(b, 1)
                ln_norms(b, 1)
                mixes(b, 1)
                gated(b, 0)
                ln_stats(b, 2)
                ln_norms(b, 2)
                gated(b, 1)
                ln_stats(b, 3)

                ln_norms(b, 3)
                for n in range(8):
                    h, g, s = qk_order(n)
                    need(dve, c_hi, b, n + 1)
                    need(dve, c_lo, b, n - 1)
                    at = (BQ, BK)[s].start + h
                    tok = slice(512 * g, 512 * g + 512)
                    nc.vector.scalar_tensor_tensor(r1[:, n % 2, :], bank[2 + n % 2], vec[:, at:at + 1],
                                                   cmp[:, h, s, 0, tok], ALU.add, ALU.subtract)\
                        .then_inc(c_r1.sem, 1)
                    need(dve, c_r1, b, n + 1)
                    nc.vector.tensor_copy(cmp[:, h, s, 1, tok], r1[:, n % 2, :]).then_inc(c_mid.sem, 1)

                def row_max(u):
                    _, _, blk, col = unit(u)
                    need(dve, mx_s, b, u + 1)
                    nc.vector.tensor_reduce(mx[:, blk, col:col + 1], bank_pair[u % 2], AX_X, ALU.max)\
                        .then_inc(mx_r.sem, 1)

                def attention_out(pr):
                    need(dve, p_wo, b, pr + 1)
                    need(dve, x_cb, b, pr + 1)
                    xs = X[:, 2 * pr:2 * pr + 2, :].rearrange("p t n -> p (t n)")
                    nc.vector.tensor_tensor(xs, bank[W_BANKS[pr] + 1], xs, ALU.add).then_inc(x_att.sem, 1)

                for u in range(AHEAD):
                    row_max(u)
                u = AHEAD
                for s in range(NS + 4):
                    if s < NS:
                        while u < units[s]:
                            row_max(u)
                            u += 1
                    k = output_before(s)
                    if k is not None:
                        need(dve, o_tp, b, k + 1)
                        o = bank[7].rearrange("p (t h d) -> p t h d", t=4, h=4)
                        hg, half = k // 2, k % 2
                        nc.vector.reciprocal(orc[:, :, :], o[:, :, :, HD]).then_inc(o_rc.sem, 1)
                        need(dve, o_rc, b, k + 1)
                        dst = aO[:, 4 * half:4 * half + 4, 64 * hg:64 * hg + 64].rearrange("p t (h d) -> p t h d", h=4)
                        for i in range(4):
                            ins_ = nc.vector.tensor_tensor(dst[:, i], o[:, i, :, 0:HD],
                                                           orc[:, i, :].unsqueeze(2).to_broadcast([P, 4, HD]), ALU.mult)
                        ins_.then_inc(o_n.sem, 1)
                    if s == WIDE.start + 1:
                        ln1_stats(b + 1)
                    if s in (NS - 3, NS - 2):
                        attention_out(s - NS + 3)
                    if s == NS - 2:
                        ln_stats(b, 4)
                        ln_norms(b, 4)
                    if s == NS + 2:
                        mixes(b, 2, (0,))
                mixes(b, 2, (1,))
                attention_out(2)
                attention_out(3)
                ln_stats(b, 5)
                ln_norms(b, 5)
                mixes(b, 3)
                gated(b, 2)
                ln1_scales(b + 1)
                gated(b, 3)
                for pr in range(2):
                    need(dve, kv_r, b, 7 + pr)
                    xs = X[:, 4 + 2 * pr:6 + 2 * pr, :].rearrange("p t n -> p (t n)")
                    nc.vector.tensor_tensor(xs, xs, th[:, pr, :], ALU.add).then_inc(x_end.sem, 1)

        @block.gpsimd
        def _(pool):
            prime(pool, "pool")
            pool.wait_ge(s_prep, 1)
            pool.wait_ge(s_eb, 1)

            def rsqrts(b, n):
                need(pool, fn_mv, b, 4 * n + 4)
                need(pool, fn_norm, b, 4 * n)
                stand_alone(pool)
                nc.gpsimd.tensor_scalar(farg[:, :], fmv[:, :, 1], EPS, None, ALU.add).then_inc(fn_arg.sem, 1)
                need(pool, fn_arg, b, n + 1)
                nc.gpsimd.tensor_tensor(frs[:, :], farg[:, :], power[:, 0:4], ALU.pow).then_inc(fn_rs.sem, 1)

            def squares(b, q):
                for o in range(2):
                    need(pool, k_relu, b, 2 * q + o + 1)
                    nc.gpsimd.tensor_tensor(kact[:, o, :], kact[:, o, :], kact[:, o, :], ALU.mult)\
                        .then_inc(k_sq.sem, 1)

            def adds(b, q):
                g = q % 2
                for pr in range(2):
                    need(pool, kv_r, b, 2 * q + pr + 1)
                    t = 4 * g + 2 * pr
                    xs = X[:, t:t + 2, :].rearrange("p t n -> p (t n)")
                    nc.gpsimd.tensor_tensor(xs, xs, th[:, pr, :], ALU.add).then_inc(x_ffn.sem, 1)

            def ln1_rsqrts(b):
                need(pool, ln1_mv, b, NT)
                need(pool, z_norm, b, 0)
                stand_alone(pool)
                nc.gpsimd.tensor_scalar(var2[:, 0, :], mv[:, :, 1], 1.0, EPS, ALU.mult, ALU.add)\
                    .then_inc(ln1_arg.sem, 1)
                nc.gpsimd.tensor_scalar(var2[:, 1, :], mv[:, :, 1], 1.0 + EPS, EPS * EPS, ALU.mult, ALU.add)\
                    .then_inc(ln1_arg.sem, 1)
                need(pool, ln1_arg, b, 2)
                nc.gpsimd.tensor_tensor(rs2[:, :, :].rearrange("p a t -> p (a t)"),
                                        var2[:, :, :].rearrange("p a t -> p (a t)"), power[:, 0:16], ALU.pow)\
                    .then_inc(ln1_rs.sem, 1)

            ln1_rsqrts(0)
            with pool.Fori(0, B) as b:
                for t in range(NT + 1):
                    if t < NT:
                        if t == 0:
                            need(pool, ln1_sc, b, 2)
                        if t % 4 == 0:
                            need(pool, stored[t // 4], b, 0)
                        need(pool, rope_ab, b, 3 * t + 3)
                        nc.gpsimd.tensor_tensor(ra[:, :], ra[:, :], rb[:, :], ALU.add).then_inc(rope_sum.sem, 1)
                        nc.gpsimd.tensor_scalar(X[:, t, :], Xin[:, t, :], one_r[:, t:t + 1], neg_mr[:, t:t + 1],
                                                ALU.mult, ALU.add).then_inc(resid.sem, 1)
                        need(pool, rope_sum, b, t + 1)
                        need(pool, att, b, t)
                        nc.gpsimd.tensor_tensor(qkr[:, t % 2, :].rearrange("p (h d) -> p h d", h=8),
                                                ra[:, :].rearrange("p (h d) -> p h d", h=8),
                                                decay[:, :].unsqueeze(2).to_broadcast([P, 8, DK]), ALU.mult)\
                            .then_inc(rope_qk.sem, 1)
                    if t >= 1:
                        u = t - 1
                        need(pool, o_sq, b, 4 * u + 4)
                        stand_alone(pool)
                        nc.gpsimd.tensor_scalar(oarg[:, :], oss[:, u % 2, :], 1.0 / DV, EPS, ALU.mult, ALU.add)\
                            .then_inc(o_arg.sem, 1)
                        need(pool, o_arg, b, u + 1)
                        need(pool, y_h, b, 4 * (u - 1))
                        nc.gpsimd.tensor_tensor(ors[:, u % 2, :], oarg[:, :], power[:, 0:4], ALU.pow)\
                            .then_inc(o_rs.sem, 1)
                    if t == 6:
                        rsqrts(b, 0)
                squares(b, 0)
                rsqrts(b, 1)
                adds(b, 0)
                squares(b, 1)
                rsqrts(b, 2)
                adds(b, 1)
                rsqrts(b, 3)
                for n in range(8):
                    h, g, s = qk_order(n)
                    need(pool, c_mid, b, n + 1)
                    tok = slice(512 * g, 512 * g + 512)
                    nc.gpsimd.tensor_tensor(cmp[:, h, s, 2, tok], r1[:, n % 2, :], cmp[:, h, s, 1, tok],
                                            ALU.subtract).then_inc(c_lo.sem, 1)
                need(pool, fn_norm, b, 16)
                for pr in range(4):
                    xs = X[:, 2 * pr:2 * pr + 2, :]
                    nc.gpsimd.tensor_tensor(xs, xs, cbias[:, :].unsqueeze(1).to_broadcast([P, 2, D]), ALU.add)\
                        .then_inc(x_cb.sem, 1)
                pool.wait_ge(s_band, 16)
                for s in range(NS):
                    if s == WIDE.start + 3:
                        ln1_rsqrts(b + 1)
                    if s == NS - 1:
                        rsqrts(b, 4)
                    if not bands[s]:
                        continue
                    hg = s // 16
                    a, z, at = bands[s]
                    for c in range(4):
                        n = 4 * s + c
                        need(pool, e_p, b, n + 1)
                        nc.gpsimd.tensor_tensor(ring[:, n % RING, a:z], ring[:, n % RING, a:z],
                                                band_exp[:, 4 * hg + c, at:at + z - a], ALU.mult)\
                            .then_inc(e_band.sem, 1)
                squares(b, 2)
                rsqrts(b, 5)
                adds(b, 2)
                squares(b, 3)


def shape_constants(T, D):
    import numpy as np

    f32 = np.float32
    dk = D // RET_HEADS
    one = f32(1)
    freq = one / (10000.0 ** (np.arange(0, dk, 2, dtype=f32) / f32(dk)).astype(np.float64)).astype(f32)
    angle = (np.arange(T, dtype=f32)[:, None] * freq[None, :]).astype(np.float64)
    c, s = np.cos(angle), np.sin(angle)
    g = 1.0 - np.exp2(-5.0 - np.arange(RET_HEADS))
    i = np.arange(P)
    decay = np.concatenate([g[None] ** (i[:, None] + 1.0) * dk ** -0.5, g[None] ** (P - 1.0 - i[:, None])], 1)
    mask = (i[:, None, None] <= i[None, None, :]) * (g ** -float(P))[None, :, None]
    head = np.arange(P) // 64
    gamma = np.stack([g[2 * pr + head] ** P for pr in range(2)], 1)
    n = np.maximum(np.arange(384) - (P - 1), 0)
    big = 16 + (np.log(np.maximum(n, 1).astype(f32) / f32(16)) / f32(np.log(8)) * f32(16)).astype(np.int32)
    bucket = np.where(n < 16, n, np.minimum(big, BUCKETS - 1))
    rows = np.zeros((32, 64))
    rows[0, 0:8] = 1
    for part in range(PARTS):
        for j in range(8):
            r, blk = 1 + 8 * part + j, np.arange(8)
            rows[r, 0:8] = blk == j
            rows[r, 8:16] = blk < j
            rows[r, 16:24] = blk > j + 1
            rows[r, 24], rows[r, 25] = -(part >= 1), -(part >= 2)
    return {
        "c_ident": np.eye(P), "c_cos": np.concatenate([c, c], 1), "c_sin": np.concatenate([-s, s], 1),
        "c_decay": decay, "c_mask": mask.reshape(P, -1), "c_gamma": gamma,
        "c_onehot": bucket[None, :] == np.arange(BUCKETS)[:, None], "c_rows": rows,
    }


_INS = ["L0_attn_a_x", "L0_attn_a_ln_w", "L0_attn_a_ln_b", "L0_attn_a_Wq", "L0_attn_a_Wk", "L0_attn_a_Wv",
        "L0_attn_a_Wg", "L0_attn_a_g_norm_w", "L0_attn_a_Wo", "L0_attn_b_wq", "L0_attn_b_bq", "L0_attn_b_wk",
        "L0_attn_b_bk", "L0_attn_b_wv", "L0_attn_b_bv", "L0_attn_b_wo", "L0_attn_b_bo", "L0_attn_b_rel_bias",
        "L0_ffn_W_r", "L0_ffn_W_k", "L0_ffn_W_v", "L0_ffn_mu_r", "L0_ffn_mu_k"]


def kernel(**inputs):
    import numpy as np
    import concourse.bacc as bacc
    from concourse.bass_utils import run_bass_kernel_spmd

    nc = bacc.Bacc("TRN2", target_bir_lowering=False, num_devices=1)
    arrays = {n: np.ascontiguousarray(inputs[n]) for n in _INS}
    shape = arrays[_INS[0]].shape
    arrays |= {n: np.ascontiguousarray(a, np.float32) for n, a in shape_constants(shape[1], shape[2]).items()}
    aps = [nc.dram_tensor(n, a.shape, mybir.dt.from_np(a.dtype), kind="ExternalInput").ap()
           for n, a in arrays.items()]
    out = nc.dram_tensor("out", shape, F32, kind="ExternalOutput").ap()
    build(nc, aps, out)
    return run_bass_kernel_spmd(nc, [arrays], core_ids=[0]).results[0]["out"]
```

```python
from contextlib import ExitStack

import concourse.bass as bass
from concourse import mybir

F32 = mybir.dt.float32
BF16 = mybir.dt.bfloat16
ALU = mybir.AluOpType
ACT = mybir.ActivationFunctionType
AX_X = mybir.AxisListType.X

P = 128
EPS = 1e-5
RET_HEADS = 4
HEADS = 16
BUCKETS = 32
PARTS = 3
Q_PARTS = (2, 1, 0, 1, 0, 0)
K_PARTS = (0, 1, 2, 0, 1, 0)
RUNS = ((0, 3), (3, 2), (5, 1))
MAX_ROW = 96
RING = 12
LAG = 2
AHEAD = 22
KEY_ORDER = ((0, 4, 1, 5, 2, 6, 3, 7), (3, 0, 4, 1, 5, 2, 6, 7))


class Tally:

    def __init__(self, sem, each, step=1):
        self.sem, self.each, self.step = sem, each, step

    def at(self, b, n):
        return (b + 1) * (self.each * self.step) + n * self.step


def band(half, j):
    lo, hi = P * j - 512 * half, P * j + 2 * P - 512 * half
    a, z = max(lo, 0), min(hi, 512)
    return (a, z, a - lo) if a < z else None


def build(nc, ins, out):
    x, ln_w, ln_b, Wq, Wk, Wv, Wg, g_norm_w, Wo = ins[:9]
    wq, bq, wk, bk, wv, bv, wo, bo, rel_bias, W_r, W_k, W_v, mu_r, mu_k = ins[9:23]
    c_ident, c_cos, c_sin, c_decay, c_mask, c_gamma, c_onehot, c_rows = ins[23:]

    B, T, D = x.shape
    NT = T // P
    NG = NT // 4
    C = D // P
    DK, DV = D // RET_HEADS, 2 * D // RET_HEADS
    HD = D // HEADS
    NU = HEADS * NT
    NS = HEADS // 4 * 2 * NT

    with ExitStack() as ctx:
        def sb(name, shape, dt=F32):
            return ctx.enter_context(nc.sbuf_tensor(name, shape, dt))

        def sem(name):
            return ctx.enter_context(nc.semaphore(name))

        tallies = {"pe": [], "act": [], "dve": [], "pool": [], "sp": []}

        def tally(owner, name, each, step=1):
            t = Tally(sem(name), each, step)
            tallies[owner].append(t)
            return t

        psum = ctx.enter_context(nc.psum_tensor("psum", [P, 8, 512], F32))
        bank = [psum[:, i, :] for i in range(8)]
        bank_pair = [psum[:, 2 * i:2 * i + 2, :].rearrange("p a n -> p (a n)") for i in range(2)]

        ident = sb("ident", [P, P])
        cos = sb("cos", [P, NT, DK])
        sin = sb("sin", [P, NT, DK])
        decay = sb("decay", [P, 8])
        mask = sb("mask", [P, 512])
        gamma = sb("gamma", [P, 2])
        Wqkvg = sb("Wqkvg", [P, C, 6 * D])
        WoS = sb("WoS", [P, 4, D])
        WT = sb("WT", [P, 7, C, D])
        W_R, W_K, W_V, A_Q, A_K, A_V, A_O = range(7)
        vec = sb("vec", [P, 24])
        LN_W, LN_B, BQ, BK, BV, MU_R, MU_K, GW, NU_R, NU_K = [slice(2 * i, 2 * i + 2) for i in range(10)]
        cbias = sb("cbias", [P, D])
        power = sb("power", [P, 16])
        X = sb("X", [P, NT, D])
        Xin = sb("Xin", [P, NT, D])
        SQ = sb("SQ", [P, HEADS, T], BF16)
        SK = sb("SK", [P, HEADS, T], BF16)
        Vx = sb("Vx", [P, NT, HEADS, HD + 1])
        band_exp = sb("band_exp", [P, HEADS, 2 * P])
        nT = sb("nT", [P, C, 1 + T])
        nrm = sb("nrm", [P, 4, D])
        xrT = sb("xrT", [P, C, 512])
        xkT = sb("xkT", [P, C, 512])
        mixed = sb("mixed", [P, 2048])
        kact = mixed[:, 0:1024].rearrange("p (a n) -> p a n", a=2)
        th = mixed[:, 1024:2048].rearrange("p (a n) -> p a n", a=2)
        aO = mixed[:, :].rearrange("p (t n) -> p t n", t=NT)
        qbd = sb("qbd", [P, 2, 2, 2, P])
        S = sb("S", [P, 2, DV])
        stat = sb("stat", [P, NT, 6])
        mv = sb("mv", [P, NT, 2])
        var2 = sb("var2", [P, 2, NT])
        rs2 = sb("rs2", [P, 2, NT])
        one_r = sb("one_r", [P, NT])
        neg_mr = sb("neg_mr", [P, NT])
        fstat = sb("fstat", [P, 4, 6])
        fmv = sb("fmv", [P, 4, 2])
        farg = sb("farg", [P, 4])
        frs = sb("frs", [P, 4])
        oss = sb("oss", [P, 2, 4])
        oarg = sb("oarg", [P, 4])
        ors = sb("ors", [P, 2, 4])
        mx = sb("mx", [P, 8, 16])
        mrow = sb("mrow", [16, 2, P], BF16)
        orc = sb("orc", [P, 4, 4])
        Z = sb("Z", [P, 7680])

        def cut(at, n):
            return Z[:, at:at + n]

        zn = cut(0, 512).rearrange("p (a n) -> p a n", a=2)
        zT = cut(512, 512).rearrange("p (a c n) -> p a c n", a=2, c=C)
        ra = cut(1024, 512)
        rb = cut(1536, 512)
        qkr = cut(2048, 1024).rearrange("p (a n) -> p a n", a=2)
        kT = cut(3072, 512).rearrange("p (a c n) -> p a c n", a=2, c=2)
        AT = cut(3584, 512)
        v_sb = cut(4096, 1024).rearrange("p (a n) -> p a n", a=2)
        gt = cut(5120, 1024).rearrange("p (a n) -> p a n", a=2)
        y = cut(6144, 512)
        yT = cut(6656, 512)
        sq_junk = cut(7168, 512)
        ring = cut(0, RING * 512).rearrange("p (s n) -> p s n", s=RING)
        cmp = cut(0, 6144).bitcast(BF16).rearrange("p (h s k n) -> p h s k n", h=2, s=2, k=PARTS)
        r1 = cut(6144, 1024).rearrange("p (a n) -> p a n", a=2)
        aT = r1
        oT = cut(7168, 512)
        raw = cut(0, 3584).rearrange("p (w c n) -> p w c n", w=7, c=C)

        scratch = nc.dram_tensor("bias_scratch", (HEADS, 384), F32, kind="Internal").ap()
        rows_scratch = nc.dram_tensor("bias_rows", (P, HEADS * 384), F32, kind="Internal").ap()

        parts_scratch = nc.dram_tensor("parts", (2, HEADS, PARTS, HD, T), BF16, kind="Internal").ap()

        s_tables = sem("s_tables")
        s_raw = sem("s_raw")
        s_const = sem("s_const")
        s_zero = sem("s_zero")
        s_top = sem("s_top")
        s_chain = sem("s_chain")
        s_wt = sem("s_wt")
        s_wts = sem("s_wts")
        s_dist = sem("s_dist")
        s_exp = sem("s_exp")
        s_table = sem("s_table")
        s_rep = sem("s_rep")
        s_band = sem("s_band")
        s_rowq = sem("s_rowq")
        s_rowk = sem("s_rowk")
        s_rowsk = sem("s_rowsk")
        s_bvb = sem("s_bvb")
        s_bvo = sem("s_bvo")
        s_cbias = sem("s_cbias")
        s_bank6 = sem("s_bank6")
        x_in = Tally(sem("x_in"), 1, 16)
        stored = [tally("sp", f"stored{g}", 1, 16) for g in range(NG)]
        ln1_stat = tally("dve", "ln1_stat", NT)
        ln1_mv = tally("dve", "ln1_mv", NT)
        ln1_arg = tally("pool", "ln1_arg", 2)
        ln1_rs = tally("pool", "ln1_rs", 2)
        ln1_sc = tally("dve", "ln1_sc", 2)
        z_norm = tally("dve", "z_norm", NT)
        resid = tally("pool", "resid", NT)
        z_tp = tally("pe", "z_tp", NT)
        z_T = tally("act", "z_T", 2 * NT)
        p_qk = tally("pe", "p_qk", NT)
        p_v = tally("pe", "p_v", NT)
        p_g = tally("pe", "p_g", NT)
        rope_ab = tally("dve", "rope_ab", 3 * NT)
        rope_sum = tally("pool", "rope_sum", NT)
        rope_qk = tally("pool", "rope_qk", NT)
        qk_tp = tally("pe", "qk_tp", NT)
        kq_T = tally("act", "kq_T", 3 * NT)
        att = tally("pe", "att", NT)
        att_m = tally("dve", "att_m", NT)
        v_cp = tally("act", "v_cp", NT)
        p_o = tally("pe", "p_o", NT)
        p_st = tally("pe", "p_st", NT - 1)
        s_upd = tally("dve", "s_upd", 2 * (NT - 1))
        o_sq = tally("act", "o_sq", 4 * NT)
        o_arg = tally("pool", "o_arg", NT)
        o_rs = tally("pool", "o_rs", NT)
        g_tanh = tally("act", "g_tanh", NT)
        gate = tally("dve", "gate", NT)
        y_h = tally("dve", "y_h", 4 * NT)
        y_tp = tally("pe", "y_tp", NT)
        y_T = tally("act", "y_T", NT)
        p_w = tally("pe", "p_w", NT)
        x1 = tally("dve", "x1", NT)
        fn_stat = tally("dve", "fn_stat", 24)
        fn_mv = tally("dve", "fn_mv", 24)
        fn_arg = tally("pool", "fn_arg", 6)
        fn_rs = tally("pool", "fn_rs", 6)
        fn_norm = tally("dve", "fn_norm", 24)
        fn_tp = tally("pe", "fn_tp", 12)
        fn_T = tally("act", "fn_T", 12)
        mix_a = tally("act", "mix_a", 16)
        mix_b = tally("dve", "mix_b", 16)
        p_k = tally("pe", "p_k", 8)
        k_relu = tally("act", "k_relu", 8)
        k_sq = tally("pool", "k_sq", 8)
        p_r = tally("pe", "p_r", 8)
        r_tanh = tally("act", "r_tanh", 8)
        p_kv = tally("pe", "p_kv", 8)
        kv_r = tally("dve", "kv_r", 8)
        x_ffn = tally("pool", "x_ffn", 6)
        x_end = tally("dve", "x_end", 2)
        x_cb = tally("pool", "x_cb", 4)
        p_qkT = tally("pe", "p_qkT", 8)
        c_hi = tally("act", "c_hi", 8)
        c_r1 = tally("dve", "c_r1", 8)
        c_mid = tally("dve", "c_mid", 8)
        c_lo = tally("pool", "c_lo", 8)
        parts_out = [tally("sp", f"parts_out_{side}", 6, 16) for side in "qk"]
        spread = [tally("sp", f"spread{share}", 6, 16) for share in range(3)]
        p_vx = tally("pe", "p_vx", 4)
        vx_cp = tally("act", "vx_cp", 4)
        mx_s = tally("pe", "mx_s", NU)
        mx_r = tally("dve", "mx_r", NU)
        mx_tp = tally("pe", "mx_tp", 8)
        mx_row = tally("act", "mx_row", 8)
        mx_in = [tally("sp", f"mx_in{i}", 16, 16) for i in range(2)]
        e_s = tally("pe", "e_s", 4 * NS)
        e_p = tally("act", "e_p", 4 * NS)
        e_band = tally("pool", "e_band", 36 * 4)
        e_pv = tally("pe", "e_pv", NS)
        o_cp = tally("act", "o_cp", 7)
        o_cp_6 = tally("dve", "o_cp_6", 1)
        o_tp = tally("pe", "o_tp", 8)
        o_rc = tally("dve", "o_rc", 8)
        o_n = tally("dve", "o_n", 8)
        w_tp = tally("pe", "w_tp", 4)
        w_T_early = tally("dve", "w_T_early", 2)
        w_T = tally("act", "w_T", 2)
        p_wo = tally("pe", "p_wo", 4)
        x_att = tally("dve", "x_att", 4)

        def prime(eng, owner):
            for t in tallies[owner]:
                eng.sem_inc(t.sem, t.each * t.step)

        def need(eng, t, b, n):
            eng.wait_ge(t.sem, t.at(b, n))

        def stand_alone(eng):
            eng.nop(nofuse=True)

        bands = [band((s // 8) % 2, KEY_ORDER[(s // 8) % 2][s % 8]) for s in range(NS)]
        banded = [sum(z is not None for z in bands[:s + 1]) for s in range(NS)]
        units = [min(NU, AHEAD + 2 * (s + 1)) for s in range(NS)]

        def unit(u):
            blk, ii, hh = u // 16, u % 16 // 4, u % 4
            return blk // 2 * 4 + hh, blk % 2 * 4 + ii, blk, hh * 4 + ii

        def qk_order(n):
            return n // 4, n // 2 % 2, n % 2

        def step(s):
            hg, half = s // 16, s // 8 % 2
            return hg, half, KEY_ORDER[half][s % 8]

        WIDE = range(units.index(NU) + 1, NS - 4)
        W_BANKS = (0, 2, 0, 6)

        def col_bank(s, c):
            return bank[(4, 5, 2, 3)[c] if s in WIDE else 4 + c % 2]

        def maxima_in(s):
            return (s + 3) // 8 if (s + 3) % 8 == 0 and 0 < (s + 3) // 8 < 8 else None

        def output_before(s):
            return (s - 11) // 8 if s >= 11 and (s - 11) % 8 == 0 else None

        SHARES = (slice(0, 4), slice(4, 8), slice(8, 16))
        N_TABLES, N_RAW, N_CONST = 6, 7, 19

        block = ctx.enter_context(nc.Block())

        @block.sync
        def _(sp):
            prime(sp, "sp")
            xv = x.rearrange("b (t p) d -> b p t d", p=P)
            ov = out.rearrange("b (t p) d -> b p t d", p=P)
            sp.dma_start(Xin[:, :, :], xv[0]).then_inc(x_in.sem, 16)

            def load(dst, src, done):
                sp.dma_start(dst, src, allow_slow_non_contiguous=True).then_inc(done, 16)

            load(ident[:, :], c_ident, s_tables)
            load(xkT[0:BUCKETS, 0, 0:384], c_onehot, s_tables)
            load(xkT[0:BUCKETS, 1, 0:HEADS], rel_bias, s_tables)
            load(xkT[0:HEADS, 1, 32:64], rel_bias.rearrange("k h -> h k"), s_tables)
            load(xrT[96:128, 0, :], bass.AP(rel_bias.tensor, 0, [[0, 32], [1, BUCKETS * HEADS]]), s_tables)
            load(xrT[96:128, 1, 0:64], c_rows, s_tables)
            for i, w in enumerate((W_r, W_k, W_v, wq, wk, wv, wo)):
                load(raw[:, i], w.rearrange("(c p) n -> p c n", p=P), s_raw)
            vectors = ((LN_W, ln_w), (LN_B, ln_b), (BQ, bq), (BK, bk), (BV, bv), (MU_R, mu_r), (MU_K, mu_k))
            for at, v in vectors:
                load(vec[:, at], v.rearrange("(c p) -> p c", p=P), s_const)
            load(vec[:, GW.start:GW.start + 1], g_norm_w.rearrange("(p c) -> p c", c=1), s_const)
            load(cos[:, :, :], c_cos.rearrange("(t p) n -> p t n", p=P), s_const)
            load(sin[:, :, :], c_sin.rearrange("(t p) n -> p t n", p=P), s_const)
            load(decay[:, :], c_decay, s_const)
            load(mask[:, :], c_mask, s_const)
            load(gamma[:, :], c_gamma, s_const)
            load(cbias[:, :], bass.AP(bo.tensor, 0, [[0, P], [1, D]]), s_const)
            for w, c0, c1 in ((Wq, 0, D), (Wk, D, 2 * D), (Wv, 2 * D, 4 * D), (Wg, 4 * D, 6 * D)):
                load(Wqkvg[:, :, c0:c1], w.rearrange("(c p) n -> p c n", p=P), s_const)
            load(WoS[:, :, :], Wo.rearrange("(c p) n -> p c n", p=P), s_const)
            sp.wait_ge(s_rowk, 1)
            load(SK[96:128, 1:HEADS, :], SK[96:128, 0, :].unsqueeze(1).to_broadcast([32, HEADS - 1, T]), s_rowsk)
            sp.wait_ge(s_exp, 1)
            sp.dma_start(scratch, kact[0:HEADS, 0, 0:384]).then_inc(s_table, 16)
            sp.wait_ge(s_table, 16)
            sp.dma_start(rows_scratch, bass.AP(scratch.tensor, 0, [[0, P], [1, HEADS * 384]])).then_inc(s_rep, 16)
            sp.wait_ge(s_rep, 16)
            sp.dma_start(band_exp[:, :, :],
                         bass.AP(rows_scratch.tensor, P - 1, [[HEADS * 384 - 1, P], [384, HEADS], [1, 2 * P]]))\
                .then_inc(s_band, 16)

            def parts_store(b, h, s):
                need(sp, c_lo, b, 4 * h + 3 + s)
                for part in range(PARTS):
                    slot = (PARTS - 1 - part, part)[s]
                    sp.dma_start(parts_scratch[s, 8 * h:8 * h + 8, slot],
                                 cmp[:, h, s, part, :]).then_inc(parts_out[s].sem, 16)

            def spread_rows(b, share, s):
                heads = SHARES[share]
                need(sp, parts_out[s], b, 3 * (heads.start // 8) + 3)
                stack, parts = ((SQ, Q_PARTS), (SK, K_PARTS))[s]
                for first, length in RUNS:
                    slot = (PARTS - 1 - parts[first], parts[first])[s]
                    sp.dma_start(stack[HD * first:HD * (first + length), heads, :],
                                 parts_scratch[s, heads, slot:slot + length]
                                 .rearrange("h k d n -> (k d) h n")).then_inc(spread[share].sem, 16)

            with sp.Fori(0, B) as b:
                need(sp, z_norm, b, NT)
                need(sp, resid, b, NT)
                sp.dma_start(Xin[:, :, :], xv[(b + 1) % B]).then_inc(x_in.sem, 16)
                for h in range(2):
                    for s in range(2):
                        parts_store(b, h, s)
                    for share in ((0, 1), (2,))[h]:
                        for s in range(2):
                            spread_rows(b, share, s)
                for blk in range(8):
                    need(sp, mx_row, b, blk + 1)
                    h0, q0 = blk // 2 * 4, blk % 2 * 512
                    for hh in range(4):
                        sp.dma_start(SQ[MAX_ROW:MAX_ROW + 1, h0 + hh, q0:q0 + 512],
                                     mrow[4 * hh:4 * hh + 4, blk % 2, :]).then_inc(mx_in[blk % 2].sem, 16)
                for g in range(NG):
                    need(sp, *((x_ffn, b, 6), (x_end, b, 2))[g])
                    sp.dma_start(ov[b, :, 4 * g:4 * g + 4], X[:, 4 * g:4 * g + 4, :]).then_inc(stored[g].sem, 16)
            for g in range(NG):
                need(sp, stored[g], B - 1, 1)
            sp.wait_ge(x_in.sem, 16 * (B + 1))

        @block.tensor
        def _(pe):
            prime(pe, "pe")
            pe.wait_ge(s_tables, 16 * N_TABLES)
            pe.matmul(bank[7][0:HEADS, 0:384], xkT[0:BUCKETS, 1, 0:HEADS], xkT[0:BUCKETS, 0, 0:384],
                      start=True, stop=True).then_inc(s_dist, 1)
            pe.wait_ge(s_raw, 16 * N_RAW)
            for w in range(7):
                for ci in range(C):
                    for co in range(C):
                        mm = pe.transpose(bank[w][:, ci * D + co * P:ci * D + co * P + P],
                                          raw[:, w, co, ci * P:ci * P + P], ident[:, :])
                mm.then_inc(s_wt, 1)
            pe.wait_ge(s_wts, 7)
            pe.wait_ge(s_bvb, 2)
            for c in range(C):
                mm = pe.matmul(bank[0][:, 0:D], nrm[:, 0, c * P:c * P + P], WT[:, A_O, c, :],
                               start=c == 0, stop=c == C - 1)
            mm.then_inc(s_bvo, 1)
            pe.wait_ge(s_cbias, 1)
            pe.wait_ge(s_exp, 1)
            pe.wait_ge(s_bank6, 1)
            pe.wait_ge(s_zero, 6)
            pe.wait_ge(s_rowq, HEADS)
            pe.wait_ge(s_rowsk, 16)

            def z_transposes(b, t):
                need(pe, z_norm, b, t + 1)
                if t == 0:
                    need(pe, fn_T, b, 0)
                else:
                    need(pe, s_upd, b, 2 * (t - 1))
                    need(pe, z_T, b, 2 * t)
                    need(pe, kv_r, b, 0)
                for c in range(C):
                    mm = pe.transpose(bank[6 if t else 0][:, c * P:c * P + P],
                                      zn[:, t % 2, c * P:c * P + P], ident[:, :])
                mm.then_inc(z_tp.sem, 1)

            def project(b, t, dst, c0, done):
                for c in range(C):
                    mm = pe.matmul(bank[dst], zT[:, t % 2, c, :], Wqkvg[:, c, c0:c0 + 512],
                                   start=c == 0, stop=c == C - 1)
                mm.then_inc(done.sem, 1)

            def ln_transposes(b, n):
                need(pe, fn_norm, b, 4 * n + 4)
                need(pe, fn_T, b, 2 * n)
                for c in range(C):
                    for i in range(4):
                        mm = pe.transpose(bank[c][:, i * P:i * P + P], nrm[:, i, c * P:c * P + P], ident[:, :])
                    mm.then_inc(fn_tp.sem, 1)

            def mix_k(b, q, o):
                need(pe, k_relu, b, 2 * q + o - 1)
                for c in range(C):
                    if o == 0:
                        need(pe, mix_b, b, 4 * q + c + 1)
                    mm = pe.matmul(bank[2 + o], WT[:, W_K, c, o * P:o * P + P], xkT[:, c, :],
                                   start=c == 0, stop=c == C - 1)
                mm.then_inc(p_k.sem, 1)

            def mix_r(b, q, pr):
                need(pe, mix_b, b, 4 * q + 4)
                need(pe, r_tanh, b, 2 * q + pr - 1)
                if q == 0 and pr == 0:
                    need(pe, att_m, b, NT)
                if q == 0 and pr == 1:
                    need(pe, y_h, b, 4 * NT)
                for i in range(2):
                    t = 2 * pr + i
                    for c in range(C):
                        mm = pe.matmul(bank[4 + pr][:, i * D:i * D + D], xrT[:, c, t * P:t * P + P],
                                       WT[:, W_R, c, :], start=c == 0, stop=c == C - 1)
                mm.then_inc(p_r.sem, 1)

            def mix_kv(b, q, pr):
                need(pe, k_sq, b, 2 * q + 2)
                need(pe, kv_r, b, 2 * q + pr - 1)
                if q == 2:
                    need(pe, *((w_T, b, 2), (x_att, b, 4))[pr])
                if q == 0 and pr == 1:
                    need(pe, x1, b, NT)
                for i in range(2):
                    t = 2 * pr + i
                    for o in range(2):
                        mm = pe.matmul(bank[6 + pr][:, i * D:i * D + D], kact[:, o, t * P:t * P + P],
                                       WT[:, W_V, o, :], start=o == 0, stop=o == 1)
                mm.then_inc(p_kv.sem, 1)

            def channel_mix(b, f):
                n, q = (0, 4)[f], 2 * f
                mix_kv(b, q, 0)
                ln_transposes(b, n + 1)
                mix_kv(b, q, 1)
                for o in range(2):
                    mix_k(b, q + 1, o)
                for pr in range(2):
                    mix_r(b, q + 1, pr)
                if f == 1:
                    z_transposes(b + 1, 0)
                for pr in range(2):
                    mix_kv(b, q + 1, pr)

            def qk_project(b, n):
                h, g, side = qk_order(n)
                need(pe, c_r1, b, n - 1)
                for c in range(C):
                    mm = pe.matmul(bank[2 + n % 2], WT[:, A_Q + side, c, h * P:h * P + P],
                                   nT[:, c, 1 + 512 * g:513 + 512 * g], start=c == 0, stop=c == C - 1)
                mm.then_inc(p_qkT.sem, 1)

            def v_project(b, pr):
                need(pe, vx_cp, b, pr - 1)
                for i in range(2):
                    t = 2 * pr + i
                    for c in range(C):
                        mm = pe.matmul(bank[4 + pr % 2][:, i * D:i * D + D], nT[:, c, 1 + t * P:1 + t * P + P],
                                       WT[:, A_V, c, :], start=c == 0, stop=c == C - 1)
                mm.then_inc(p_vx.sem, 1)

            def score_rows(b, u):
                h, i, _, _ = unit(u)
                for share, heads in enumerate(SHARES):
                    if u == NT * heads.start:
                        need(pe, spread[share], b, 6)
                if u < 2:
                    need(pe, fn_T, b, 8)
                    need(pe, c_r1, b, 8)
                else:
                    need(pe, mx_r, b, u - 1)
                for k in range(2):
                    mm = pe.matmul(bank[2 * (u % 2) + k], SQ[0:MAX_ROW, h, i * P:i * P + P],
                                   SK[0:MAX_ROW, h, 512 * k:512 * k + 512], start=True, stop=True)
                mm.then_inc(mx_s.sem, 1)

            def max_transpose(b, blk):
                need(pe, mx_r, b, 16 * blk + 16)
                if blk == 0:
                    need(pe, kv_r, b, 4)
                else:
                    need(pe, mx_row, b, blk)
                    need(pe, o_n, b, blk - 1)
                pe.transpose(bank[7][0:16, 0:P], mx[:, blk, :], ident[:, :]).then_inc(mx_tp.sem, 1)

            def score_cols(b, s, c):
                hg, half, j = step(s)
                n = 4 * s + c
                if c == 0 and s % 8 == 0:
                    need(pe, mx_in[(s // 8) % 2], b, 4 * (s // 16 + 1))
                if n < 2:
                    need(pe, vx_cp, b, 4)
                elif s == WIDE.start and c >= 2:
                    need(pe, mx_r, b, NU)
                elif s in WIDE and s > WIDE.start:
                    need(pe, e_p, b, n - 3)
                else:
                    need(pe, e_p, b, n - 1)
                h = 4 * hg + c
                pe.matmul(col_bank(s, c), SK[:, h, j * P:j * P + P], SQ[:, h, 512 * half:512 * half + 512],
                          start=True, stop=True).then_inc(e_s.sem, 1)

            def output_copied(b, k):
                if k == 6:
                    need(pe, o_cp_6, b, 1)
                else:
                    need(pe, o_cp, b, k + 1 if k < 6 else 7)

            def weigh(b, s):
                hg, half, j = step(s)
                if bands[s]:
                    need(pe, e_band, b, 4 * banded[s])
                else:
                    need(pe, e_p, b, 4 * s + 4)
                if s == 0:
                    need(pe, kv_r, b, 4)
                elif s % 8 == 0:
                    output_copied(b, s // 8 - 1)
                for c in range(4):
                    mm = pe.matmul(bank[6][32 * c:32 * c + HD + 1, :], Vx[:, j, 4 * hg + c, :],
                                   ring[:, (4 * s + c) % RING, :], start=s % 8 == 0, stop=s % 8 == 7)
                mm.then_inc(e_pv.sem, 1)

            def output_transposes(b, k):
                output_copied(b, k)
                need(pe, mx_row, b, min(k + 2, 8))
                need(pe, o_n, b, k)
                for i in range(4):
                    mm = pe.transpose(bank[7][:, i * P:i * P + P], oT[:, i * P:i * P + P], ident[:, :])
                mm.then_inc(o_tp.sem, 1)

            def w_transposes(b, pr):
                need(pe, o_n, b, 7 + pr // 2)
                if pr == 0:
                    need(pe, mx_r, b, NU)
                elif pr == 1:
                    need(pe, e_p, b, 4 * WIDE.stop)
                elif pr == 2:
                    need(pe, fn_T, b, 10)
                else:
                    output_copied(b, 7)
                for i in range(2):
                    for c in range(C):
                        mm = pe.transpose(bank[W_BANKS[pr]][:, (2 * i + c) * P:(2 * i + c) * P + P],
                                          aO[:, 2 * pr + i, c * P:c * P + P], ident[:, :])
                mm.then_inc(w_tp.sem, 1)

            def w_project(b, pr):
                need(pe, *((w_T_early, b, pr + 1) if pr < 2 else (w_T, b, pr - 1)))
                for i in range(2):
                    for c in range(C):
                        mm = pe.matmul(bank[W_BANKS[pr] + 1][:, i * D:i * D + D],
                                       aT[:, pr % 2, (2 * i + c) * P:(2 * i + c) * P + P],
                                       WT[:, A_O, c, :], start=c == 0, stop=c == C - 1)
                mm.then_inc(p_wo.sem, 1)

            def y_transposes(b, u):
                need(pe, y_h, b, 4 * u + 4)
                need(pe, x1, b, u)
                if u == 0:
                    need(pe, kv_r, b, 0)
                for i in range(4):
                    mm = pe.transpose(bank[7][:, i * P:i * P + P], y[:, i * P:i * P + P], ident[:, :])
                mm.then_inc(y_tp.sem, 1)

            def y_project(b, u):
                need(pe, y_T, b, u + 1)
                for h in range(RET_HEADS):
                    mm = pe.matmul(bank[7][:, 0:D], yT[:, h * P:h * P + P], WoS[:, h, :],
                                   start=h == 0, stop=h == 3)
                mm.then_inc(p_w.sem, 1)

            z_transposes(0, 0)
            with pe.Fori(0, B) as b:
                for t in range(NT + 1):
                    if t == NT:
                        need(pe, rope_ab, b, 3 * NT)
                        need(pe, v_cp, b, NT)
                        ln_transposes(b, 0)
                    if t < NT:
                        need(pe, z_T, b, 2 * t + 2)
                        need(pe, rope_ab, b, 3 * t)
                        project(b, t, 0, 0, p_qk)
                    if 3 <= t <= NT:
                        y_project(b, t - 3)
                    if 1 <= t <= NT:
                        u = t - 1
                        need(pe, kq_T, b, 3 * u + 3)
                        need(pe, att_m, b, u)
                        if u == 0:
                            need(pe, r_tanh, b, 0)
                        for pr in range(2):
                            mm = pe.matmul(bank[4][:, 256 * pr:256 * pr + 256], kT[:, u % 2, pr, :],
                                           qbd[:, u % 2, pr, :, :].rearrange("p a n -> p (a n)"),
                                           start=True, stop=True)
                        mm.then_inc(att.sem, 1)
                    if t < NT:
                        need(pe, v_cp, b, t)
                        project(b, t, 1, 512, p_v)
                    if 1 <= t <= NT:
                        need(pe, att_m, b, u + 1)
                        need(pe, v_cp, b, u + 1)
                        need(pe, s_upd, b, 2 * u)
                        need(pe, y_h, b, 4 * u)
                        for h in range(RET_HEADS):
                            o = bank[5][:, h * DV:h * DV + DV]
                            mm = pe.matmul(o, AT[:, h * P:h * P + P], v_sb[:, u % 2, h * DV:h * DV + DV],
                                           start=True, stop=u == 0)
                            if u > 0:
                                mm = pe.matmul(o, qbd[:, u % 2, h // 2, h % 2, :], S[:, h // 2, :],
                                               start=False, stop=True)
                        mm.then_inc(p_o.sem, 1)
                        if u < NT - 1:
                            need(pe, z_T, b, 2 * u + 4)
                            for h in range(RET_HEADS):
                                rows, at = DK * (h % 2), DV * (h // 2)
                                mm = pe.matmul(bank[6][rows:rows + DK, at:at + DV],
                                               qkr[:, u % 2, 256 + h * DK:256 + h * DK + DK],
                                               v_sb[:, u % 2, h * DV:h * DV + DV], start=True, stop=True,
                                               skip_group_check=True)
                            mm.then_inc(p_st.sem, 1)
                    if t < NT:
                        need(pe, gate, b, t)
                        if t == 0:
                            need(pe, k_relu, b, 0)
                        project(b, t, 2, 1024, p_g)
                        if t + 1 < NT:
                            z_transposes(b, t + 1)
                        need(pe, rope_qk, b, t + 1)
                        need(pe, kq_T, b, 3 * t)
                        for i in range(4):
                            mm = pe.transpose(bank[3][:, i * P:i * P + P], qkr[:, t % 2, i * P:i * P + P], ident[:, :])
                        mm.then_inc(qk_tp.sem, 1)
                    if 2 <= t <= NT:
                        y_transposes(b, t - 2)
                need(pe, gate, b, NT)
                need(pe, kq_T, b, 3 * NT)
                mix_k(b, 0, 0)
                y_project(b, NT - 2)
                y_transposes(b, NT - 1)
                mix_k(b, 0, 1)
                y_project(b, NT - 1)
                mix_r(b, 0, 0)
                mix_r(b, 0, 1)
                need(pe, s_upd, b, 2 * (NT - 1))
                channel_mix(b, 0)
                ln_transposes(b, 2)
                need(pe, k_relu, b, 4)
                need(pe, fn_T, b, 6)
                need(pe, r_tanh, b, 4)
                for n in range(8):
                    if n == 2:
                        v_project(b, 0)
                        ln_transposes(b, 3)
                        v_project(b, 1)
                        need(pe, fn_T, b, 8)
                    qk_project(b, n)
                v_project(b, 2)
                v_project(b, 3)
                for u in range(AHEAD):
                    score_rows(b, u)
                    if u == 17:
                        max_transpose(b, 0)
                u = AHEAD
                for s in range(NS + LAG):
                    if output_before(s) is not None:
                        output_transposes(b, output_before(s))
                    if s < NS:
                        for c in range(4):
                            score_cols(b, s, c)
                            while c == 1 and u < units[s]:
                                score_rows(b, u)
                                u += 1
                        if maxima_in(s) is not None:
                            max_transpose(b, maxima_in(s))
                    if s == NS:
                        need(pe, x_att, b, 1)
                        ln_transposes(b, 4)
                    if s >= LAG:
                        weigh(b, s - LAG)
                    if s == NS - 4:
                        w_transposes(b, 0)
                        w_transposes(b, 1)
                    if s == NS - 3:
                        w_project(b, 0)
                        w_project(b, 1)
                output_transposes(b, 7)
                need(pe, x_att, b, 2)
                mix_k(b, 2, 0)
                mix_k(b, 2, 1)
                for pr in (2, 3):
                    w_transposes(b, pr)
                for pr in (2, 3):
                    w_project(b, pr)
                mix_r(b, 2, 0)
                mix_r(b, 2, 1)
                channel_mix(b, 1)

        @block.scalar
        def _(act):
            prime(act, "act")
            act.wait_ge(s_tables, 16 * N_TABLES)
            nc.scalar.activation(SK[96:128, 0, :].rearrange("p (k n) -> p k n", n=P),
                                 xrT[96:128, 1, 0:8].unsqueeze(2).to_broadcast([32, 8, P]),
                                 ACT.Identity).then_inc(s_rowk, 1)
            act.wait_ge(s_dist, 1)
            act.wait_ge(s_top, 1)
            nc.scalar.activation(kact[0:HEADS, 0, 0:384], bank[7][0:HEADS, 0:384], ACT.Exp,
                                 bias=frs[0:HEADS, 0:1]).then_inc(s_exp, 1)
            for w in range(7):
                act.wait_ge(s_wt, w + 1)
                scale = {A_Q: 0.25, W_V: 0.5}.get(w, 1.0)
                nc.scalar.activation(WT[:, w].rearrange("p c n -> p (c n)"), bank[w], ACT.Identity,
                                     scale=scale).then_inc(s_wts, 1)
            act.wait_ge(s_const, 16 * N_CONST)
            act.wait_ge(s_table, 16)

            def share(b, q, n, i, c):
                g = q % 2
                dst, mu, read = ((xkT, MU_K, p_k), (xrT, MU_R, p_r))[i]
                need(act, fn_T, b, 2 * n + c + 1)
                need(act, read, b, 2 * q)
                nc.scalar.activation(dst[:, c, :], nT[:, c, 1 + 512 * g:513 + 512 * g], ACT.Identity,
                                     scale=vec[:, mu.start + c:mu.start + c + 1]).then_inc(mix_a.sem, 1)

            def ln_copies(b, n):
                g = n % 2
                if n < 2:
                    need(act, mix_b, b, 0)
                elif n < 4:
                    need(act, mix_b, b, 8)
                else:
                    need(act, p_vx, b, 4)
                for c in range(C):
                    need(act, fn_tp, b, 2 * n + c + 1)
                    nc.scalar.copy(nT[:, c, 1 + 512 * g:513 + 512 * g], bank[c]).then_inc(fn_T.sem, 1)
                    if n not in (2, 3):
                        share(b, n % 2 + (0, 2)[n // 4], n, 0, c)

            def shares(b, q):
                for c in range(C):
                    share(b, q, q % 2 + (0, 4)[q // 2], 1, c)

            def relus(b, q, chunks=(0, 1)):
                for o in chunks:
                    need(act, p_k, b, 2 * q + o + 1)
                    need(act, p_kv, b, 2 * q)
                    nc.scalar.activation(kact[:, o, :], bank[2 + o], ACT.Relu).then_inc(k_relu.sem, 1)

            def tanhs(b, q):
                for pr in range(2):
                    need(act, p_r, b, 2 * q + pr + 1)
                    if q == 0:
                        need(act, x_end, b, 0)
                    else:
                        need(act, x_ffn, b, 2 * q + pr - 1)
                    nc.scalar.activation(th[:, pr, :], bank[4 + pr], ACT.Tanh, scale=0.5)\
                        .then_inc(r_tanh.sem, 1)

            def channel_mix(b, f):
                n, q = (0, 4)[f], 2 * f
                tanhs(b, q)
                ln_copies(b, n + 1)
                shares(b, q + 1)
                relus(b, q + 1)
                tanhs(b, q + 1)

            def z_copies(b, t):
                need(act, z_tp, b, t + 1)
                for c in range(C):
                    need(act, p_g, b, t - 1)
                    nc.scalar.activation(zT[:, t % 2, c, :], bank[6 if t else 0][:, c * P:c * P + P], ACT.Identity,
                                         scale=vec[:, LN_W.start + c:LN_W.start + c + 1],
                                         bias=vec[:, LN_B.start + c:LN_B.start + c + 1]).then_inc(z_T.sem, 1)

            z_copies(0, 0)
            with act.Fori(0, B) as b:
                for t in range(NT + 2):
                    if t == NT:
                        ln_copies(b, 0)
                    if t < NT:
                        need(act, p_v, b, t + 1)
                        need(act, *((p_o, b, 0) if t == 1 else (p_st, b, max(t - 1, 0))))
                        nc.scalar.copy(v_sb[:, t % 2, :], bank[1]).then_inc(v_cp.sem, 1)
                    if 1 <= t <= NT:
                        u = t - 1
                        need(act, p_o, b, u + 1)
                        need(act, o_arg, b, u - 1)
                        need(act, o_sq, b, 4 * u)
                        for h in range(RET_HEADS):
                            head = slice(h * DV, h * DV + DV)
                            nc.scalar.activation(sq_junk[:, head], bank[5][:, head], ACT.Square,
                                                 accum_out=oss[:, u % 2, h:h + 1]).then_inc(o_sq.sem, 1)
                    if t < NT:
                        need(act, p_g, b, t + 1)
                        need(act, y_h, b, 4 * (t - 1))
                        nc.scalar.activation(gt[:, t % 2, :], bank[2], ACT.Tanh, scale=0.5)\
                            .then_inc(g_tanh.sem, 1)
                        if t + 1 < NT:
                            z_copies(b, t + 1)
                        need(act, qk_tp, b, t + 1)
                        need(act, p_o, b, t - 1)
                        quad = bank[3].rearrange("p (a n) -> p a n", a=4)
                        nc.scalar.copy(qbd[0:64, t % 2, :, 0, :], quad[0:64, 0:2, :]).then_inc(kq_T.sem, 1)
                        nc.scalar.copy(qbd[64:128, t % 2, :, 1, :], quad[64:128, 0:2, :]).then_inc(kq_T.sem, 1)
                        nc.scalar.copy(kT[:, t % 2, :, :], quad[:, 2:4, :]).then_inc(kq_T.sem, 1)
                    if t >= 2:
                        need(act, y_tp, b, t - 1)
                        need(act, p_w, b, t - 2)
                        nc.scalar.copy(yT[:, :], bank[7]).then_inc(y_T.sem, 1)
                    if t == NT:
                        shares(b, 0)
                        relus(b, 0, (0,))
                relus(b, 0, (1,))
                channel_mix(b, 0)
                def v_copies(pr):
                    need(act, p_vx, b, pr + 1)
                    nc.scalar.copy(Vx[:, 2 * pr:2 * pr + 2, :, 0:HD],
                                   bank[4 + pr % 2].rearrange("p (t h d) -> p t h d", t=2, h=HEADS))\
                        .then_inc(vx_cp.sem, 1)

                ln_copies(b, 2)
                for n in range(8):
                    h, g, s = qk_order(n)
                    if n == 2:
                        v_copies(0)
                        ln_copies(b, 3)
                        v_copies(1)
                    need(act, p_qkT, b, n + 1)
                    at = (BQ, BK)[s].start + h
                    nc.scalar.activation(cmp[:, h, s, 0, 512 * g:512 * g + 512], bank[2 + n % 2],
                                         ACT.Identity, bias=vec[:, at:at + 1]).then_inc(c_hi.sem, 1)
                v_copies(2)
                v_copies(3)

                def max_rows(blk):
                    need(act, mx_tp, b, blk + 1)
                    need(act, mx_in[blk % 2], b, 4 * (blk // 2))
                    nc.scalar.mul(mrow[:, blk % 2, :], bank[7][0:16, 0:P], -1.0).then_inc(mx_row.sem, 1)

                def output_copy(k):
                    need(act, e_pv, b, 8 * k + 8)
                    need(act, o_tp, b, k)
                    nc.scalar.copy(oT[:, :], bank[6]).then_inc(o_cp.sem, 1)

                def w_copy(pr):
                    need(act, w_tp, b, pr + 1)
                    need(act, p_wo, b, pr - 1)
                    nc.scalar.copy(aT[:, pr % 2, :], bank[W_BANKS[pr]]).then_inc(w_T.sem, 1)

                max_rows(0)
                for out_side in parts_out:
                    need(act, out_side, b, 6)
                for s in range(NS):
                    need(act, e_pv, b, max(s - 2, 0))
                    for c in range(4):
                        n = 4 * s + c
                        need(act, e_s, b, n + 1)
                        nc.scalar.activation(ring[:, n % RING, :], col_bank(s, c), ACT.Exp)\
                            .then_inc(e_p.sem, 1)
                        if c == 3 and maxima_in(s) is not None:
                            max_rows(maxima_in(s))
                        if c == 1 and s % 8 == 2 and 2 < s < NS - 8:
                            output_copy(s // 8 - 1)
                ln_copies(b, 4)
                output_copy(7)
                shares(b, 2)
                relus(b, 2)
                w_copy(2)
                w_copy(3)
                channel_mix(b, 1)
                z_copies(b + 1, 0)

        @block.vector
        def _(dve):
            prime(dve, "dve")
            chain = 0

            def link(i):
                nonlocal chain
                chain += 1
                i.then_inc(s_chain, 1)
                dve.wait_ge(s_chain, chain)

            def z_norms(b, t):
                need(dve, z_tp, b, t - 1)
                nc.vector.tensor_scalar(zn[:, t % 2, :], Xin[:, t, :], mv[:, t, 0:1], rs2[:, 1, t:t + 1],
                                        ALU.subtract, ALU.mult).then_inc(z_norm.sem, 1)

            def ln1_stats(b):
                dve.wait_ge(x_in.sem, 16 * (b + 1))
                for t in range(NT):
                    nc.vector.bn_stats(stat[:, t, :], Xin[:, t, :]).then_inc(ln1_stat.sem, 1)
                need(dve, resid, b, 0)
                need(dve, ln1_stat, b, NT)
                stand_alone(dve)
                for t in range(NT):
                    nc.vector.bn_aggr(mv[:, t, :], stat[:, t, :]).then_inc(ln1_mv.sem, 1)

            def ln1_scales(b):
                need(dve, ln1_rs, b, 2)
                z_norms(b, 0)
                nc.vector.tensor_scalar(one_r[:, :], rs2[:, 0, :], 1.0, None, ALU.add).then_inc(ln1_sc.sem, 1)
                nc.vector.scalar_tensor_tensor(neg_mr[:, :], mv[:, :, 0], -1.0, rs2[:, 0, :], ALU.mult, ALU.mult)\
                    .then_inc(ln1_sc.sem, 1)

            for dst, value in ((power[:, :], -0.5), (nT[:, :, 0:1], 0.0), (qbd[:, :, :, :, :], 0.0),
                               (Vx[:, :, :, HD:HD + 1], 1.0), (S[:, :, :], 0.0), (nrm[:, 0, :], 1.0)):
                nc.vector.memset(dst, value).then_inc(s_zero, 1)
            ln1_stats(0)
            dve.wait_ge(s_tables, 16 * N_TABLES)
            nc.vector.tensor_reduce(frs[0:HEADS, 0:1], xkT[0:HEADS, 1, 32:64], AX_X, ALU.max, negate=True)\
                .then_inc(s_top, 1)
            R = slice(96, 128)
            table = xrT[R, 0, :].rearrange("p (k h) -> p h k", k=BUCKETS)
            top, d0, d1 = (xrT[R, 1, 64 + 16 * i:80 + 16 * i] for i in range(3))
            wide = [xrT[R, 1, 128 + 128 * i:256 + 128 * i] for i in range(3)]
            cut3 = [w.rearrange("p (h k) -> p h k", h=HEADS) for w in wide]
            hi, mid, low = (nrm[R, 2, 64 * i:64 * i + 64].bitcast(BF16).rearrange("p (h k) -> p h k", h=HEADS)
                            for i in range(3))
            where0 = xrT[R, 1, 8:16].unsqueeze(1).to_broadcast([32, HEADS, 8])
            where1 = xrT[R, 1, 16:24].unsqueeze(1).to_broadcast([32, HEADS, 8])
            link(nc.vector.tensor_reduce(top, table, AX_X, ALU.max))
            link(nc.vector.tensor_tensor(d0, table[:, :, 0], top, ALU.subtract))
            link(nc.vector.tensor_tensor(d1, table[:, :, BUCKETS - 1], top, ALU.subtract))
            link(nc.vector.tensor_tensor(cut3[0], d0.unsqueeze(2).to_broadcast([32, HEADS, 8]), where0, ALU.mult))
            link(nc.vector.tensor_tensor(cut3[1], d1.unsqueeze(2).to_broadcast([32, HEADS, 8]), where1, ALU.mult))
            link(nc.vector.tensor_tensor(wide[0], wide[0], wide[1], ALU.add))
            link(nc.vector.tensor_copy(hi, cut3[0]))
            link(nc.vector.scalar_tensor_tensor(cut3[1], hi, xrT[R, 1, 24:25], cut3[0], ALU.mult, ALU.add))
            link(nc.vector.tensor_copy(mid, cut3[1]))
            link(nc.vector.scalar_tensor_tensor(cut3[2], mid, xrT[R, 1, 25:26], cut3[1], ALU.mult, ALU.add))
            link(nc.vector.tensor_copy(low, cut3[2]))
            for h in range(HEADS):
                nc.vector.tensor_copy(SQ[R, h, :].rearrange("p (k n) -> p k n", n=P),
                                      low[:, h, :].unsqueeze(2).to_broadcast([32, 8, P])).then_inc(s_rowq, 1)
            dve.wait_ge(s_wt, 7)
            ln1_scales(0)
            dve.wait_ge(s_zero, 6)
            dve.wait_ge(s_rowq, HEADS)
            dve.wait_ge(s_const, 16 * N_CONST)
            for c in range(C):
                nc.vector.tensor_scalar(nrm[:, 0, c * P:c * P + P], nrm[:, 0, c * P:c * P + P],
                                        vec[:, BV.start + c:BV.start + c + 1], None, ALU.mult).then_inc(s_bvb, 1)
            for a, z in ((MU_R, NU_R), (MU_K, NU_K)):
                link(nc.vector.tensor_scalar(vec[:, z], vec[:, a], -1.0, 1.0, ALU.mult, ALU.add))
            link(nc.vector.tensor_scalar(vec[:, BQ], vec[:, BQ], 0.25, None, ALU.mult))
            link(nc.vector.tensor_scalar(WoS[:, :, :], WoS[:, :, :], vec[:, GW.start:GW.start + 1], 0.5,
                                         ALU.mult, ALU.mult))
            dve.wait_ge(s_bvo, 1)
            nc.vector.tensor_tensor(cbias[:, :], bank[0][:, 0:D], cbias[:, :], ALU.add).then_inc(s_cbias, 1)
            dve.wait_ge(s_cbias, 1)
            dve.wait_ge(s_wts, 7)
            nc.vector.memset(bank[6], 0.0).then_inc(s_bank6, 1)
            dve.wait_ge(s_bank6, 1)

            def ln_stats(b, n):
                g = n % 2
                if n < 2:
                    need(dve, x1, b, 4 * g + 4)
                elif n < 4:
                    need(dve, x_ffn, b, 2 * g + 2)
                else:
                    need(dve, x_att, b, 2 * g + 2)
                need(dve, fn_norm, b, 4 * n)
                for i in range(4):
                    nc.vector.bn_stats(fstat[:, i, :], X[:, 4 * g + i, :]).then_inc(fn_stat.sem, 1)
                need(dve, fn_stat, b, 4 * n + 4)
                stand_alone(dve)
                for i in range(4):
                    nc.vector.bn_aggr(fmv[:, i, :], fstat[:, i, :]).then_inc(fn_mv.sem, 1)

            def ln_norms(b, n):
                g = n % 2
                need(dve, fn_rs, b, n + 1)
                need(dve, fn_tp, b, 2 * n)
                for i in range(4):
                    nc.vector.tensor_scalar(nrm[:, i, :], X[:, 4 * g + i, :], fmv[:, i, 0:1], frs[:, i:i + 1],
                                            ALU.subtract, ALU.mult).then_inc(fn_norm.sem, 1)

            def mixes(b, q, sides=(0, 1)):
                g, n = q % 2, q % 2 + (0, 4)[q // 2]
                for i in sides:
                    dst, nu = ((xkT, NU_K), (xrT, NU_R))[i]
                    for c in range(C):
                        need(dve, fn_T, b, 2 * n + c + 1)
                        need(dve, mix_a, b, 4 * q + 2 * i + c + 1)
                        nc.vector.scalar_tensor_tensor(dst[:, c, :], nT[:, c, 512 * g:512 + 512 * g],
                                                       vec[:, nu.start + c:nu.start + c + 1], dst[:, c, :],
                                                       ALU.mult, ALU.add).then_inc(mix_b.sem, 1)

            def gated(b, q):
                for pr in range(2):
                    need(dve, p_kv, b, 2 * q + pr + 1)
                    need(dve, r_tanh, b, 2 * q + pr + 1)
                    nc.vector.scalar_tensor_tensor(th[:, pr, :], th[:, pr, :], 1.0, bank[6 + pr],
                                                   ALU.add, ALU.mult).then_inc(kv_r.sem, 1)

            def x_out(b, t):
                need(dve, p_w, b, t + 1)
                need(dve, resid, b, t + 1)
                nc.vector.tensor_tensor(X[:, t, :], bank[7][:, 0:D], X[:, t, :], ALU.add).then_inc(x1.sem, 1)


            with dve.Fori(0, B) as b:
                for t in range(NT + 1):
                    if t + 1 < NT:
                        z_norms(b, t + 1)
                    if t < NT:
                        need(dve, p_qk, b, t + 1)
                        need(dve, rope_sum, b, t)
                        qk = bank[0].rearrange("p (h a d) -> p h a d", h=8, a=2)
                        rbv = rb[:, :].rearrange("p (h a d) -> p h a d", h=8, a=2)
                        nc.vector.tensor_tensor(ra[:, :].rearrange("p (h d) -> p h d", h=8),
                                                bank[0].rearrange("p (h d) -> p h d", h=8),
                                                cos[:, t, :].unsqueeze(1).to_broadcast([P, 8, DK]), ALU.mult)\
                            .then_inc(rope_ab.sem, 1)
                        for a in range(2):
                            sn = sin[:, t, 32 * a:32 * a + 32].unsqueeze(1).to_broadcast([P, 8, DK // 2])
                            nc.vector.tensor_tensor(rbv[:, :, a, :], qk[:, :, 1 - a, :], sn, ALU.mult)\
                                .then_inc(rope_ab.sem, 1)
                    if t >= 3:
                        x_out(b, t - 3)
                    if 1 <= t <= NT:
                        u = t - 1
                        need(dve, att, b, u + 1)
                        need(dve, p_o, b, u)
                        nc.vector.tensor_tensor(AT[:, :], bank[4], mask[:, :], ALU.mult)\
                            .then_inc(att_m.sem, 1)
                        if t == NT:
                            mixes(b, 0, (0,))
                        if u < NT - 1:
                            need(dve, p_st, b, u + 1)
                            for pr in range(2):
                                new = bank[6][:, pr * DV:pr * DV + DV]
                                if u == 0:
                                    i = nc.vector.tensor_copy(S[:, pr, :], new)
                                else:
                                    need(dve, s_upd, b, 2 * u + pr - 1)
                                    i = nc.vector.scalar_tensor_tensor(S[:, pr, :], S[:, pr, :], gamma[:, pr:pr + 1],
                                                                       new, ALU.mult, ALU.add)
                                i.then_inc(s_upd.sem, 1)
                    if t == 7:
                        ln_norms(b, 0)
                    if t < NT:
                        need(dve, p_g, b, t + 1)
                        need(dve, g_tanh, b, t + 1)
                        nc.vector.scalar_tensor_tensor(gt[:, t % 2, :], gt[:, t % 2, :], 1.0, bank[2],
                                                       ALU.add, ALU.mult).then_inc(gate.sem, 1)
                    if 1 <= t <= NT:
                        need(dve, o_rs, b, u + 1)
                        need(dve, gate, b, u + 1)
                        need(dve, y_tp, b, u)
                        for h in range(RET_HEADS):
                            nc.vector.scalar_tensor_tensor(y[:, h * DV:h * DV + DV], bank[5][:, h * DV:h * DV + DV],
                                                           ors[:, u % 2, h:h + 1], gt[:, u % 2, h * DV:h * DV + DV],
                                                           ALU.mult, ALU.mult).then_inc(y_h.sem, 1)
                    if t == 6:
                        ln_stats(b, 0)
                x_out(b, NT - 2)
                mixes(b, 0, (1,))
                x_out(b, NT - 1)
                ln_stats(b, 1)
                ln_norms(b, 1)
                mixes(b, 1)
                gated(b, 0)
                ln_stats(b, 2)
                ln_norms(b, 2)
                gated(b, 1)
                ln_stats(b, 3)

                ln_norms(b, 3)
                for n in range(8):
                    h, g, s = qk_order(n)
                    need(dve, c_hi, b, n + 1)
                    need(dve, c_lo, b, n - 1)
                    at = (BQ, BK)[s].start + h
                    tok = slice(512 * g, 512 * g + 512)
                    nc.vector.scalar_tensor_tensor(r1[:, n % 2, :], bank[2 + n % 2], vec[:, at:at + 1],
                                                   cmp[:, h, s, 0, tok], ALU.add, ALU.subtract)\
                        .then_inc(c_r1.sem, 1)
                    need(dve, c_r1, b, n + 1)
                    nc.vector.tensor_copy(cmp[:, h, s, 1, tok], r1[:, n % 2, :]).then_inc(c_mid.sem, 1)

                def row_max(u):
                    _, _, blk, col = unit(u)
                    need(dve, mx_s, b, u + 1)
                    nc.vector.tensor_reduce(mx[:, blk, col:col + 1], bank_pair[u % 2], AX_X, ALU.max)\
                        .then_inc(mx_r.sem, 1)

                def attention_out(pr):
                    need(dve, p_wo, b, pr + 1)
                    need(dve, x_cb, b, pr + 1)
                    xs = X[:, 2 * pr:2 * pr + 2, :].rearrange("p t n -> p (t n)")
                    nc.vector.tensor_tensor(xs, bank[W_BANKS[pr] + 1], xs, ALU.add).then_inc(x_att.sem, 1)

                for u in range(AHEAD):
                    row_max(u)
                u = AHEAD
                for s in range(NS + 4):
                    if s < NS:
                        while u < units[s]:
                            row_max(u)
                            u += 1
                    k = output_before(s)
                    if k is not None:
                        need(dve, o_tp, b, k + 1)
                        o = bank[7].rearrange("p (t h d) -> p t h d", t=4, h=4)
                        hg, half = k // 2, k % 2
                        nc.vector.reciprocal(orc[:, :, :], o[:, :, :, HD]).then_inc(o_rc.sem, 1)
                        need(dve, o_rc, b, k + 1)
                        dst = aO[:, 4 * half:4 * half + 4, 64 * hg:64 * hg + 64].rearrange("p t (h d) -> p t h d", h=4)
                        for i in range(4):
                            ins_ = nc.vector.tensor_tensor(dst[:, i], o[:, i, :, 0:HD],
                                                           orc[:, i, :].unsqueeze(2).to_broadcast([P, 4, HD]), ALU.mult)
                        ins_.then_inc(o_n.sem, 1)
                    if s == WIDE.start + 1:
                        ln1_stats(b + 1)
                    if s == NS - 6:
                        need(dve, e_pv, b, NS - 8)
                        need(dve, o_tp, b, 6)
                        nc.vector.tensor_copy(oT[:, :], bank[6]).then_inc(o_cp_6.sem, 1)
                    if s == NS - 4:
                        for pr in range(2):
                            need(dve, w_tp, b, pr + 1)
                            nc.vector.tensor_copy(aT[:, pr, :], bank[W_BANKS[pr]]).then_inc(w_T_early.sem, 1)
                    if s == NS - 3:
                        attention_out(0)
                        attention_out(1)
                        ln_stats(b, 4)
                        ln_norms(b, 4)
                    if s == NS + 2:
                        mixes(b, 2, (0,))
                mixes(b, 2, (1,))
                attention_out(2)
                attention_out(3)
                ln_stats(b, 5)
                ln_norms(b, 5)
                mixes(b, 3)
                gated(b, 2)
                ln1_scales(b + 1)
                gated(b, 3)
                for pr in range(2):
                    need(dve, kv_r, b, 7 + pr)
                    xs = X[:, 4 + 2 * pr:6 + 2 * pr, :].rearrange("p t n -> p (t n)")
                    nc.vector.tensor_tensor(xs, xs, th[:, pr, :], ALU.add).then_inc(x_end.sem, 1)

        @block.gpsimd
        def _(pool):
            prime(pool, "pool")
            pool.wait_ge(s_zero, 6)
            pool.wait_ge(s_exp, 1)

            def rsqrts(b, n):
                need(pool, fn_mv, b, 4 * n + 4)
                need(pool, fn_norm, b, 4 * n)
                stand_alone(pool)
                nc.gpsimd.tensor_scalar(farg[:, :], fmv[:, :, 1], EPS, None, ALU.add).then_inc(fn_arg.sem, 1)
                need(pool, fn_arg, b, n + 1)
                nc.gpsimd.tensor_tensor(frs[:, :], farg[:, :], power[:, 0:4], ALU.pow).then_inc(fn_rs.sem, 1)

            def squares(b, q):
                for o in range(2):
                    need(pool, k_relu, b, 2 * q + o + 1)
                    nc.gpsimd.tensor_tensor(kact[:, o, :], kact[:, o, :], kact[:, o, :], ALU.mult)\
                        .then_inc(k_sq.sem, 1)

            def adds(b, q):
                g = q % 2
                for pr in range(2):
                    need(pool, kv_r, b, 2 * q + pr + 1)
                    t = 4 * g + 2 * pr
                    xs = X[:, t:t + 2, :].rearrange("p t n -> p (t n)")
                    nc.gpsimd.tensor_tensor(xs, xs, th[:, pr, :], ALU.add).then_inc(x_ffn.sem, 1)

            def ln1_args(b):
                need(pool, ln1_mv, b, NT)
                need(pool, z_norm, b, 0)
                stand_alone(pool)
                nc.gpsimd.tensor_scalar(var2[:, 0, :], mv[:, :, 1], 1.0, EPS, ALU.mult, ALU.add)\
                    .then_inc(ln1_arg.sem, 1)
                nc.gpsimd.tensor_scalar(var2[:, 1, :], mv[:, :, 1], 1.0 + EPS, EPS * EPS, ALU.mult, ALU.add)\
                    .then_inc(ln1_arg.sem, 1)

            def ln1_rsqrt(b, i):
                need(pool, ln1_arg, b, i + 1)
                nc.gpsimd.tensor_tensor(rs2[:, i, :], var2[:, i, :], power[:, 0:NT], ALU.pow)\
                    .then_inc(ln1_rs.sem, 1)

            ln1_args(0)
            ln1_rsqrt(0, 0)
            ln1_rsqrt(0, 1)
            with pool.Fori(0, B) as b:
                for t in range(NT + 1):
                    if t < NT:
                        if t == 0:
                            need(pool, ln1_sc, b, 2)
                        if t % 4 == 0:
                            need(pool, stored[t // 4], b, 0)
                        need(pool, rope_ab, b, 3 * t + 3)
                        nc.gpsimd.tensor_tensor(ra[:, :], ra[:, :], rb[:, :], ALU.add).then_inc(rope_sum.sem, 1)
                        nc.gpsimd.tensor_scalar(X[:, t, :], Xin[:, t, :], one_r[:, t:t + 1], neg_mr[:, t:t + 1],
                                                ALU.mult, ALU.add).then_inc(resid.sem, 1)
                        need(pool, rope_sum, b, t + 1)
                        need(pool, att, b, t)
                        nc.gpsimd.tensor_tensor(qkr[:, t % 2, :].rearrange("p (h d) -> p h d", h=8),
                                                ra[:, :].rearrange("p (h d) -> p h d", h=8),
                                                decay[:, :].unsqueeze(2).to_broadcast([P, 8, DK]), ALU.mult)\
                            .then_inc(rope_qk.sem, 1)
                    if t >= 1:
                        u = t - 1
                        need(pool, o_sq, b, 4 * u + 4)
                        stand_alone(pool)
                        nc.gpsimd.tensor_scalar(oarg[:, :], oss[:, u % 2, :], 1.0 / DV, EPS, ALU.mult, ALU.add)\
                            .then_inc(o_arg.sem, 1)
                        need(pool, o_arg, b, u + 1)
                        need(pool, y_h, b, 4 * (u - 1))
                        nc.gpsimd.tensor_tensor(ors[:, u % 2, :], oarg[:, :], power[:, 0:4], ALU.pow)\
                            .then_inc(o_rs.sem, 1)
                    if t == 6:
                        rsqrts(b, 0)
                squares(b, 0)
                rsqrts(b, 1)
                adds(b, 0)
                squares(b, 1)
                rsqrts(b, 2)
                adds(b, 1)
                rsqrts(b, 3)
                for n in range(8):
                    h, g, s = qk_order(n)
                    need(pool, c_mid, b, n + 1)
                    tok = slice(512 * g, 512 * g + 512)
                    nc.gpsimd.tensor_tensor(cmp[:, h, s, 2, tok], r1[:, n % 2, :], cmp[:, h, s, 1, tok],
                                            ALU.subtract).then_inc(c_lo.sem, 1)
                need(pool, fn_norm, b, 16)
                for pr in range(4):
                    xs = X[:, 2 * pr:2 * pr + 2, :]
                    nc.gpsimd.tensor_tensor(xs, xs, cbias[:, :].unsqueeze(1).to_broadcast([P, 2, D]), ALU.add)\
                        .then_inc(x_cb.sem, 1)
                pool.wait_ge(s_band, 16)
                for s in range(NS):
                    if s == NS - 7:
                        ln1_args(b + 1)
                        ln1_rsqrt(b + 1, 0)
                    if s == NS - 5:
                        ln1_rsqrt(b + 1, 1)
                    if s == NS - 2:
                        rsqrts(b, 4)
                    if not bands[s]:
                        continue
                    hg = s // 16
                    a, z, at = bands[s]
                    for c in range(4):
                        n = 4 * s + c
                        need(pool, e_p, b, n + 1)
                        nc.gpsimd.tensor_tensor(ring[:, n % RING, a:z], ring[:, n % RING, a:z],
                                                band_exp[:, 4 * hg + c, at:at + z - a], ALU.mult)\
                            .then_inc(e_band.sem, 1)
                squares(b, 2)
                rsqrts(b, 5)
                adds(b, 2)
                squares(b, 3)


def shape_constants(T, D):
    import numpy as np

    f32 = np.float32
    dk = D // RET_HEADS
    one = f32(1)
    freq = one / (10000.0 ** (np.arange(0, dk, 2, dtype=f32) / f32(dk)).astype(np.float64)).astype(f32)
    angle = (np.arange(T, dtype=f32)[:, None] * freq[None, :]).astype(np.float64)
    c, s = np.cos(angle), np.sin(angle)
    g = 1.0 - np.exp2(-5.0 - np.arange(RET_HEADS))
    i = np.arange(P)
    decay = np.concatenate([g[None] ** (i[:, None] + 1.0) * dk ** -0.5, g[None] ** (P - 1.0 - i[:, None])], 1)
    mask = (i[:, None, None] <= i[None, None, :]) * (g ** -float(P))[None, :, None]
    head = np.arange(P) // 64
    gamma = np.stack([g[2 * pr + head] ** P for pr in range(2)], 1)
    n = np.maximum(np.arange(384) - (P - 1), 0)
    big = 16 + (np.log(np.maximum(n, 1).astype(f32) / f32(16)) / f32(np.log(8)) * f32(16)).astype(np.int32)
    bucket = np.where(n < 16, n, np.minimum(big, BUCKETS - 1))
    rows = np.zeros((32, 64))
    rows[0, 0:8] = 1
    for part in range(PARTS):
        for j in range(8):
            r, blk = 1 + 8 * part + j, np.arange(8)
            rows[r, 0:8] = blk == j
            rows[r, 8:16] = blk < j
            rows[r, 16:24] = blk > j + 1
            rows[r, 24], rows[r, 25] = -(part >= 1), -(part >= 2)
    return {
        "c_ident": np.eye(P), "c_cos": np.concatenate([c, c], 1), "c_sin": np.concatenate([-s, s], 1),
        "c_decay": decay, "c_mask": mask.reshape(P, -1), "c_gamma": gamma,
        "c_onehot": bucket[None, :] == np.arange(BUCKETS)[:, None], "c_rows": rows,
    }


_INS = ["L0_attn_a_x", "L0_attn_a_ln_w", "L0_attn_a_ln_b", "L0_attn_a_Wq", "L0_attn_a_Wk", "L0_attn_a_Wv",
        "L0_attn_a_Wg", "L0_attn_a_g_norm_w", "L0_attn_a_Wo", "L0_attn_b_wq", "L0_attn_b_bq", "L0_attn_b_wk",
        "L0_attn_b_bk", "L0_attn_b_wv", "L0_attn_b_bv", "L0_attn_b_wo", "L0_attn_b_bo", "L0_attn_b_rel_bias",
        "L0_ffn_W_r", "L0_ffn_W_k", "L0_ffn_W_v", "L0_ffn_mu_r", "L0_ffn_mu_k"]


def kernel(**inputs):
    import numpy as np
    import concourse.bacc as bacc
    from concourse.bass_utils import run_bass_kernel_spmd

    nc = bacc.Bacc("TRN2", target_bir_lowering=False, num_devices=1)
    arrays = {n: np.ascontiguousarray(inputs[n]) for n in _INS}
    shape = arrays[_INS[0]].shape
    arrays |= {n: np.ascontiguousarray(a, np.float32) for n, a in shape_constants(shape[1], shape[2]).items()}
    aps = [nc.dram_tensor(n, a.shape, mybir.dt.from_np(a.dtype), kind="ExternalInput").ap()
           for n, a in arrays.items()]
    out = nc.dram_tensor("out", shape, F32, kind="ExternalOutput").ap()
    build(nc, aps, out)
    return run_bass_kernel_spmd(nc, [arrays], core_ids=[0]).results[0]["out"]
```
